# Optimizing a Trainium2 kernel written in Bass

```python
import numpy as np
import jax
import jax.numpy as jnp

def _softmax(x, axis=-1):
    return jax.nn.softmax(x, axis=axis)

def _gelu(x):
    return jax.nn.gelu(x, approximate=True)

def _silu(x):
    return jax.nn.silu(x)

def _sigmoid(x):
    return jax.nn.sigmoid(x)

def _layernorm(x, axis=-1, eps=1e-05):
    m = jnp.mean(x, axis=axis, keepdims=True)
    v = jnp.var(x, axis=axis, keepdims=True)
    return (x - m) / jnp.sqrt(v + eps)

def _scatter_add(tgt, idx, src, axis=0):
    return tgt.at[idx].add(src)

def _segment_sum(src, seg, n):
    return jax.ops.segment_sum(src, seg, n)
kernel_name = 'mk_gnn_resnorm_d4_gnn_r32_c1c59d'

def setup_inputs(seed: int=0):
    np.random.seed(seed)
    _w = jnp.asarray

    def _rec_inputs():
        import jax
        import jax.numpy as jnp
        _gk = jax.random.key(seed)
        x = -0.000202 + 1 * jax.random.normal(jax.random.fold_in(_gk, 1), (3125, 64), jnp.float32)
        _s = jax.random.randint(jax.random.fold_in(_gk, 2), (25000,), 0, 3125, jnp.int32)
        _d = jax.random.randint(jax.random.fold_in(_gk, 3), (25000,), 0, 3125, jnp.int32)
        _loop = jnp.arange(3125, dtype=jnp.int32)
        src = jnp.concatenate([_s, _d, _loop])
        dst = jnp.concatenate([_d, _s, _loop])
        _o = jnp.argsort(dst, stable=True)
        src = src[_o]
        dst = dst[_o]
        edge_weight = jax.random.uniform(jax.random.fold_in(_gk, 13), (53125,), jnp.float32, 0.0, 1)
        edge_weight1 = jax.random.uniform(jax.random.fold_in(_gk, 14), (53125, 1), jnp.float32, 0.0, 0.999999)
        node_vec1 = 0.0014194 + 1.00024 * jax.random.normal(jax.random.fold_in(_gk, 15), (3125, 1), jnp.float32)
        return (x, src, dst, edge_weight, edge_weight1, node_vec1)
    x, src, dst, edge_weight, edge_weight1, node_vec1 = _rec_inputs()

    def _L0_gnn_setup():
        import jax, jax.numpy as jnp
        import numpy as np
        N_NODES = 3125
        N_EDGES = 50000
        IN_CH = 64
        HID_CH = 64

        def _gcn_layer(x, src, dst, W, b, num_nodes):
            h = x @ W
            msgs = h[src]
            agg = jax.ops.segment_sum(msgs, dst, num_segments=num_nodes)
            return agg + b
        key = jax.random.key(seed)
        k1, k2, k3, k4, k5, k6 = jax.random.split(key, 6)
        v0 = jax.random.normal(k1, (N_NODES, IN_CH), dtype=jnp.float32)
        edge_index = jax.random.randint(k2, (2, N_EDGES), 0, N_NODES, dtype=jnp.int64)
        W1 = jax.random.normal(k3, (IN_CH, HID_CH), dtype=jnp.float32) / np.sqrt(IN_CH)
        b1 = jnp.zeros((HID_CH,), dtype=jnp.float32)
        W2 = jax.random.normal(k4, (HID_CH, HID_CH), dtype=jnp.float32) / np.sqrt(HID_CH)
        b2 = jnp.zeros((HID_CH,), dtype=jnp.float32)
        return {'v0': v0, 'edge_index': edge_index, 'W1': W1, 'b1': b1, 'W2': W2, 'b2': b2}
    _L0_gnn_all = _L0_gnn_setup()
    _L0_gnn_in = {k: v for k, v in _L0_gnn_all.items() if k in ('W1', 'b1', 'W2', 'b2')}
    del _L0_gnn_all

    def _L1_gnn_setup():
        import jax, jax.numpy as jnp
        import numpy as np
        N_NODES = 50000
        N_EDGES = 25000
        NODE_NF = 64
        HIDDEN_NF = 128

        def _linear_params(key, fan_in, fan_out):
            kw, kb = jax.random.split(key)
            bound = 1.0 / np.sqrt(fan_in)
            W = jax.random.uniform(kw, (fan_in, fan_out), minval=-bound, maxval=bound, dtype=jnp.float32)
            b = jax.random.uniform(kb, (fan_out,), minval=-bound, maxval=bound, dtype=jnp.float32)
            return (W, b)
        key = jax.random.key(seed)
        ks = jax.random.split(key, 8)
        h = jax.random.normal(ks[0], (N_NODES, NODE_NF), dtype=jnp.float32)
        row = jax.random.randint(ks[1], (N_EDGES,), 0, N_NODES)
        col = jax.random.randint(ks[2], (N_EDGES,), 0, N_NODES)
        dist = jax.random.uniform(ks[3], (N_EDGES, 1), dtype=jnp.float32)
        eW1, eb1 = _linear_params(ks[4], 2 * NODE_NF + 1, HIDDEN_NF)
        eW2, eb2 = _linear_params(ks[5], HIDDEN_NF, HIDDEN_NF)
        nW1, nb1 = _linear_params(ks[6], HIDDEN_NF + NODE_NF, HIDDEN_NF)
        nW2, nb2 = _linear_params(ks[7], HIDDEN_NF, NODE_NF)
        return {'h': h, 'row': row, 'col': col, 'dist': dist, 'eW1': eW1, 'eb1': eb1, 'eW2': eW2, 'eb2': eb2, 'nW1': nW1, 'nb1': nb1, 'nW2': nW2, 'nb2': nb2}
    _L1_gnn_all = _L1_gnn_setup()
    _L1_gnn_in = {k: v for k, v in _L1_gnn_all.items() if k in ('eW1', 'eb1', 'eW2', 'eb2', 'nW1', 'nb1', 'nW2', 'nb2')}
    del _L1_gnn_all

    def _L2_gnn_setup():
        import jax, jax.numpy as jnp
        import numpy as np
        N = 50000
        E = 50000
        IN_DIM = 64
        OUT_DIM = 64
        key = jax.random.key(seed)
        ks = jax.random.split(key, 8)
        mu = jax.random.normal(ks[0], (N, IN_DIM), dtype=jnp.float32)
        x = jax.random.normal(ks[1], (N, 1), dtype=jnp.float32)
        edge_index = jax.random.randint(ks[2], (2, E), 0, N, dtype=jnp.int64)
        edge_w = jax.random.uniform(ks[3], (E,), dtype=jnp.float32)
        W1 = jax.random.normal(ks[4], (OUT_DIM, 1), dtype=jnp.float32) * (1.0 / 1.0)
        W2 = jax.random.normal(ks[5], (OUT_DIM, 1), dtype=jnp.float32) * (1.0 / 1.0)
        W3 = jax.random.normal(ks[6], (OUT_DIM, IN_DIM), dtype=jnp.float32) * (1.0 / np.sqrt(IN_DIM))
        W4 = jax.random.normal(ks[7], (OUT_DIM, 3 * OUT_DIM), dtype=jnp.float32) * (1.0 / np.sqrt(3 * OUT_DIM))
        return {'mu': mu, 'x': x, 'edge_index': edge_index, 'edge_w': edge_w, 'W1': W1, 'W2': W2, 'W3': W3, 'W4': W4}
    _L2_gnn_all = _L2_gnn_setup()
    _L2_gnn_in = {k: v for k, v in _L2_gnn_all.items() if k in ('W1', 'W2', 'W3', 'W4')}
    del _L2_gnn_all

    def _L3_gnn_setup():
        import jax, jax.numpy as jnp
        import numpy as np
        N = 3125
        E = 50000
        DIN = 64
        DOUT = 64
        K = 10
        T = 1.0
        key = jax.random.key(seed)
        k1, k2, k3 = jax.random.split(key, 3)
        x = jax.random.normal(k1, (N, DIN), dtype=jnp.float32)
        W = jax.random.normal(k2, (K + 1, DIN, DOUT), dtype=jnp.float32) / np.sqrt(DIN).astype(np.float32)
        bias = jnp.zeros((DOUT,), dtype=jnp.float32)
        edge_index = jax.random.randint(k3, (2, E), 0, N, dtype=jnp.int32)
        return {'x': x, 'W': W, 'bias': bias, 'edge_index': edge_index, 'num_nodes': N}
    _L3_gnn_all = _L3_gnn_setup()
    _L3_gnn_in = {k: v for k, v in _L3_gnn_all.items() if k in ('W', 'bias')}
    del _L3_gnn_all
    return {'x': x, 'src': src, 'dst': dst, 'edge_weight': edge_weight, 'edge_weight1': edge_weight1, 'node_vec1': node_vec1, 'L0_gnn_W1': _L0_gnn_in['W1'], 'L0_gnn_b1': _L0_gnn_in['b1'], 'L0_gnn_W2': _L0_gnn_in['W2'], 'L0_gnn_b2': _L0_gnn_in['b2'], 'L1_gnn_eW1': _L1_gnn_in['eW1'], 'L1_gnn_eb1': _L1_gnn_in['eb1'], 'L1_gnn_eW2': _L1_gnn_in['eW2'], 'L1_gnn_eb2': _L1_gnn_in['eb2'], 'L1_gnn_nW1': _L1_gnn_in['nW1'], 'L1_gnn_nb1': _L1_gnn_in['nb1'], 'L1_gnn_nW2': _L1_gnn_in['nW2'], 'L1_gnn_nb2': _L1_gnn_in['nb2'], 'L2_gnn_W1': _L2_gnn_in['W1'], 'L2_gnn_W2': _L2_gnn_in['W2'], 'L2_gnn_W3': _L2_gnn_in['W3'], 'L2_gnn_W4': _L2_gnn_in['W4'], 'L3_gnn_W': _L3_gnn_in['W'], 'L3_gnn_bias': _L3_gnn_in['bias']}

def reference(x, src, dst, edge_weight, edge_weight1, node_vec1, L0_gnn_W1, L0_gnn_b1, L0_gnn_W2, L0_gnn_b2, L1_gnn_eW1, L1_gnn_eb1, L1_gnn_eW2, L1_gnn_eb2, L1_gnn_nW1, L1_gnn_nb1, L1_gnn_nW2, L1_gnn_nb2, L2_gnn_W1, L2_gnn_W2, L2_gnn_W3, L2_gnn_W4, L3_gnn_W, L3_gnn_bias):
    import jax
    import jax.numpy as jnp

    def _L0_gnn_ref(v0, edge_index, W1, b1, W2, b2):
        import jax, jax.numpy as jnp
        import numpy as np
        N_NODES = 3125
        N_EDGES = 50000
        IN_CH = 64
        HID_CH = 64

        def _gcn_layer(x, src, dst, W, b, num_nodes):
            h = x @ W
            msgs = h[src]
            agg = jax.ops.segment_sum(msgs, dst, num_segments=num_nodes)
            return agg + b
        src, dst = (edge_index[0], edge_index[1])
        n = v0.shape[0]
        x = jax.nn.relu(_gcn_layer(v0, src, dst, W1, b1, n))
        return _gcn_layer(x, src, dst, W2, b2, n)

    def _L1_gnn_ref(h, row, col, dist, eW1, eb1, eW2, eb2, nW1, nb1, nW2, nb2):
        import jax, jax.numpy as jnp
        import numpy as np
        N_NODES = 50000
        N_EDGES = 25000
        NODE_NF = 64
        HIDDEN_NF = 128

        def _linear_params(key, fan_in, fan_out):
            kw, kb = jax.random.split(key)
            bound = 1.0 / np.sqrt(fan_in)
            W = jax.random.uniform(kw, (fan_in, fan_out), minval=-bound, maxval=bound, dtype=jnp.float32)
            b = jax.random.uniform(kb, (fan_out,), minval=-bound, maxval=bound, dtype=jnp.float32)
            return (W, b)
        edge_in = jnp.concatenate([h[row], h[col], dist], axis=1)
        e = jax.nn.silu(edge_in @ eW1 + eb1)
        e = jax.nn.silu(e @ eW2 + eb2)
        agg = jax.ops.segment_sum(e, row, num_segments=h.shape[0])
        node_in = jnp.concatenate([h, agg], axis=1)
        out = jax.nn.silu(node_in @ nW1 + nb1) @ nW2 + nb2
        return out

    def _L2_gnn_ref(mu, x, edge_index, edge_w, W1, W2, W3, W4):
        import jax, jax.numpy as jnp
        import numpy as np
        N = 50000
        E = 50000
        IN_DIM = 64
        OUT_DIM = 64
        relu = jax.nn.relu
        n_nodes = mu.shape[0]
        h_x = relu(x @ W1.T)
        h_e = relu(edge_w[:, None] @ W2.T)
        h_mu = relu(mu @ W3.T)
        dst = edge_index[1]
        src = edge_index[0]
        cat_feat = jnp.concatenate([h_x[dst], h_e, h_mu[dst]], axis=1)
        agg = jax.ops.segment_sum(cat_feat, src, num_segments=n_nodes)
        agg = relu(agg @ W4.T)
        return relu(h_x + h_mu + agg)

    def _L3_gnn_ref(x, W, bias, edge_index, num_nodes):
        import jax, jax.numpy as jnp
        import numpy as np
        N = 3125
        E = 50000
        DIN = 64
        DOUT = 64
        K = 10
        T = 1.0
        row, col = (edge_index[0], edge_index[1])
        ones = jnp.ones((edge_index.shape[1],), dtype=x.dtype)
        deg = jax.ops.segment_sum(ones, row, num_segments=num_nodes)
        dinv = jnp.where(deg > 0, 1.0 / jnp.sqrt(jnp.where(deg > 0, deg, 1.0)), 0.0)
        norm = dinv[row] * dinv[col]

        def L_apply(h):
            msg = norm[:, None] * h[col]
            return h - jax.ops.segment_sum(msg, row, num_segments=num_nodes)
        out = jnp.zeros((num_nodes, W.shape[2]), dtype=x.dtype)
        h_k = x
        inv_f = 1.0
        for k in range(K + 1):
            out = out + h_k @ W[k] * inv_f
            if k < K:
                h_k = -T * L_apply(h_k)
                inv_f = inv_f / (k + 1)
        return out + bias
    edge_index = jnp.stack([src, dst])
    x = _layernorm(x + _L0_gnn_ref(x, edge_index, L0_gnn_W1, L0_gnn_b1, L0_gnn_W2, L0_gnn_b2), axis=-1)
    x = _layernorm(x + _L1_gnn_ref(x, src, dst, edge_weight1, L1_gnn_eW1, L1_gnn_eb1, L1_gnn_eW2, L1_gnn_eb2, L1_gnn_nW1, L1_gnn_nb1, L1_gnn_nW2, L1_gnn_nb2), axis=-1)
    x = _layernorm(x + _L2_gnn_ref(x, node_vec1, edge_index, edge_weight, L2_gnn_W1, L2_gnn_W2, L2_gnn_W3, L2_gnn_W4), axis=-1)
    x = _layernorm(x + _L3_gnn_ref(x, L3_gnn_W, L3_gnn_bias, edge_index, 3125), axis=-1)
    return x

_drawn_inputs = setup_inputs


def setup_inputs(seed=0):
    import zlib

    import numpy as np

    out = dict(_drawn_inputs(seed))
    spreads = {'L0_gnn_b1': (0.0, 0.384), 'L0_gnn_b2': (0.0, 2.0), 'L3_gnn_bias': (0.0, 0.1)}
    factors = {'edge_weight1': 64.0, 'L1_gnn_eb1': 3.528, 'L1_gnn_nb1': 5.923}
    for name, (base, spread) in spreads.items():
        noise = np.random.default_rng([zlib.crc32(name.encode()), seed]).standard_normal(out[name].shape)
        drawn = base * np.exp(spread * noise) if base else spread * noise
        out[name] = jnp.asarray(drawn.astype(out[name].dtype))
    for name, factor in factors.items():
        out[name] = (out[name] * factor).astype(out[name].dtype)
    return out
```

```python
import numpy as np
import concourse.bass as bass
from concourse import mybir
from contextlib import ExitStack, contextmanager

F32, BF16, I32 = mybir.dt.float32, mybir.dt.bfloat16, mybir.dt.int32
ALU = mybir.AluOpType
ACT = mybir.ActivationFunctionType
X = mybir.AxisListType.X

P = 128
V, E, D, H = 3125, 53125, 64, 128
NB = 25
B = V // NB
CH = E // B
W = 18
WIN = P * W
CAP = P
NC = NB + 1
NT = NB * NC
MW = 3128
KMAX = 10
REC = 3
WP = 7
GROUPS = [list(range(g, min(g + 4, NC))) for g in range(0, NC, 4)]
EPS = 1e-5


class Steps:

    def __init__(self, eng, sem):
        self.eng, self.sem, self.base, self.n = eng, sem, 0, 0

    def __call__(self, ins):
        ins.then_inc(self.sem, 1)
        self.n += 1
        return ins

    def wait(self):
        self.eng.wait_ge(self.sem, self.base + self.n)


def in_pairs(eng, count, body):
    body(0, 0)
    with eng.Fori(1, count, 2) as i:
        i = i.with_bounds(min_val=1, max_val=count - 2)
        body(i, 1)
        body((i + 1).with_bounds(min_val=2, max_val=count - 1), 0)


def place_edges(nc, a, c, t):
    with ExitStack() as s:
        sb = lambda n, sh, d: s.enter_context(nc.sbuf_tensor(n, sh, d))
        sem = lambda n: s.enter_context(nc.semaphore(n))
        dst_i = sb("dst_i", [B, CH], I32)
        dst_f = sb("dst_f", [B, CH], F32)
        below = sb("below", [B, NB, CH], BF16)
        cnt = sb("cnt", [B, NB], F32)
        start_f = sb("start_f", [1, NB], F32)
        start_i = sb("start_i", [1, NB], I32)
        ew = sb("ew", [P, NB, W, 2], I32)
        ww = sb("ww", [P, NB, W, 2], F32)
        bcol = sb("bcol", [P, NB, W], F32)
        bsb = sb("bsb", [P, NB, W], F32)
        keep = sb("keep", [P, NB * W], BF16)
        tri = sb("tri", [P, P], BF16)
        ps_cnt = s.enter_context(nc.psum_tensor("ps_cnt", [P, 512], F32))
        ps_cross = s.enter_context(nc.psum_tensor("ps_cross", [P, 1024], F32))
        ps_slot = [s.enter_context(nc.psum_tensor(f"ps_slot{i}", [P, 512], F32)) for i in range(2)]

        dst_in, counted, start_sum, start_ready = map(sem, ("dst_in", "counted", "start_sum", "start_ready"))
        edges_in, weights_in, consts = map(sem, ("edges_in", "weights_in", "consts"))
        with nc.Block() as block:
            @block.sync
            def _(sp):
                sp.dma_start(dst_i[:], a["dst"].rearrange("(p j) -> p j", p=B)).then_inc(dst_in, 16)
                sp.wait_ge(start_ready, 1)
                with sp.Fori(0, NB) as b:
                    first = sp.value_load(start_i[0:1, bass.ds(b, 1)], min_val=0, max_val=E - WIN)
                    sp.dma_start(ew[:, bass.ds(b, 1), :, :].rearrange("p o j k -> p (o j k)"),
                                 a["edges"][bass.ds(first * 2, WIN * 2)].rearrange("(p j) -> p j", p=P)
                                 ).then_inc(edges_in, 16)
                sp.wait_ge(edges_in, 16 * NB)

            @block.scalar
            def _(act):
                act.wait_ge(start_ready, 1)
                with act.Fori(0, NB) as b:
                    first = act.value_load(start_i[0:1, bass.ds(b, 1)], min_val=0, max_val=E - WIN)
                    act.dma_start(ww[:, bass.ds(b, 1), :, :].rearrange("p o j k -> p (o j k)"),
                                  a["weights"][bass.ds(first * 2, WIN * 2)].rearrange("(p j) -> p j", p=P)
                                  ).then_inc(weights_in, 16)
                act.wait_ge(weights_in, 16 * NB)

            @block.gpsimd
            def _(pool):
                nc.gpsimd.memset(c.ones[:], 1.0)
                nc.gpsimd.memset(c.ones_bf[:], 1.0)
                nc.gpsimd.memset(c.eps[:], EPS)
                nc.gpsimd.iota(c.sign[:], [[0, 1]], base=1, channel_multiplier=-2,
                               allow_small_or_imprecise_dtypes=True)
                nc.gpsimd.iota(c.iota1[:], [[1, P]], base=1, channel_multiplier=0,
                               allow_small_or_imprecise_dtypes=True)
                nc.gpsimd.iota(c.iota1_bf[:], [[1, P]], base=1, channel_multiplier=0,
                               allow_small_or_imprecise_dtypes=True)
                nc.gpsimd.iota(c.row1[:], [[0, 1]], base=1, channel_multiplier=1,
                               allow_small_or_imprecise_dtypes=True)
                nc.gpsimd.iota(bcol[:], [[1, NB], [0, W]], base=0, channel_multiplier=0,
                               allow_small_or_imprecise_dtypes=True)
                nc.gpsimd.iota(bsb[:], [[1, NB], [0, W]], base=1, channel_multiplier=0,
                               allow_small_or_imprecise_dtypes=True)
                nc.gpsimd.memset(keep[:], 1.0).then_inc(consts, 1)
                pool.wait_ge(consts, 1)
                nc.gpsimd.memset(keep[:].rearrange("p (c j) -> p c j", j=W)[:, :, 0:1], 0.0)
                nc.gpsimd.affine_select(out=c.ident[:], in_=c.ones[:], compare_op=ALU.is_equal, fill=0.0, base=0,
                                        pattern=[[-1, P]], channel_multiplier=1)
                nc.gpsimd.affine_select(out=c.ident_bf[:], in_=c.ones_bf[:], compare_op=ALU.is_equal, fill=0.0,
                                        base=0, pattern=[[-1, P]], channel_multiplier=1)
                nc.gpsimd.affine_select(out=tri[:], in_=c.ones_bf[:], compare_op=ALU.is_gt, fill=0.0, base=0,
                                        pattern=[[1, P]], channel_multiplier=-1).then_inc(consts, 1)

            @block.vector
            def _(dve):
                nc.vector.memset(cnt[:, 0:1], 0.0)
                dve.wait_ge(dst_in, 16)
                nc.vector.tensor_copy(dst_f[:], dst_i[:]).then_inc(counted, 1)
                dve.wait_ge(counted, 1)
                for b in range(1, NB):
                    last = nc.vector.tensor_scalar(below[:, b, :], dst_f[:], float(B * b), 0.0, ALU.is_lt, ALU.add,
                                                   accum_out=cnt[:, b:b + 1])
                last.then_inc(counted, 1)
                dve.wait_ge(start_sum, 1)
                nc.vector.tensor_scalar(start_f[:], ps_cnt[0:1, 0:NB], float(E - WIN), None, ALU.min
                                        ).then_inc(counted, 1)
                dve.wait_ge(counted, 3)
                nc.vector.tensor_copy(start_i[:], start_f[:]).then_inc(start_ready, 1)

            @block.tensor
            def _(pe):
                pe.wait_ge(counted, 2)
                pe.wait_ge(consts, 2)
                nc.tensor.matmul(ps_cnt[0:1, 0:NB], c.ones[0:B, 0:1], cnt[:], start=True, stop=True
                                 ).then_inc(start_sum, 1)

        srcf = sb("srcf", [P, NB, W], F32)
        dstf = sb("dstf", [P, NB, W], F32)
        sblk_i = sb("sblk_i", [P, NB, W], I32)
        dblk_i = sb("dblk_i", [P, NB, W], I32)
        sblk = sb("sblk", [P, NB, W], F32)
        dblk = sb("dblk", [P, NB, W], F32)
        key = sb("key", [P, NB, W], F32)
        diag = sb("diag", [P, NB, W], F32)
        rank = sb("rank", [P, NB, W], F32)
        slot = sb("slot", [P, NB, W], F32)
        col = sb("col", [P, NB, W], F32)
        rec = sb("rec", [P, NB, W, REC], F32)
        tmp = sb("tmp", [P, NB, W], F32)
        oh = sb("oh", [P, NB, NB, W], BF16)
        run = sb("run", [P, NB * NB, W], BF16)
        hit = [sb(f"hit{i}", [P, NB * W], F32) for i in range(2)]
        placed = sb("placed", [P, 1], F32)
        d1, ran, crossed = map(sem, ("place_step", "ran", "crossed"))
        with nc.Block() as block:
            @block.vector
            def _(dve):
                D1 = Steps(dve, d1)
                D1(nc.vector.tensor_copy(srcf[:], ew[:, :, :, 0]))
                D1(nc.vector.tensor_copy(dstf[:], ew[:, :, :, 1]))
                nc.vector.tensor_copy(rec[:, :, :, 1:3], ww[:])
                D1.wait()
                D1(nc.vector.tensor_scalar(sblk_i[:], srcf[:], 1.0 / B, 0.5 / B - 0.5, ALU.mult, ALU.add))
                D1(nc.vector.tensor_scalar(dblk_i[:], dstf[:], 1.0 / B, 0.5 / B - 0.5, ALU.mult, ALU.add))
                D1.wait()
                D1(nc.vector.tensor_copy(sblk[:], sblk_i[:]))
                D1(nc.vector.tensor_copy(dblk[:], dblk_i[:]))
                D1.wait()
                D1(nc.vector.tensor_tensor(tmp[:], dblk[:], bcol[:], ALU.is_equal))
                D1(nc.vector.tensor_tensor(diag[:], sblk[:], dblk[:], ALU.is_equal))
                D1(nc.vector.scalar_tensor_tensor(srcf[:], sblk[:], -float(B), srcf[:], ALU.mult, ALU.add))
                D1(nc.vector.scalar_tensor_tensor(dstf[:], dblk[:], -float(B), dstf[:], ALU.mult, ALU.add))
                D1.wait()
                D1(nc.vector.scalar_tensor_tensor(key[:], sblk[:], 1.0, tmp[:], ALU.add, ALU.mult))
                D1.wait()
                D1(nc.vector.scalar_tensor_tensor(tmp[:], dstf[:], 256.0, srcf[:], ALU.mult, ALU.add))
                D1.wait()
                D1(nc.vector.tensor_scalar(rec[:, :, :, 0], tmp[:], 257.0, None, ALU.add))
                for b in range(NB):
                    D1(nc.vector.tensor_tensor(oh[:, b], key[:, b:b + 1, :].broadcast_to([P, NB, W]), bsb[:],
                                               ALU.is_equal))
                D1.wait()
                for b in range(NB):
                    last = nc.vector.tensor_tensor_scan(
                        run[:, b * NB:(b + 1) * NB, :].rearrange("p c j -> p (c j)"), keep[:],
                        oh[:, b].rearrange("p c j -> p (c j)"), 0.0, ALU.mult, ALU.add)
                last.then_inc(ran, 1)
                dve.wait_ge(crossed, 1)
                for b in range(NB):
                    k, s0 = b % 2, (b * NB if b * NB < 500 else b * NB + 12)
                    D1.wait()
                    D1(nc.vector.tensor_tensor(
                        hit[k][:].rearrange("p (c j) -> p c j", j=W), run[:, b * NB:(b + 1) * NB, :],
                        ps_cross[:, s0:s0 + NB].unsqueeze(2).broadcast_to([P, NB, W]), ALU.add))
                    D1.wait()
                    D1(nc.vector.tensor_tensor(hit[k][:], hit[k][:], oh[:, b].rearrange("p c j -> p (c j)"),
                                               ALU.mult))
                    D1.wait()
                    D1(nc.vector.reduce_sum(rank[:, b, :], hit[k][:].rearrange("p (c j) -> p j c", j=W), X))
                D1.wait()
                D1(nc.vector.scalar_tensor_tensor(tmp[:], rank[:], float(CAP), diag[:], ALU.is_gt, ALU.mult))
                D1(nc.vector.tensor_scalar(col[:], sblk[:], -1.0, float(NB), ALU.mult, ALU.add))
                D1.wait()
                D1(nc.vector.scalar_tensor_tensor(slot[:], tmp[:], -float(CAP), rank[:], ALU.mult, ALU.add))
                D1(nc.vector.tensor_tensor(col[:], col[:], tmp[:], ALU.mult))
                D1.wait()
                D1(nc.vector.scalar_tensor_tensor(col[:], col[:], 1.0, sblk[:], ALU.add, ALU.add))
                D1(nc.vector.tensor_scalar(tmp[:], slot[:], 1.0, None, ALU.is_ge))
                D1.wait()
                D1(nc.vector.scalar_tensor_tensor(diag[:], slot[:], float(CAP), tmp[:], ALU.is_le, ALU.mult))
                D1.wait()
                nc.vector.reduce_sum(placed[:], diag[:].rearrange("p b j -> p (b j)"), X).then_inc(ran, 1)

            @block.tensor
            def _(pe):
                pe.wait_ge(ran, 1)
                nc.tensor.matmul(ps_cross[:, 0:500], tri[:], run[:, 0:500, W - 1], start=True, stop=True)
                nc.tensor.matmul(ps_cross[:, 512:637], tri[:], run[:, 500:625, W - 1], start=True, stop=True
                                 ).then_inc(crossed, 1)
                pe.wait_ge(ran, 2)
                nc.tensor.matmul(ps_cnt[0:1, 0:1], placed[:], c.ones[:, 0:1], start=True, stop=True
                                 ).then_inc(crossed, 1)

            @block.scalar
            def _(act):
                act.wait_ge(crossed, 2)
                nc.scalar.copy(c.placed_i[:], ps_cnt[0:1, 0:1])

        ohr = sb("ohr", [P, 2, W, P], F32)
        ohc = sb("ohc", [P, 2, W, NC], F32)
        rows = sb("rows", [P, 2, W, NC * REC], F32)
        iotac = sb("iotac", [P, W, NC], F32)
        stage = sb("stage", [P, 2, W], F32)
        iotac_set, stage_set, ohc_ready, win_ready, win_used, slot_ready, slot_used = map(sem, (
            "iotac_set", "stage_set", "ohc_ready", "win_ready", "win_used", "slot_ready", "slot_used"))
        with nc.Block() as block:
            @block.gpsimd
            def _(pool):
                nc.gpsimd.iota(iotac[:], [[0, W], [1, NC]], base=1, channel_multiplier=0,
                               allow_small_or_imprecise_dtypes=True).then_inc(iotac_set, 1)

            @block.vector
            def _(dve):
                dve.wait_ge(iotac_set, 1)

                def body(b, k):
                    dve.wait_ge(win_used, b + 1)
                    nc.vector.tensor_copy(stage[:, k, :], slot[:, bass.ds(b, 1), :].rearrange("p o j -> p (o j)")
                                          ).then_inc(stage_set, 1)
                    nc.vector.tensor_tensor(
                        ohc[:, k], col[:, bass.ds(b, 1), :].rearrange("p o j -> p j o").broadcast_to([P, W, NC]),
                        iotac[:], ALU.is_equal).then_inc(ohc_ready, 1)
                    dve.wait_ge(ohc_ready, b + 1)
                    nc.vector.tensor_tensor(
                        rows[:, k].rearrange("p j (c r) -> p j c r", r=REC),
                        ohc[:, k].unsqueeze(3).broadcast_to([P, W, NC, REC]),
                        rec[:, bass.ds(b, 1), :, :].rearrange("p o j r -> p (o j) r").unsqueeze(2)
                        .broadcast_to([P, W, NC, REC]), ALU.mult)
                    dve.wait_ge(stage_set, b + 1)
                    for j in range(W):
                        last = nc.vector.tensor_scalar(ohr[:, k, j, :], c.iota1[:], stage[:, k, j:j + 1], None,
                                                       ALU.is_equal)
                    last.then_inc(win_ready, 1)
                in_pairs(dve, NB, body)

            @block.tensor
            def _(pe):
                pe.sem_inc(win_used, 2)

                def body(b, k):
                    pe.wait_ge(win_ready, b + 1)
                    pe.wait_ge(slot_used, b + 1)
                    for j in range(W):
                        last = nc.tensor.matmul(ps_slot[k][:, 0:NC * REC], ohr[:, k, j, :], rows[:, k, j, :],
                                                start=(j == 0), stop=(j == W - 1))
                    last.then_inc(win_used, 1)
                in_pairs(pe, NB, body)

            @block.scalar
            def _(act):
                act.sem_inc(slot_used, 2)

                def body(b, k):
                    act.wait_ge(win_used, b + 3)
                    nc.scalar.copy(t.slots[:, :, :, bass.ds(b, 1)].rearrange("p r c o -> p r (c o)"),
                                   ps_slot[k][:, 0:NC * REC].rearrange("p (c r) -> p r c", r=REC)
                                   ).then_inc(slot_used, 1)
                in_pairs(act, NB, body)




def edge_tables(nc, c, t, slots, rows_d):
    with ExitStack() as s:
        sb = lambda n, sh, d: s.enter_context(nc.sbuf_tensor(n, sh, d))
        sem = lambda n: s.enter_context(nc.semaphore(n))
        code = sb("code", [P, NT], I32)
        si, di = sb("si", [P, NT], I32), sb("di", [P, NT], I32)
        fields = sb("fields", [P, 5, NT], BF16)
        rest = [sb(f"rest{i}", [P, NT], F32) for i in range(3)]
        wpm = sb("wpm", [P, 2, NT], F32)
        row_sb = sb("row_sb", [B, NC, P], BF16)
        ps = [s.enter_context(nc.psum_tensor(f"ps_row{i}", [P, 8, P], BF16)) for i in range(4)]
        done, rowed, row_out, rows_out = map(sem, ("table_step", "rowed", "row_out", "rows_out"))
        wv = lambda k: t.wparts[:, :, k]
        u, w1, w = (slots[:, r].rearrange("p c b -> p (c b)") for r in range(REC))
        with nc.Block() as block:
            @block.vector
            def _(dve):
                S = Steps(dve, done)
                v = nc.vector
                S(v.tensor_copy(code[:], u))
                S(v.tensor_copy(fields[:, 2], w1))
                S(v.tensor_scalar(wpm[:, 0], w, 0.0, None, ALU.max))
                S(v.tensor_scalar(wpm[:, 1], w, -1.0, 0.0, ALU.mult, ALU.max))
                S(v.memset(wv(6), 1.0))
                S.wait()
                S(v.tensor_scalar(si[:], code[:], 255, None, ALU.bitwise_and))
                S(v.tensor_scalar(di[:], code[:], 8, None, ALU.logical_shift_right))
                S(v.tensor_tensor(rest[0][:], w1, fields[:, 2], ALU.subtract))
                S(v.tensor_copy(wv(0), wpm[:, 0]))
                S(v.tensor_copy(wv(3), wpm[:, 1]))
                S.wait()
                S(v.tensor_copy(t.src1[:], si[:]))
                S(v.tensor_copy(t.dst1[:], di[:]))
                S(v.tensor_copy(fields[:, 0], si[:]))
                S(v.tensor_copy(fields[:, 1], di[:]))
                S(v.tensor_copy(fields[:, 3], rest[0][:]))
                S(v.tensor_tensor(rest[1][:], wpm[:, 0], wv(0), ALU.subtract))
                S(v.tensor_tensor(rest[2][:], wpm[:, 1], wv(3), ALU.subtract))
                S.wait()
                S(v.tensor_tensor(fields[:, 4], rest[0][:], fields[:, 3], ALU.subtract))
                S(v.tensor_copy(wv(1), rest[1][:]))
                S(v.tensor_copy(wv(4), rest[2][:]))
                S.wait()
                S(v.tensor_tensor(wv(2), rest[1][:], wv(1), ALU.subtract))
                S(v.tensor_tensor(wv(5), rest[2][:], wv(4), ALU.subtract))
                t.n_fields = 18

            @block.tensor
            def _(pe):
                pe.wait_ge(done, 18)
                flat = fields[:].rearrange("p f n -> p (f n)")
                for i in range(NC):
                    last = nc.tensor.transpose(ps[i // 8][0:B, i % 8, :], flat[:, i * B:(i + 1) * B], c.ident_bf[:])
                    if i % 8 == 7 or i == NC - 1:
                        last.then_inc(rowed, 1)

            @block.scalar
            def _(act):
                for g in range(4):
                    n = min(8, NC - 8 * g)
                    act.wait_ge(rowed, g + 1)
                    nc.scalar.copy(row_sb[:, 8 * g:8 * g + n, :], ps[g][0:B, 0:n, :]).then_inc(row_out, 1)

            @block.sync
            def _(sp):
                sp.wait_ge(row_out, 4)
                sp.dma_start(rows_d.rearrange("(n p r) -> p n r", p=B, r=P), row_sb[:]).then_inc(rows_out, 16)
                sp.wait_ge(rows_out, 16)


def count_matrices(nc, c, t, m2_d):
    with ExitStack() as s:
        sb = lambda n, sh, d: s.enter_context(nc.sbuf_tensor(n, sh, d))
        sem = lambda n: s.enter_context(nc.semaphore(n))
        pb = lambda n: s.enter_context(nc.psum_tensor(n, [P, 512], F32))
        onehot = [sb(f"onehot{i}", [P, 4, 2, P], BF16) for i in range(2)]
        stage = [sb(f"codes{i}", [P, 2, NC], F32) for i in range(2)]
        panel = [sb(f"panel{i}", [B, MW], BF16) for i in range(2)]
        extra = sb("w_extra", [B, NB, WP], F32)
        A2, A1, WS = ([pb(f"{n}{i}") for i in range(2)] for n in ("ps_dst", "ps_src", "ps_w"))
        NG = len(GROUPS)
        stored = [sem("panel0_stored"), sem("panel1_stored")]
        padded, staged, oh_ready, counted, moved, added, wdone = map(sem, (
            "padded", "codes_staged", "onehots_ready", "counted", "blocks_moved", "extras_added",
            "w_summed"))
        src1 = t.src1[:].rearrange("p (c b) -> p c b", b=NB)
        dst1 = t.dst1[:].rearrange("p (c b) -> p c b", b=NB)
        wparts = t.wparts[:].rearrange("p (c b) k -> p c b k", b=NB)
        with nc.Block() as block:
            @block.gpsimd
            def _(pool):
                nc.gpsimd.memset(t.mat[0:B, :, V:MW], 0.0)
                for k in range(2):
                    nc.gpsimd.memset(panel[k][:, V:MW], 0.0)
                nc.gpsimd.memset(t.wsum[:], 0.0).then_inc(padded, 1)

            @block.vector
            def _(dve):
                dve.wait_ge(padded, 1)

                def add_extras(b, k):
                    bank = (k * NG + NG - 1) % 2
                    dve.wait_ge(moved, NG * b + NG)
                    v = panel[k][:, bass.ds(b * B, B)]
                    nc.vector.tensor_tensor(v, v, A2[bank][0:B, 128:128 + B], ALU.add)
                    m = t.mat[0:B, bass.ds(b, 1), bass.ds(b * B, B)].rearrange("p o n -> p (o n)")
                    nc.vector.tensor_tensor(m, m, A1[bank][0:B, 128:128 + B], ALU.add)
                    nc.vector.tensor_copy(extra[:, bass.ds(b, 1), :].rearrange("p o w -> p (o w)"),
                                          WS[k][0:B, NB * WP:NC * WP])
                    w = t.wsum[:].rearrange("p b w -> p (b w)")
                    nc.vector.tensor_tensor(w, w, WS[k][0:B, 0:NB * WP], ALU.add).then_inc(added, 1)

                def body(b, k):
                    dve.wait_ge(oh_ready, NG * b)
                    nc.vector.tensor_copy(stage[k][:, 0, :], src1[:, :, bass.ds(b, 1)].rearrange("p c o -> p (c o)"))
                    nc.vector.tensor_copy(stage[k][:, 1, :], dst1[:, :, bass.ds(b, 1)].rearrange("p c o -> p (c o)")
                                          ).then_inc(staged, 1)
                    for g, tiles in enumerate(GROUPS):
                        dve.wait_ge(counted, NG * b + g + 1)
                        if g == 0:
                            dve.wait_ge(staged, b + 1)
                        for i, cc in enumerate(tiles):
                            for e in range(2):
                                last = nc.vector.tensor_scalar(onehot[(k * NG + g) % 2][:, i, e, :], c.iota1_bf[:],
                                                               stage[k][:, e, cc:cc + 1], None, ALU.is_equal)
                        last.then_inc(oh_ready, 1)
                        if g == 1 and not (isinstance(b, int) and b == 0):
                            dve.wait_ge(added, b - 1)
                            add_extras(b - 1, 1 - k)
                in_pairs(dve, NB, body)
                dve.wait_ge(added, NB - 1)
                add_extras(NB - 1, 0)
                dve.wait_ge(added, NB)
                nc.vector.tensor_tensor(t.wsum[:], t.wsum[:], extra[:], ALU.add).then_inc(wdone, 1)

            @block.tensor
            def _(pe):
                pe.sem_inc(counted, 2)

                def body(b, k):
                    for g, tiles in enumerate(GROUPS):
                        bank = (k * NG + g) % 2
                        pe.wait_ge(oh_ready, NG * b + g + 1)
                        if not (isinstance(b, int) and b == 0 and g < 2):
                            pe.wait_ge(moved, NG * b + g - 1)
                        if g == 1 and not (isinstance(b, int) and b == 0):
                            pe.wait_ge(added, b)
                        for i, cc in enumerate(tiles):
                            s1, d1 = onehot[bank][:, i, 0, :], onehot[bank][:, i, 1, :]
                            o = slice(i * B, i * B + B) if cc < NB else slice(128, 128 + B)
                            nc.tensor.matmul(A2[bank][:, o], d1, s1[:, 0:B], start=True, stop=True)
                            nc.tensor.matmul(A1[bank][:, o], s1, d1[:, 0:B], start=True, stop=True)
                            last = nc.tensor.matmul(
                                WS[k][:, cc * WP:(cc + 1) * WP], s1,
                                wparts[:, cc, bass.ds(b, 1), :].rearrange("p o w -> p (o w)"), start=True, stop=True)
                        last.then_inc(counted, 1)
                in_pairs(pe, NB, body)

            @block.scalar
            def _(act):
                act.wait_ge(padded, 1)

                def body(b, k):
                    for g, tiles in enumerate(GROUPS):
                        bank, n = (k * NG + g) % 2, min(len(tiles), NB - tiles[0])
                        act.wait_ge(counted, NG * b + g + 3)
                        if g == 0 and not (isinstance(b, int) and b == 0):
                            act.wait_ge(stored[k], 8 * (b - k))
                        nc.scalar.copy(panel[k][:, tiles[0] * B:(tiles[0] + n) * B], A2[bank][0:B, 0:n * B])
                        nc.scalar.copy(t.mat[0:B, tiles[0]:tiles[0] + n, bass.ds(b * B, B)],
                                       A1[bank][0:B, 0:n * B].rearrange("p (c n) -> p c n", n=B)).then_inc(moved, 1)
                in_pairs(act, NB, body)

            @block.sync
            def _(sp):
                def body(b, k):
                    sp.wait_ge(added, b + 1)
                    sp.dma_start(m2_d[bass.ds(b, 1)].rearrange("o p n -> p (o n)"), panel[k][:]).then_inc(stored[k], 16)
                in_pairs(sp, NB, body)
                sp.wait_ge(stored[0], 16 * (NB + 1) // 2)
                sp.wait_ge(stored[1], 16 * (NB // 2))


def spread(pe, nc, mat, ob, parts, ps):
    for kb in range(NB):
        last = nc.tensor.matmul(ps[:, 0:3 * D], mat[0:B, kb, ob * B:ob * B + P],
                                parts[:, kb].rearrange("p r d -> p (r d)"), start=(kb == 0), stop=(kb == NB - 1))
    return last


def split(nc, S, parts, src, rest):
    S(nc.vector.tensor_copy(parts(0), src))
    S.wait()
    S(nc.vector.tensor_tensor(rest, src, parts(0), ALU.subtract))
    S.wait()
    S(nc.vector.tensor_copy(parts(1), rest))
    S.wait()
    return nc.vector.tensor_tensor(parts(2), rest, parts(1), ALU.subtract)


def normalize(nc, dve, S, y, stats, mv, std, rstd, out, var_ready, std_ready):
    S.wait()
    for b in range(NB):
        last = S(nc.vector.bn_stats(stats[:, b, :], y[:, b, :]))
    S.wait()
    for b in range(NB):
        last = nc.vector.bn_aggr(mv[:, b, :], stats[:, b, :])
    last.then_inc(var_ready, 1)
    dve.wait_ge(std_ready, 1)
    S(nc.vector.reciprocal(rstd[:], std[:]))
    S(nc.vector.tensor_tensor(y[:], y[:], mv[:, :, 0:1].broadcast_to([B, NB, D]), ALU.subtract))
    S.wait()
    return nc.vector.tensor_tensor(out, y[:], rstd[:].unsqueeze(2).broadcast_to([B, NB, D]), ALU.mult)


def roots(nc, act, c, mv, std, var_ready, std_ready):
    act.wait_ge(var_ready, 1)
    nc.scalar.activation(std[:], mv[:, :, 1], ACT.Sqrt, bias=c.eps[0:B, :]).then_inc(std_ready, 1)


def norm_buffers(sb):
    return (sb("bn", [B, NB, 6], F32), sb("mean_var", [B, NB, 2], F32), sb("std", [B, NB], F32),
            sb("rstd", [B, NB], F32))


def gcn_layers(nc, a, c, t):
    with ExitStack() as s:
        sb = lambda n, sh, d: s.enter_context(nc.sbuf_tensor(f"L0_{n}", sh, d))
        sem = lambda n: s.enter_context(nc.semaphore(f"L0_{n}"))
        pb = lambda n: s.enter_context(nc.psum_tensor(f"L0_{n}", [P, 512], F32))
        parts = [sb(f"gparts{i}", [B, NB, 3, D], BF16) for i in range(2)]
        xT, W1, W2 = [sb(f"xT{i}", [D, 8 * B], F32) for i in range(2)], sb("W1", [D, D], F32), sb("W2", [D, D], F32)
        b1, b2 = sb("b1", [D, 1], F32), sb("b2", [B, D], F32)
        rest = sb("rest", [B, 8, D], F32)
        sumr = [sb(f"sumr{i}", [B, D], F32) for i in range(2)]
        hT = [sb(f"hT{i}", [D, B], F32) for i in range(2)]
        bn, mv, std, rstd = norm_buffers(sb)
        psA, psT, psZ = ([pb(f"{n}{i}") for i in range(2)] for n in ("psA", "psT", "psZ"))
        xT_in = [sem("xT0_in"), sem("xT1_in")]
        small_in, x_in, h_ready, parts_ready, sums, summed, turned, relued, z_ready, step, xb, y2, var, root = map(
            sem, ("small_in", "x_in", "h_ready", "parts_ready", "sums_ready", "sum_kept",
                  "turned", "hidden_ready", "z_ready", "gcn_step", "x_bias", "rows_done", "var_ready", "std_ready"))
        groups = [range(g, min(g + 8, NB)) for g in range(0, NB, 8)]
        y = t.xa
        with nc.Block() as block:
            @block.sync
            def _(sp):
                sp.dma_start(W1[:], a["L0_gnn_W1"]).then_inc(small_in, 16)
                sp.dma_start(W2[:], a["L0_gnn_W2"]).then_inc(small_in, 16)
                sp.dma_start(b1[:], a["L0_gnn_b1"].rearrange("(d o) -> d o", o=1)).then_inc(small_in, 16)
                sp.dma_start(b2[:], a["L0_gnn_b2"].partition_broadcast(B)).then_inc(small_in, 16)
                sp.dma_start(t.xb[:], a["x"].rearrange("(b p) d -> p b d", p=B)).then_inc(x_in, 16)
                for g, blocks in enumerate(groups):
                    if g >= 2:
                        sp.wait_ge(h_ready, g - 1)
                    sp.dma_start(xT[g % 2][:, 0:len(blocks) * B], a["xT"][:, blocks[0] * B:(blocks[-1] + 1) * B]
                                 ).then_inc(xT_in[g % 2], 16)

            @block.tensor
            def _(pe):
                pe.wait_ge(small_in, 64)
                for g, blocks in enumerate(groups):
                    pe.wait_ge(xT_in[g % 2], 16 * (g // 2 + 1))
                    if g >= 2:
                        pe.wait_ge(parts_ready, g - 1)
                    for b in blocks:
                        last = nc.tensor.matmul(psZ[g % 2][0:B, (b % 8) * D:(b % 8 + 1) * D], xT[g % 2][:, b % 8 * B:(b % 8 + 1) * B],
                                                W1[:], start=True, stop=True)
                    last.then_inc(h_ready, 1)
                pe.wait_ge(parts_ready, len(groups))

                def turn(b):
                    pe.wait_ge(summed, b + 1)
                    if b >= 2:
                        pe.wait_ge(relued, b - 1)
                    nc.tensor.transpose(psT[b % 2][0:D, 0:B], sumr[b % 2][:], c.ident[0:B, 0:B]).then_inc(turned, 1)

                def times_w2(b):
                    pe.wait_ge(relued, b + 1)
                    if b >= 2:
                        pe.wait_ge(parts_ready, len(groups) + b - 1)
                    nc.tensor.matmul(psZ[b % 2][0:B, 0:D], hT[b % 2][:], W2[:], start=True, stop=True
                                     ).then_inc(z_ready, 1)

                for b in range(NB):
                    if b >= 2:
                        pe.wait_ge(summed, b - 1)
                    spread(pe, nc, t.mat, b, parts[0], psA[b % 2]).then_inc(sums, 1)
                    if b >= 1:
                        turn(b - 1)
                    if b >= 2:
                        times_w2(b - 2)
                turn(NB - 1)
                times_w2(NB - 2)
                times_w2(NB - 1)
                pe.wait_ge(parts_ready, len(groups) + NB)
                for b in range(NB):
                    if b >= 2:
                        pe.wait_ge(y2, b - 1)
                    spread(pe, nc, t.mat, b, parts[1], psA[b % 2]).then_inc(sums, 1)

            @block.scalar
            def _(act):
                act.wait_ge(small_in, 64)
                for b in range(NB):
                    act.wait_ge(turned, b + 1)
                    if b >= 2:
                        act.wait_ge(z_ready, b - 1)
                    nc.scalar.activation(hT[b % 2][:], psT[b % 2][0:D, 0:B], ACT.Relu, bias=b1[:]).then_inc(relued, 1)
                roots(nc, act, c, mv, std, var, root)

            @block.vector
            def _(dve):
                S = Steps(dve, step)

                def hidden_parts(b):
                    dve.wait_ge(z_ready, b + 1)
                    dve.wait_ge(parts_ready, len(groups) + b)
                    split(nc, S, lambda r: parts[1][:, b, r, :], psZ[b % 2][0:B, 0:D], rest[:, 0, :]
                          ).then_inc(parts_ready, 1)

                dve.wait_ge(small_in, 64)
                dve.wait_ge(x_in, 16)
                nc.vector.tensor_tensor(t.xb[:], t.xb[:], b2[:].unsqueeze(1).broadcast_to([B, NB, D]), ALU.add
                                        ).then_inc(xb, 1)
                for g, blocks in enumerate(groups):
                    n, b = len(blocks), blocks[0]
                    src = psZ[g % 2][0:B, 0:n * D].rearrange("p (b d) -> p b d", d=D)
                    dve.wait_ge(h_ready, g + 1)
                    if g:
                        dve.wait_ge(parts_ready, g)
                    split(nc, S, lambda r: parts[0][:, b:b + n, r, :], src, rest[:, 0:n, :]).then_inc(parts_ready, 1)
                for b in range(NB):
                    dve.wait_ge(sums, b + 1)
                    if b >= 2:
                        dve.wait_ge(turned, b - 1)
                    nc.vector.reduce_sum(sumr[b % 2][:], psA[b % 2][0:B, 0:3 * D].rearrange("p (r d) -> p d r", r=3),
                                         X).then_inc(summed, 1)
                    if b >= 2:
                        hidden_parts(b - 2)
                hidden_parts(NB - 2)
                hidden_parts(NB - 1)
                dve.wait_ge(xb, 1)
                for b in range(NB):
                    k = b % 2
                    dve.wait_ge(sums, NB + b + 1)
                    if b == 0:
                        S.wait()
                        dve.wait_ge(summed, NB)
                    else:
                        dve.wait_ge(y2, b)
                    S(nc.vector.reduce_sum(sumr[k][:], psA[k][0:B, 0:3 * D].rearrange("p (r d) -> p d r", r=3), X))
                    S.wait()
                    nc.vector.tensor_tensor(y[:, b, :], sumr[k][:], t.xb[:, b, :], ALU.add).then_inc(y2, 1)
                dve.wait_ge(y2, NB)
                normalize(nc, dve, S, y, bn, mv, std, rstd, t.xb[:], var, root).then_inc(xb, 1)


def edge_network(nc, a, c, t, rows_d, m2_d):
    HEAD = 17
    HOT = NC * P
    with ExitStack() as s:
        sb = lambda n, sh, d: s.enter_context(nc.sbuf_tensor(f"L1_{n}", sh, d))
        sem = lambda n: s.enter_context(nc.semaphore(f"L1_{n}"))
        pb = lambda n: s.enter_context(nc.psum_tensor(f"L1_{n}", [P, 512], F32))
        room = t.mat[:, HEAD:NB, :].rearrange("p a b -> p (a b)")
        q = room[:, 0:NB * 3 * H].rearrange("p (b r h) -> p b r h", r=3, h=H)
        o = NB * 3 * H
        x1T = room[0:D, o:o + 2 * (NB + 1) * B].bitcast(F32)
        o += 2 * (NB + 1) * B
        srow = [room[:, o + i * HOT:o + (i + 1) * HOT] for i in range(2)]
        drow = [sb(f"drow{i}", [P, HOT], BF16) for i in range(2)]
        eWa, eWb, eW2 = sb("eWa", [D, H], F32), sb("eWb", [D, H], F32), sb("eW2", [H, H], F32)
        nWa, nWb, nW2 = sb("nWa", [D, H], F32), sb("nWb", [H, H], F32), sb("nW2", [H, D], F32)
        eb1, nb1, nb2 = sb("eb1", [H, 1], F32), sb("nb1", [H, 1], F32), sb("nb2", [B, D], F32)
        wd, eb2 = sb("wd", [P, H], F32), sb("eb2", [96, H], F32)
        wd3, eb3 = sb("wd3", [P, 3, H], BF16), sb("eb3", [96, 3, H], BF16)
        eb2x = sb("eb2x", [96, 4, H], BF16)
        o += 2 * HOT
        rest = room[:, o:o + 8 * H].bitcast(F32)
        rest2 = room[:, o + 8 * H:o + 16 * H].bitcast(F32)
        pp = [sb(f"pp{i}", [B, 3, H], BF16) for i in range(2)]
        xs = [sb(f"xs{i}", [D, B], F32) for i in range(2)]
        codes = [sb(f"scodes{i}", [P, NC], F32) for i in range(2)]
        hot = [sb(f"hot{i}", [P, 4, B], F32) for i in range(2)]
        e1 = [sb("e1", [H, 4 * P], F32), rest2]
        e2 = [sb(f"e2_{i}", [P, 4 * H], F32) for i in range(2)]
        aggs = [sb(f"aggs{i}", [H, B], F32) for i in range(2)]
        z1 = sb("z1", [H, B], F32)
        bn, mv, std, rstd = norm_buffers(sb)
        ps_pre, ps_z2, ps_agg = ([pb(f"{n}{i}") for i in range(2)] for n in ("ps_pre", "ps_z2", "ps_agg"))
        ps_n, ps_p = pb("ps_n"), pb("ps_p")
        w_in, turned, x1t_ready, q_ps, q_done, prep, wd_set, q_tail = map(sem, (
            "weights_in", "x1_turned", "x1T_ready", "q_ready", "q_split", "prep_step", "wd_parts", "q_tail"))
        NG = len(GROUPS)
        tile_groups = [range(g, min(g + 4, NB)) for g in range(0, NB, 4)]
        with nc.Block() as block:
            @block.sync
            def _(sp):
                n = "L1_gnn_"
                for out_, in_ in ((eWa[:], a[n + "eW1"][0:D]), (eWb[:], a[n + "eW1"][D:2 * D]), (eW2[:], a[n + "eW2"]),
                                  (nWa[:], a[n + "nW1"][0:D]), (nWb[:], a[n + "nW1"][D:D + H]), (nW2[:], a[n + "nW2"]),
                                  (eb1[:], a[n + "eb1"].rearrange("(d o) -> d o", o=1)),
                                  (nb1[:], a[n + "nb1"].rearrange("(d o) -> d o", o=1)),
                                  (nb2[:], a[n + "nb2"].partition_broadcast(B)),
                                  (wd[:], a[n + "eW1"][2 * D].partition_broadcast(P)),
                                  (eb2[:], a[n + "eb2"].partition_broadcast(96))):
                    sp.dma_start(out_, in_).then_inc(w_in, 16)
                sp.wait_ge(w_in, 16 * 11)

            @block.gpsimd
            def _(pool):
                nc.gpsimd.memset(x1T[:, NB * B:], 0.0)

            @block.tensor
            def _(pe):
                for g, blocks in enumerate(tile_groups):
                    if g >= 2:
                        pe.wait_ge(x1t_ready, g - 1)
                    for i, b in enumerate(blocks):
                        last = nc.tensor.transpose(ps_pre[g % 2][0:D, i * P:i * P + B], t.xb[:, b, :],
                                                   c.ident[0:B, 0:B])
                    last.then_inc(turned, 1)
                pe.wait_ge(w_in, 16 * 11)
                for g, blocks in enumerate(tile_groups):
                    pe.wait_ge(x1t_ready, g + 1)
                    if g >= 2:
                        pe.wait_ge(q_done, g - 1)
                    for i, b in enumerate(blocks):
                        last = nc.tensor.matmul(ps_z2[g % 2][0:B, i * H:(i + 1) * H], x1T[:, b * B:(b + 1) * B],
                                                eWb[:], start=True, stop=True)
                    last.then_inc(q_ps, 1)

            @block.scalar
            def _(act):
                for g, blocks in enumerate(tile_groups):
                    act.wait_ge(turned, g + 1)
                    n = len(blocks)
                    nc.scalar.copy(x1T[:, 4 * g * B:(4 * g + n) * B].rearrange("p (b n) -> p b n", n=B),
                                   ps_pre[g % 2][0:D, 0:n * P].rearrange("p (b n) -> p b n", n=P)[:, :, 0:B]
                                   ).then_inc(x1t_ready, 1)
                act.wait_ge(wd_set, 1)
                for r in range(3):
                    last = nc.scalar.copy(q[96:P, :, r, :], wd3[96:P, r, :].unsqueeze(1).broadcast_to([32, NB, H]))
                last.then_inc(q_tail, 1)

            @block.vector
            def _(dve):
                S = Steps(dve, prep)
                S(nc.vector.memset(eb2x[:], 0.0))
                dve.wait_ge(w_in, 16 * 11)
                split(nc, S, lambda r: wd3[:, r, :], wd[:], rest[:, 0:H]).then_inc(wd_set, 1)
                S(split(nc, S, lambda r: eb3[:, r, :], eb2[:], rest[0:96, H:2 * H]))
                S.wait()
                for r in range(3):
                    for i in range(4):
                        S(nc.vector.tensor_copy(eb2x[32 * r:32 * r + 1, i, :], eb3[32 * r:32 * r + 1, r, :]))
                dve.wait_ge(turned, len(tile_groups))
                S(nc.vector.tensor_tensor(t.xb[:], t.xb[:], nb2[:].unsqueeze(1).broadcast_to([B, NB, D]), ALU.add))
                dve.wait_ge(q_tail, 1)
                for g, blocks in enumerate(tile_groups):
                    n, b = len(blocks), blocks[0]
                    dve.wait_ge(q_ps, g + 1)
                    if g:
                        dve.wait_ge(q_done, g)
                    else:
                        S.wait()
                    split(nc, S, lambda r: q[0:B, b:b + n, r, :],
                          ps_z2[g % 2][0:B, 0:n * H].rearrange("p (b h) -> p b h", h=H),
                          rest[0:B, 0:n * H].rearrange("p (b h) -> p b h", h=H)).then_inc(q_done, 1)

        rows_in = [sem("rows0_in"), sem("rows1_in")]
        (panels_in, rows_hot, staged, pre_done, e1_ready, z2_done, e2_ready, hot_ready, seg_done, agg_ready, n1_ready,
         z1_ready, out_ready, out_kept, xs_ready, p_ps, p_ready, var, root, step) = map(sem, (
             "panels_in", "rows_hot", "codes_staged", "pre_done", "e1_ready", "z2_done", "e2_ready", "onehots_ready",
             "seg_done", "agg_ready", "n1_ready", "z1_ready", "out_ready", "out_kept", "xs_ready", "p_product",
             "p_ready", "var_ready", "std_ready", "net_step"))
        rows = rows_d.rearrange("(f c b r) -> f c b r", f=5, c=NC, r=P)
        first = lambda b: isinstance(b, int) and b == 0
        one = lambda ap: ap.rearrange("o n -> (o n)")
        with nc.Block() as block:
            @block.sync
            def _(sp):
                def body(b, k):
                    if not first(b):
                        sp.wait_ge(pre_done, NG * (b - 1))
                    for buf, f in ((srow, 0), (drow, 1)):
                        sp.dma_start(buf[k][0:B, 0:NB * P],
                                     one(rows[f, bass.ds(b, 1)].rearrange("o b r -> o (b r)")).partition_broadcast(B)
                                     ).then_inc(rows_in[k], 16)
                        sp.dma_start(buf[k][0:B, NB * P:HOT],
                                     one(rows[f, NB, bass.ds(b, 1)]).partition_broadcast(B)).then_inc(rows_in[k], 16)
                    sp.dma_start(drow[k][B:P, 0:NB * P], rows[2:5, bass.ds(b, 1)].rearrange("f o b r -> f (o b r)")
                                 ).then_inc(rows_in[k], 16)
                    sp.dma_start(drow[k][B:P, NB * P:HOT], rows[2:5, NB, bass.ds(b, 1)].rearrange("f o r -> f (o r)")
                                 ).then_inc(rows_in[k], 16)
                in_pairs(sp, NB, body)
                sp.wait_ge(panels_in, 16 * HEAD)

            @block.gpsimd
            def _(pool):
                with pool.Fori(0, HEAD) as i:
                    pool.wait_ge(pre_done, NG * i)
                    pool.wait_ge(xs_ready, 1)
                    pool.dma_start(t.mat[0:B, bass.ds(i, 1), :].rearrange("p o n -> p (o n)"),
                                   m2_d[bass.ds(i, 1)].rearrange("o p n -> p (o n)")).then_inc(panels_in, 16)

            @block.tensor
            def _(pe):
                def product_p(b, k):
                    pe.wait_ge(xs_ready, b + 1)
                    nc.tensor.matmul(ps_p[0:B, 0:H], xs[k][:], eWa[:], start=True, stop=True).then_inc(p_ps, 1)

                def layer1(b, k, g):
                    bank, tiles = (k * NG + g) % 2, GROUPS[g]
                    lo, hi = tiles[0] * P, (tiles[-1] + 1) * P
                    if g == 0:
                        pe.wait_ge(rows_hot, b + 1)
                        pe.wait_ge(p_ready, b + 1)
                    if not (first(b) and g < 2):
                        pe.wait_ge(e1_ready, NG * b + g - 1)
                    for r in range(3):
                        nc.tensor.matmul(ps_pre[bank][:, 0:hi - lo], pp[k][:, r, :], srow[k][0:B, lo:hi],
                                         start=(r == 0), stop=False)
                    for i, cc in enumerate(tiles):
                        for r in range(3):
                            w = (q[:, cc, r, :] if cc < NB else
                                 q[:, bass.ds(b, 1), r, :].rearrange("p o h -> p (o h)"))
                            last = nc.tensor.matmul(ps_pre[bank][:, i * P:(i + 1) * P], w,
                                                    drow[k][:, cc * P:(cc + 1) * P], start=False,
                                                    stop=(r == 2 and cc == tiles[-1]))
                    last.then_inc(pre_done, 1)

                def layer2(b, k, g):
                    bank, tiles = (k * NG + g) % 2, GROUPS[g]
                    pe.wait_ge(e1_ready, NG * b + g + 1)
                    if not (first(b) and g < 2):
                        pe.wait_ge(e2_ready, NG * b + g - 1)
                    nc.tensor.matmul(ps_z2[bank][:, 0:len(tiles) * H], c.ones_bf[0:96, :],
                                     eb2x[:, 0:len(tiles), :].rearrange("p i h -> p (i h)"), start=True, stop=False)
                    for i, cc in enumerate(tiles):
                        last = nc.tensor.matmul(ps_z2[bank][:, i * H:(i + 1) * H], e1[bank][:, i * P:(i + 1) * P],
                                                eW2[:], start=False, stop=(cc == tiles[-1]))
                    last.then_inc(z2_done, 1)

                def by_src(b, k, g):
                    bank, tiles = (k * NG + g) % 2, GROUPS[g]
                    pe.wait_ge(e2_ready, NG * b + g + 1)
                    pe.wait_ge(hot_ready, NG * b + g + 1)
                    if g == 0 and not first(b):
                        pe.wait_ge(agg_ready, b - 1)
                    for i, cc in enumerate(tiles):
                        last = nc.tensor.matmul(ps_agg[k][:, 0:B], e2[bank][:, i * H:(i + 1) * H], hot[bank][:, i, :],
                                                start=(cc == 0), stop=(cc == NC - 1))
                    last.then_inc(seg_done, 1)

                def node1(b, k):
                    pe.wait_ge(agg_ready, b + 1)
                    if not first(b):
                        pe.wait_ge(out_kept, b)
                    nc.tensor.matmul(ps_n[:, 0:B], nWa[:], xs[k][:], start=True, stop=False)
                    nc.tensor.matmul(ps_n[:, 0:B], nWb[:], aggs[k][:], start=False, stop=True).then_inc(n1_ready, 1)

                def node2(b, k):
                    pe.wait_ge(z1_ready, b + 1)
                    nc.tensor.matmul(ps_n[0:B, 256:256 + D], z1[:], nW2[:], start=True, stop=True
                                     ).then_inc(out_ready, 1)

                def body(b, k):
                    was = None if first(b) else (b - 1, 1 - k)
                    for g in range(NG):
                        layer1(b, k, g)
                        if g >= 1:
                            layer2(b, k, g - 1)
                        elif was:
                            layer2(*was, NG - 1)
                        if g >= 2:
                            by_src(b, k, g - 2)
                        elif was:
                            by_src(*was, NG - 2 + g)
                        if was and g == 2:
                            node1(*was)
                        if was and g == 3:
                            node2(*was)
                        if g == 4:
                            product_p(b + 1, 1 - k)
                product_p(0, 0)
                in_pairs(pe, NB, body)
                z = NB - 1
                layer2(z, 0, NG - 1)
                by_src(z, 0, NG - 2)
                by_src(z, 0, NG - 1)
                node1(z, 0)
                node2(z, 0)

            @block.scalar
            def _(act):
                def stage_x(b, k):
                    nc.scalar.copy(xs[k][:], x1T[:, bass.ds(b * B, B)]).then_inc(xs_ready, 1)

                def silu1(b, k, g):
                    bank, n = (k * NG + g) % 2, len(GROUPS[g]) * P
                    act.wait_ge(pre_done, NG * b + g + 1)
                    if not (first(b) and g < 2):
                        act.wait_ge(z2_done, NG * b + g - 1)
                    nc.scalar.activation(e1[bank][:, 0:n], ps_pre[bank][:, 0:n], ACT.Silu, bias=eb1[:]
                                         ).then_inc(e1_ready, 1)

                def silu2(b, k, g):
                    bank, n = (k * NG + g) % 2, len(GROUPS[g]) * H
                    act.wait_ge(z2_done, NG * b + g + 1)
                    if not (first(b) and g < 2):
                        act.wait_ge(seg_done, NG * b + g - 1)
                    nc.scalar.activation(e2[bank][:, 0:n], ps_z2[bank][:, 0:n], ACT.Silu).then_inc(e2_ready, 1)

                def keep_agg(b, k):
                    act.wait_ge(seg_done, NG * b + NG)
                    act.wait_ge(n1_ready, b)
                    nc.scalar.copy(aggs[k][:], ps_agg[k][:, 0:B]).then_inc(agg_ready, 1)

                def node_silu(b, k):
                    act.wait_ge(n1_ready, b + 1)
                    if not first(b):
                        act.wait_ge(out_ready, b)
                    nc.scalar.activation(z1[:], ps_n[:, 0:B], ACT.Silu, bias=nb1[:]).then_inc(z1_ready, 1)

                def body(b, k):
                    was = None if first(b) else (b - 1, 1 - k)
                    for g in range(NG):
                        silu1(b, k, g)
                        if g >= 1:
                            silu2(b, k, g - 1)
                        elif was:
                            silu2(*was, NG - 1)
                        if was and g == 1:
                            keep_agg(*was)
                        if was and g == 2:
                            node_silu(*was)
                        if g == 3:
                            act.wait_ge(p_ps, b + 1)
                            stage_x(b + 1, 1 - k)
                stage_x(0, 0)
                in_pairs(act, NB, body)
                z = NB - 1
                silu2(z, 0, NG - 1)
                keep_agg(z, 0)
                node_silu(z, 0)
                roots(nc, act, c, mv, std, var, root)

            @block.vector
            def _(dve):
                S = Steps(dve, step)

                def split_p(b, k):
                    dve.wait_ge(p_ps, b + 1)
                    if not first(b):
                        dve.wait_ge(p_ready, b)
                        dve.wait_ge(pre_done, NG * (b - 1))
                    dve.wait_ge(step, 3 * b if not isinstance(b, int) else 3 * b)
                    v = nc.vector
                    v.tensor_copy(pp[k][:, 0, :], ps_p[0:B, 0:H]).then_inc(step, 1)
                    dve.wait_ge(step, 3 * b + 1)
                    v.tensor_tensor(rest[0:B, 0:H], ps_p[0:B, 0:H], pp[k][:, 0, :], ALU.subtract).then_inc(step, 1)
                    dve.wait_ge(step, 3 * b + 2)
                    v.tensor_copy(pp[k][:, 1, :], rest[0:B, 0:H]).then_inc(step, 1)
                    dve.wait_ge(step, 3 * b + 3)
                    v.tensor_tensor(pp[k][:, 2, :], rest[0:B, 0:H], pp[k][:, 1, :], ALU.subtract).then_inc(p_ready, 1)

                def keep_out(b, k):
                    dve.wait_ge(out_ready, b + 1)
                    nc.vector.tensor_tensor(t.xa[:, bass.ds(b, 1), :].rearrange("p o d -> p (o d)"),
                                            ps_n[0:B, 256:256 + D],
                                            t.xb[:, bass.ds(b, 1), :].rearrange("p o d -> p (o d)"), ALU.add
                                            ).then_inc(out_kept, 1)

                def body(b, k):
                    if not first(b):
                        dve.wait_ge(hot_ready, NG * (b - 1))
                    nc.vector.tensor_copy(codes[k][:, 0:NB], t.src1[:, bass.ds(b * NB, NB)])
                    nc.vector.tensor_copy(codes[k][:, NB:NC], t.src1[:, bass.ds(b + NB * NB, 1)]).then_inc(staged, 1)
                    dve.wait_ge(rows_in[k], 48 * (b - k) + 96)
                    nc.vector.tensor_scalar(srow[k][0:B, :], srow[k][0:B, :], c.row1[0:B, :], None, ALU.is_equal)
                    nc.vector.tensor_scalar(drow[k][0:B, :], drow[k][0:B, :], c.row1[0:B, :], None, ALU.is_equal
                                            ).then_inc(rows_hot, 1)
                    dve.wait_ge(staged, b + 1)
                    for g, tiles in enumerate(GROUPS):
                        bank = (k * NG + g) % 2
                        if not (first(b) and g < 2):
                            dve.wait_ge(seg_done, NG * b + g - 1)
                        for i, cc in enumerate(tiles):
                            last = nc.vector.tensor_scalar(hot[bank][:, i, :], c.iota1[:, 0:B],
                                                           codes[k][:, cc:cc + 1], None, ALU.is_equal)
                        last.then_inc(hot_ready, 1)
                        if g == 4 and not first(b):
                            keep_out(b - 1, 1 - k)
                        if g == 5:
                            split_p(b + 1, 1 - k)
                split_p(0, 0)
                in_pairs(dve, NB, body)
                keep_out(NB - 1, 0)
                dve.wait_ge(out_kept, NB)
                S.n = 3 * (NB + 1)
                normalize(nc, dve, S, t.xa, bn, mv, std, rstd, t.xb[:], var, root)


def message_layer(nc, a, c, t, m2_d, HEAD=17):
    with ExitStack() as s:
        sb = lambda n, sh, d: s.enter_context(nc.sbuf_tensor(f"L2_{n}", sh, d))
        sem = lambda n: s.enter_context(nc.semaphore(f"L2_{n}"))
        pb = lambda n: s.enter_context(nc.psum_tensor(f"L2_{n}", [P, 512], F32))
        parts = sb("parts", [B, NB, 3, D], BF16)
        base = sb("base", [B, NB, D], F32)
        x2T = [sb(f"x2T{i}", [D, 4 * B], F32) for i in range(2)]
        hmuT = [sb(f"hmuT{i}", [D, 4 * B], F32) for i in range(2)]
        nv = [sb(f"nv{i}", [2, 4 * B], F32) for i in range(2)]
        W3T, W4a, W4b, W4c = (sb(n, [D, D], F32) for n in ("W3T", "W4a", "W4b", "W4c"))
        w1c, w2c, w1r = sb("w1c", [D, 1], F32), sb("w2c", [D, 1], F32), sb("w1r", [2, D], F32)
        w1pm, w2pm, gx, ge = (sb("w1pm", [D, 2], F32), sb("w2pm", [D, 2, B], F32), sb("gx", [2, D], F32),
                              sb("ge", [B, 2, D], F32))
        we = sb("we", [B, NB, 2], F32)
        sumr = [sb(f"sumr{i}", [B, D], F32) for i in range(2)]
        rest = sb("rest", [B, 4, D], F32)
        bn, mv, std, rstd = norm_buffers(sb)
        psT, psM, psZ, psH = ([pb(f"{n}{i}") for i in range(2)] for n in ("psT", "psM", "psZ", "psH"))
        nv_in = [sem("nv0_in"), sem("nv1_in")]
        (w_in, tail_in, turned, x2t, hmu_ps, hmut, z_ps, parts_ready, nv_set, w_set, g_ps, g_set, sums, kept, var, root,
         step) = map(sem, ("weights_in", "tail_in", "x2_turned", "x2T_ready", "hmu_product", "hmuT_ready", "z_product",
                           "parts_ready", "nv_set", "w_parts", "g_product", "g_set", "sums_ready", "rows_kept",
                           "var_ready", "std_ready", "msg_step"))
        groups = [range(g, min(g + 4, NB)) for g in range(0, NB, 4)]
        with nc.Block() as block:
            @block.sync
            def _(sp):
                n = "L2_gnn_"
                for out_, in_ in ((W3T[:], a["W3T"]), (W4a[:], a["W4T"][0:D]), (W4b[:], a["W4T"][D:2 * D]),
                                  (W4c[:], a["W4T"][2 * D:3 * D]), (w1c[:], a[n + "W1"]), (w2c[:], a[n + "W2"]),
                                  (w1r[:], a[n + "W1"].rearrange("d o -> (d o)").partition_broadcast(2))):
                    sp.dma_start(out_, in_).then_inc(w_in, 16)
                for g, blocks in enumerate(groups):
                    if g >= 2:
                        sp.wait_ge(z_ps, g - 1)
                    lo, hi = blocks[0] * B, (blocks[-1] + 1) * B
                    sp.dma_start(nv[g % 2][:, 0:hi - lo], a["node_vec1"][lo:hi].partition_broadcast(2)
                                 ).then_inc(nv_in[g % 2], 16)

            @block.scalar
            def _(act):
                act.dma_start(t.mat[0:B, HEAD:NB, :], m2_d[HEAD:NB].rearrange("b p n -> p b n")).then_inc(tail_in, 16)
                for g, blocks in enumerate(groups):
                    n = len(blocks)
                    act.wait_ge(turned, g + 1)
                    if g >= 2:
                        act.wait_ge(z_ps, g - 1)
                    nc.scalar.copy(x2T[g % 2][:, 0:n * B].rearrange("p (b n) -> p b n", n=B),
                                   psT[g % 2][0:D, 0:n * P].rearrange("p (b n) -> p b n", n=P)[:, :, 0:B]
                                   ).then_inc(x2t, 1)
                    act.wait_ge(hmu_ps, g + 1)
                    nc.scalar.activation(hmuT[g % 2][:, 0:n * B], psM[g % 2][0:D, 0:n * B], ACT.Relu).then_inc(hmut, 1)
                roots(nc, act, c, mv, std, var, root)

            @block.tensor
            def _(pe):
                def turn(g):
                    if g >= 2:
                        pe.wait_ge(x2t, g - 1)
                    for i, b in enumerate(groups[g]):
                        last = nc.tensor.transpose(psT[g % 2][0:D, i * P:i * P + B], t.xb[:, b, :], c.ident[0:B, 0:B])
                    last.then_inc(turned, 1)
                turn(0)
                pe.wait_ge(w_in, 16 * 7)
                pe.wait_ge(w_set, 1)
                nc.tensor.matmul(psH[1][0:2, 128:128 + D], w1pm[:], W4a[:], start=True, stop=True)
                for i in range(2):
                    last = nc.tensor.matmul(psH[1][0:B, i * D:(i + 1) * D], w2pm[:, i, :], W4b[:], start=True,
                                            stop=True)
                last.then_inc(g_ps, 1)
                for g, blocks in enumerate(groups):
                    k, n = g % 2, len(blocks)
                    if g + 1 < len(groups):
                        turn(g + 1)
                    pe.wait_ge(x2t, g + 1)
                    if g >= 2:
                        pe.wait_ge(hmut, g - 1)
                    nc.tensor.matmul(psM[k][0:D, 0:n * B], W3T[:], x2T[k][:, 0:n * B], start=True, stop=True
                                     ).then_inc(hmu_ps, 1)
                    if g >= 2:
                        pe.wait_ge(parts_ready, g - 1)
                    pe.wait_ge(nv_set, g + 1)
                    pe.wait_ge(g_set, 1)
                    pe.wait_ge(hmut, g + 1)
                    for i in range(n):
                        cols = slice(i * B, (i + 1) * B)
                        nc.tensor.matmul(psZ[k][0:B, 256 + i * D:256 + (i + 1) * D], x2T[k][:, cols], W3T[:],
                                         start=True, stop=True)
                        nc.tensor.matmul(psH[k][0:B, 256 + i * D:256 + (i + 1) * D], nv[k][:, cols], w1r[:],
                                         start=True, stop=True)
                        nc.tensor.matmul(psZ[k][0:B, i * D:(i + 1) * D], hmuT[k][:, cols], W4c[:], start=True,
                                         stop=False)
                        last = nc.tensor.matmul(psZ[k][0:B, i * D:(i + 1) * D], nv[k][:, cols], gx[:], start=False,
                                                stop=True)
                    last.then_inc(z_ps, 1)
                pe.wait_ge(tail_in, 16)
                pe.wait_ge(parts_ready, len(groups))
                for b in range(NB):
                    if b >= 2:
                        pe.wait_ge(kept, b - 1)
                    spread(pe, nc, t.mat, b, parts, psT[b % 2]).then_inc(sums, 1)

            @block.vector
            def _(dve):
                S = Steps(dve, step)
                v = nc.vector
                dve.wait_ge(w_in, 16 * 7)
                S(v.tensor_scalar(w1pm[:, 0:1], w1c[:], 0.0, None, ALU.max))
                S(v.tensor_scalar(w1pm[:, 1:2], w1c[:], -1.0, 0.0, ALU.mult, ALU.max))
                S(v.tensor_scalar(w2pm[:, 0, :], c.ones[0:D, 0:B], w2c[:], 0.0, ALU.mult, ALU.max))
                S(v.tensor_scalar(w2pm[:, 1, :], c.ones[0:D, 0:B], w2c[:], -1.0, ALU.mult, ALU.mult))
                S(v.tensor_scalar(w1r[:], w1r[:], c.sign[0:2, :], 0.0, ALU.mult, ALU.max))
                S(v.reduce_sum(we[:], t.wsum[:, :, 0:6].rearrange("p b (s r) -> p b s r", r=3), X))
                S.wait()
                v.tensor_scalar(w2pm[:, 1, :], w2pm[:, 1, :], 0.0, None, ALU.max).then_inc(w_set, 1)
                dve.wait_ge(g_ps, 1)
                v.tensor_copy(ge[:].rearrange("p s d -> p (s d)"), psH[1][0:B, 0:2 * D])
                v.tensor_copy(gx[:], psH[1][0:2, 128:128 + D]).then_inc(g_set, 1)
                for g, blocks in enumerate(groups):
                    k, n, b = g % 2, len(blocks), blocks[0]
                    dve.wait_ge(nv_in[k], 16 * (g // 2 + 1))
                    v.tensor_scalar(nv[k][:, 0:n * B], nv[k][:, 0:n * B], c.sign[0:2, :], 0.0, ALU.mult, ALU.max
                                    ).then_inc(nv_set, 1)
                    dve.wait_ge(z_ps, g + 1)
                    grp = lambda ap: ap.rearrange("p (b d) -> p b d", d=D)
                    S(v.tensor_scalar(base[:, b:b + n, :], grp(psZ[k][0:B, 256:256 + n * D]), 0.0, None, ALU.max))
                    S.wait()
                    S(v.tensor_tensor(base[:, b:b + n, :], base[:, b:b + n, :], grp(psH[k][0:B, 256:256 + n * D]),
                                      ALU.add))
                    if g:
                        dve.wait_ge(parts_ready, g)
                    split(nc, S, lambda r: parts[:, b:b + n, r, :], grp(psZ[k][0:B, 0:n * D]), rest[:, 0:n, :]
                          ).then_inc(parts_ready, 1)
                dve.wait_ge(parts_ready, len(groups))
                for b in range(NB):
                    r = sumr[b % 2][:]
                    dve.wait_ge(sums, b + 1)
                    if b >= 1:
                        dve.wait_ge(kept, b)
                    S(v.reduce_sum(r, psT[b % 2][0:B, 0:3 * D].rearrange("p (r d) -> p d r", r=3), X))
                    S.wait()
                    for i in range(2):
                        S(v.scalar_tensor_tensor(r, ge[:, i, :], we[:, b, i:i + 1], r, ALU.mult, ALU.add))
                        S.wait()
                    S(v.scalar_tensor_tensor(r, r, 0.0, base[:, b, :], ALU.max, ALU.add))
                    S.wait()
                    v.scalar_tensor_tensor(t.xa[:, b, :], r, 0.0, t.xb[:, b, :], ALU.max, ALU.add).then_inc(kept, 1)
                dve.wait_ge(kept, NB)
                normalize(nc, dve, S, t.xa, bn, mv, std, rstd, t.xb[:], var, root)


def polynomial_layer(nc, a, c, t, out):
    with ExitStack() as s:
        sb = lambda n, sh, d: s.enter_context(nc.sbuf_tensor(f"L3_{n}", sh, d))
        sem = lambda n: s.enter_context(nc.semaphore(f"L3_{n}"))
        pb = lambda n: s.enter_context(nc.psum_tensor(f"L3_{n}", [P, 512], F32))
        parts = [sb(f"parts{i}", [B, NB, 3, D], BF16) for i in range(2)]
        x3T = sb("x3T", [D, V], F32)
        Wk = sb("Wk", [D, KMAX + 1, D], F32)
        wk = [sb(f"wk{i}", [D, D], F32) for i in range(2)]
        bias = sb("bias", [B, D], F32)
        some, root_deg, dinv = sb("some", [B, NB], F32), sb("root_deg", [B, NB], F32), sb("dinv", [B, NB], F32)
        safe = sb("safe", [B, NB], F32)
        sumr, diff, rest = ([sb(f"{n}{i}", [B, D], F32) for i in range(2)] for n in ("sumr", "diff", "rest"))
        old = lambda lo, hi: t.src1[0:B, lo * NB:hi * NB].rearrange("p (b s) -> p b s", s=hi - lo)
        bn, mv = old(0, 6), old(6, 8)
        std, rstd = t.src1[0:B, 8 * NB:9 * NB], t.src1[0:B, 9 * NB:10 * NB]
        scaled = t.src1[0:B, 10 * NB:10 * NB + 4 * D].rearrange("p (b d) -> p b d", d=D)
        psT, psA, psY = ([pb(f"{n}{i}") for i in range(2)] for n in ("psT", "psA", "psY"))
        (w_in, turned, x3t, wk_set, wk_staged, deg_set, droot, y_ps, parts_ready, sums, bank_free, var, root, step, stored
         ) = map(sem, ("weights_in", "x3_turned", "x3T_ready", "Wk_scaled", "wk_staged", "deg_set", "deg_root", "y_product",
                       "parts_ready", "sums_ready", "bank_read", "var_ready", "std_ready", "poly_step", "out_stored"))
        groups = [range(g, min(g + 4, NB)) for g in range(0, NB, 4)]
        y = t.xa
        PER = 6
        with nc.Block() as block:
            @block.sync
            def _(sp):
                sp.dma_start(Wk[:], a["L3_gnn_W"].rearrange("k i o -> i k o")).then_inc(w_in, 16)
                sp.dma_start(bias[:], a["L3_gnn_bias"].partition_broadcast(B)).then_inc(w_in, 16)

            @block.scalar
            def _(act):
                act.wait_ge(w_in, 32)
                inv = 1.0
                for k in range(1, KMAX + 1):
                    inv /= k
                    last = nc.scalar.mul(Wk[:, k, :], Wk[:, k, :], inv)
                last.then_inc(wk_set, 1)
                act.wait_ge(deg_set, 1)
                nc.scalar.activation(root_deg[:], safe[:], ACT.Sqrt).then_inc(droot, 1)
                for g, blocks in enumerate(groups):
                    n = len(blocks)
                    act.wait_ge(turned, g + 1)
                    nc.scalar.copy(x3T[:, 4 * g * B:(4 * g + n) * B].rearrange("p (b n) -> p b n", n=B),
                                   psT[g % 2][0:D, 0:n * P].rearrange("p (b n) -> p b n", n=P)[:, :, 0:B]
                                   ).then_inc(x3t, 1)

                def stage(it, k):
                    act.wait_ge(sums, NB * it)
                    nc.scalar.copy(wk[k][:], Wk[:, bass.ds(KMAX - 1 - it, 1), :].rearrange("p o d -> p (o d)")
                                   ).then_inc(wk_staged, 1)

                act.wait_ge(wk_set, 1)
                with act.Fori(0, KMAX, 2) as it:
                    it = it.with_bounds(min_val=0, max_val=KMAX - 2)
                    stage(it, 0)
                    stage((it + 1).with_bounds(min_val=1, max_val=KMAX - 1), 1)
                roots(nc, act, c, mv, std, var, root)

            @block.tensor
            def _(pe):
                for g, blocks in enumerate(groups):
                    if g >= 2:
                        pe.wait_ge(x3t, g - 1)
                    for i, b in enumerate(blocks):
                        last = nc.tensor.transpose(psT[g % 2][0:D, i * P:i * P + B], t.xb[:, b, :], c.ident[0:B, 0:B])
                    last.then_inc(turned, 1)
                pe.wait_ge(wk_set, 1)
                for g, blocks in enumerate(groups):
                    pe.wait_ge(x3t, g + 1)
                    if g >= 2:
                        pe.wait_ge(parts_ready, 4 * (g - 1))
                    for i, b in enumerate(blocks):
                        last = nc.tensor.matmul(psY[g % 2][0:B, i * D:(i + 1) * D], x3T[:, b * B:(b + 1) * B],
                                                Wk[:, KMAX, :], start=True, stop=True)
                    last.then_inc(y_ps, 1)

                def term(it, src):
                    for b in range(NB):
                        ps = psA[(NB * src + b) % 2]
                        pe.wait_ge(bank_free, NB * it + b + 1)
                        if b == 0:
                            pe.wait_ge(wk_staged, it + 1)
                        nc.tensor.matmul(ps[0:B, 256:256 + D], x3T[:, b * B:(b + 1) * B], wk[src][:], start=True,
                                         stop=True)
                        for kb in range(NB):
                            if b == 0:
                                pe.wait_ge(parts_ready, NB * it + kb + 1)
                            last = nc.tensor.matmul(ps[:, 0:3 * D], t.mat[0:B, kb, b * B:b * B + P],
                                                    parts[src][:, kb].rearrange("p r d -> p (r d)"),
                                                    start=(kb == 0), stop=(kb == NB - 1))
                        last.then_inc(sums, 1)

                with pe.Fori(0, KMAX, 2) as it:
                    it = it.with_bounds(min_val=0, max_val=KMAX - 2)
                    term(it, 0)
                    term((it + 1).with_bounds(min_val=1, max_val=KMAX - 1), 1)

            @block.vector
            def _(dve):
                S = Steps(dve, step)
                v = nc.vector
                dve.sem_inc(bank_free, 2)
                deg = t.wsum[:, :, WP - 1]
                S(v.tensor_scalar(some[:], deg, 0.0, None, ALU.is_gt))
                v.tensor_scalar(safe[:], deg, 1.0, None, ALU.max).then_inc(deg_set, 1)
                dve.wait_ge(droot, 1)
                S(v.reciprocal(dinv[:], root_deg[:]))
                S.wait()
                S(v.tensor_tensor(dinv[:], dinv[:], some[:], ALU.mult))
                dve.wait_ge(w_in, 32)
                dve.wait_ge(turned, len(groups))
                S(v.tensor_tensor(t.xb[:], t.xb[:], bias[:].unsqueeze(1).broadcast_to([B, NB, D]), ALU.add))
                S.wait()
                for g, blocks in enumerate(groups):
                    n, b = len(blocks), blocks[0]
                    dve.wait_ge(y_ps, g + 1)
                    if g:
                        dve.wait_ge(parts_ready, 4 * g)
                    S(v.tensor_copy(y[:, b:b + n, :], psY[g % 2][0:B, 0:n * D].rearrange("p (b d) -> p b d", d=D)))
                    S.wait()
                    S(v.tensor_tensor(scaled[:, 0:n, :], y[:, b:b + n, :],
                                      dinv[:, b:b + n].unsqueeze(2).broadcast_to([B, n, D]), ALU.mult))
                    S.wait()
                    split(nc, S, lambda r: parts[0][:, b:b + n, r, :], scaled[:, 0:n, :], scaled[:, 0:n, :]
                          ).then_inc(parts_ready, n)
                start = S.n

                def term(it, src):
                    S.base, S.n = start + NB * PER * it, 0
                    for b in range(NB):
                        k = b % 2
                        ps, r, d, e = psA[(NB * src + b) % 2], sumr[k][:], diff[k][:], rest[k][:]
                        p = lambda i: parts[1 - src][:, b, i, :]
                        dve.wait_ge(sums, NB * it + b + 1)
                        dve.wait_ge(parts_ready, NB * it + NB + b)
                        S(v.reduce_sum(r, ps[0:B, 0:3 * D].rearrange("p (r d) -> p d r", r=3), X))
                        v.tensor_tensor(d, ps[0:B, 256:256 + D], y[:, b, :], ALU.subtract).then_inc(bank_free, 1)
                        dve.wait_ge(bank_free, NB * it + b + 3)
                        S(v.scalar_tensor_tensor(y[:, b, :], r, dinv[:, b:b + 1], d, ALU.mult, ALU.add))
                        S.wait()
                        S(v.tensor_scalar(p(0), y[:, b, :], dinv[:, b:b + 1], None, ALU.mult))
                        S(v.tensor_scalar(r, y[:, b, :], dinv[:, b:b + 1], None, ALU.mult))
                        S.wait()
                        S(v.tensor_tensor(e, r, p(0), ALU.subtract))
                        S.wait()
                        S(v.tensor_copy(p(1), e))
                        S.wait()
                        v.tensor_tensor(p(2), e, p(1), ALU.subtract).then_inc(parts_ready, 1)
                    assert S.n == NB * PER

                with dve.Fori(0, KMAX, 2) as it:
                    it = it.with_bounds(min_val=0, max_val=KMAX - 2)
                    term(it, 0)
                    term((it + 1).with_bounds(min_val=1, max_val=KMAX - 1), 1)
                S.base, S.n = start + NB * PER * KMAX, 0
                dve.wait_ge(parts_ready, NB * (KMAX + 1))
                S(v.tensor_tensor(y[:], y[:], t.xb[:], ALU.add))
                normalize(nc, dve, S, y, bn, mv, std, rstd, t.xb[:], var, root).then_inc(root, 1)

        with nc.Block() as block:
            @block.sync
            def _(sp):
                sp.dma_start(out.rearrange("(b p) d -> p b d", p=B), t.xb[:]).then_inc(stored, 16)
                sp.wait_ge(stored, 16)


@contextmanager
def cleared_semaphores(nc, prefix, *names):
    sems = [nc.alloc_semaphore(name=f"{prefix}_{n}") for n in names]
    yield sems
    nc.clear_and_free_semaphores(sems)
    nc.all_engine_barrier()


def edge_sums(nc, name, g, table, pick, node, acc):
    C = D + 3
    with ExitStack() as s:
        sb = lambda n, sh, d: s.enter_context(nc.sbuf_tensor(f"{name}_{n}", sh, d))
        pick_i, node_f, rows = sb("pick_i", [B, 1], I32), sb("node_f", [B, 1], F32), sb("rows", [B, C], F32)
        ps = s.enter_context(nc.psum_tensor(f"{name}_ps", [P, 4, 512], F32))
        turn = sb("turn", [B, 1], F32)
        cleared, staged, turns, gathered, hot_ready, product, added = s.enter_context(cleared_semaphores(
            nc, name, "cleared", "staged", "turns", "gathered", "onehot_ready", "product", "added"))
        banks = [range(lo, min(lo + 7, NB)) for lo in range(0, NB, 7)]
        with nc.Block() as block:
            @block.vector
            def _(dve):
                nc.vector.memset(acc[:], 0.0).then_inc(cleared, 1)
                dve.wait_ge(cleared, 1)
                with dve.Fori(0, CH) as it:
                    dve.wait_ge(added, it)
                    dve.wait_ge(turns, it)
                    nc.vector.tensor_copy(pick_i[:], pick[:, bass.ds(it, 1)])
                    nc.vector.tensor_copy(node_f[:], node[:, bass.ds(it, 1)])
                    nc.vector.tensor_copy(rows[:, D:C], g.own[:, bass.ds(it, 1), :].rearrange("p o k -> p (o k)")
                                          ).then_inc(staged, 1)
                    dve.wait_ge(staged, it + 1)
                    nc.vector.tensor_scalar(g.hot[:], g.nodes[:], node_f[:], None, ALU.is_equal
                                            ).then_inc(hot_ready, 1)
                    dve.wait_ge(product, it + 1)
                    for k, blocks in enumerate(banks):
                        n, v = len(blocks), acc[:, blocks[0]:blocks[-1] + 1, :]
                        last = nc.vector.tensor_tensor(
                            v, v, ps[0:B, k, 0:n * C].rearrange("p (b c) -> p b c", c=C), ALU.add)
                    last.then_inc(added, 1)

            @block.gpsimd
            def _(pool):
                with pool.Fori(0, CH) as it:
                    pool.wait_ge(staged, it + 1)
                    nc.gpsimd.tensor_tensor(turn[:], g.ident[0:B, 0:1], g.ident[0:B, 0:1], ALU.add
                                            ).then_inc(turns, 1)
                    nc.gpsimd.indirect_dma_start(
                        out=rows[:, 0:D], out_offset=None, in_=table,
                        in_offset=bass.IndirectOffsetOnAxis(ap=pick_i[:, 0:1], axis=0)).then_inc(gathered, 16)

            @block.tensor
            def _(pe):
                with pe.Fori(0, CH) as it:
                    pe.wait_ge(gathered, 16 * it + 16)
                    pe.wait_ge(hot_ready, it + 1)
                    for k, blocks in enumerate(banks):
                        for i, b in enumerate(blocks):
                            last = nc.tensor.matmul(ps[0:B, k, i * C:(i + 1) * C], g.hot[:, b * B:(b + 1) * B],
                                                    rows[:], start=True, stop=True)
                    last.then_inc(product, 1)


def edge_network_sums(nc, g, p_table, q_table, wd, eb1, eb2, eW2, acc):
    with ExitStack() as s:
        sb = lambda n, sh, d: s.enter_context(nc.sbuf_tensor(f"EN_{n}", sh, d))
        src_i, dst_i = sb("src_i", [B, 1], I32), sb("dst_i", [B, 1], I32)
        src_f, w1 = sb("src_f", [B, 1], F32), sb("w1", [B, 1], F32)
        pre, q, h1, h1T, z2, h2 = (sb("pre", [B, H], F32), sb("q", [B, H], F32), sb("h1", [B, H], F32),
                                   sb("h1T", [H, B], F32), sb("z2", [B, H], F32), sb("h2", [B, H], F32))
        ps = s.enter_context(nc.psum_tensor("EN_ps", [P, 4, 512], F32))
        ps_t = s.enter_context(nc.psum_tensor("EN_ps_t", [P, 512], F32))
        ps_z = s.enter_context(nc.psum_tensor("EN_ps_z", [P, 512], F32))
        turn = sb("turn", [B, 1], F32)
        (cleared, staged, turns, gathered, summed, h1_ready, turned, h1t_ready, z_ps, z2_ready, h2_ready, hot_ready, product,
         added) = s.enter_context(cleared_semaphores(
             nc, "EN", "cleared", "staged", "turns", "gathered", "summed", "h1_ready", "h1_turned", "h1T_ready", "z_product",
             "z2_ready", "h2_ready", "onehot_ready", "product", "added"))
        banks = [range(lo, min(lo + 8, NB)) for lo in range(0, NB, 8)]
        with nc.Block() as block:
            @block.vector
            def _(dve):
                nc.vector.memset(acc[:], 0.0).then_inc(cleared, 1)
                dve.wait_ge(cleared, 1)
                with dve.Fori(0, CH) as it:
                    dve.wait_ge(added, 2 * it)
                    dve.wait_ge(turns, it)
                    nc.vector.tensor_copy(src_i[:], g.src_i[:, bass.ds(it, 1)])
                    nc.vector.tensor_copy(dst_i[:], g.dst_i[:, bass.ds(it, 1)])
                    nc.vector.tensor_copy(src_f[:], g.src_f[:, bass.ds(it, 1)])
                    nc.vector.tensor_copy(w1[:], g.w1[:, bass.ds(it, 1)]).then_inc(staged, 1)
                    dve.wait_ge(staged, it + 1)
                    nc.vector.tensor_scalar(g.hot[:], g.nodes[:], src_f[:], None, ALU.is_equal).then_inc(hot_ready, 1)
                    dve.wait_ge(gathered, 32 * it + 32)
                    nc.vector.tensor_tensor(pre[:], pre[:], q[:], ALU.add).then_inc(summed, 1)
                    dve.wait_ge(summed, 3 * it + 1)
                    nc.vector.scalar_tensor_tensor(pre[:], wd[:], w1[:], pre[:], ALU.mult, ALU.add
                                                   ).then_inc(summed, 1)
                    dve.wait_ge(summed, 3 * it + 2)
                    nc.vector.tensor_tensor(pre[:], pre[:], eb1[:], ALU.add).then_inc(summed, 1)
                    dve.wait_ge(z_ps, it + 1)
                    nc.vector.tensor_tensor(z2[:], ps_z[0:B, 0:H], eb2[:], ALU.add).then_inc(z2_ready, 1)
                    for half in range(2):
                        dve.wait_ge(product, 2 * it + half + 1)
                        for k, blocks in enumerate(banks):
                            n, v = len(blocks), acc[:, blocks[0]:blocks[-1] + 1, half * D:(half + 1) * D]
                            last = nc.vector.tensor_tensor(
                                v, v, ps[0:B, k, 0:n * D].rearrange("p (b c) -> p b c", c=D), ALU.add)
                        last.then_inc(added, 1)

            @block.gpsimd
            def _(pool):
                with pool.Fori(0, CH) as it:
                    pool.wait_ge(staged, it + 1)
                    nc.gpsimd.tensor_tensor(turn[:], g.ident[0:B, 0:1], g.ident[0:B, 0:1], ALU.add
                                            ).then_inc(turns, 1)
                    nc.gpsimd.indirect_dma_start(
                        out=pre[:], out_offset=None, in_=p_table,
                        in_offset=bass.IndirectOffsetOnAxis(ap=src_i[:, 0:1], axis=0)).then_inc(gathered, 16)
                    nc.gpsimd.indirect_dma_start(
                        out=q[:], out_offset=None, in_=q_table,
                        in_offset=bass.IndirectOffsetOnAxis(ap=dst_i[:, 0:1], axis=0)).then_inc(gathered, 16)

            @block.scalar
            def _(act):
                with act.Fori(0, CH) as it:
                    act.wait_ge(summed, 3 * it + 3)
                    nc.scalar.activation(h1[:], pre[:], ACT.Silu).then_inc(h1_ready, 1)
                    act.wait_ge(turned, it + 1)
                    nc.scalar.copy(h1T[:], ps_t[:, 0:B]).then_inc(h1t_ready, 1)
                    act.wait_ge(z2_ready, it + 1)
                    nc.scalar.activation(h2[:], z2[:], ACT.Silu).then_inc(h2_ready, 1)

            @block.tensor
            def _(pe):
                with pe.Fori(0, CH) as it:
                    pe.wait_ge(h1_ready, it + 1)
                    nc.tensor.transpose(ps_t[:, 0:B], h1[:], g.ident[0:B, 0:B]).then_inc(turned, 1)
                    pe.wait_ge(h1t_ready, it + 1)
                    nc.tensor.matmul(ps_z[0:B, 0:H], h1T[:], eW2[:], start=True, stop=True).then_inc(z_ps, 1)
                    pe.wait_ge(h2_ready, it + 1)
                    pe.wait_ge(hot_ready, it + 1)
                    for half in range(2):
                        if half:
                            pe.wait_ge(added, 2 * it + 1)
                        for k, blocks in enumerate(banks):
                            for i, b in enumerate(blocks):
                                last = nc.tensor.matmul(ps[0:B, k, i * D:(i + 1) * D], g.hot[:, b * B:(b + 1) * B],
                                                        h2[:, half * D:(half + 1) * D], start=True, stop=True)
                        last.then_inc(product, 1)


def node_product(nc, name, g, terms, out, bias):
    with ExitStack() as s:
        N = out.shape[2]
        staged_rows = [s.enter_context(nc.sbuf_tensor(f"{name}_rows{i}", [B, w.shape[0]], F32))
                       for i, (_, w) in enumerate(terms)]
        rowsT = [s.enter_context(nc.sbuf_tensor(f"{name}_rowsT{i}", [w.shape[0], B], F32))
                 for i, (_, w) in enumerate(terms)]
        ps_t = [s.enter_context(nc.psum_tensor(f"{name}_ps_t{i}", [P, 512], F32)) for i in range(len(terms))]
        ps = s.enter_context(nc.psum_tensor(f"{name}_ps", [P, 512], F32))
        staged, turned, rows_t, product, kept = s.enter_context(cleared_semaphores(
            nc, name, "staged", "turned", "rowsT_ready", "product", "kept"))
        with nc.Block() as block:
            @block.vector
            def _(dve):
                with dve.Fori(0, NB) as b:
                    dve.wait_ge(kept, b)
                    for (rows, w), st in zip(terms, staged_rows):
                        last = nc.vector.tensor_copy(
                            st[:], rows[:, bass.ds(b, 1), 0:w.shape[0]].rearrange("p o d -> p (o d)"))
                    last.then_inc(staged, 1)
                    dve.wait_ge(product, b + 1)
                    nc.vector.tensor_tensor(out[:, bass.ds(b, 1), :].rearrange("p o d -> p (o d)"), ps[0:B, 0:N],
                                            bias, ALU.add).then_inc(kept, 1)

            @block.tensor
            def _(pe):
                with pe.Fori(0, NB) as b:
                    pe.wait_ge(staged, b + 1)
                    for st, pt in zip(staged_rows, ps_t):
                        last = nc.tensor.matmul(pt[0:st.shape[1], 0:B], st[:], g.ident[0:B, 0:B], start=True,
                                                stop=True)
                    last.then_inc(turned, 1)
                    pe.wait_ge(rows_t, b + 1)
                    for i, (_, w) in enumerate(terms):
                        last = nc.tensor.matmul(ps[0:B, 0:N], rowsT[i][:], w, start=(i == 0),
                                                stop=(i == len(terms) - 1))
                    last.then_inc(product, 1)

            @block.scalar
            def _(act):
                with act.Fori(0, NB) as b:
                    act.wait_ge(turned, b + 1)
                    for rt, pt in zip(rowsT, ps_t):
                        last = nc.scalar.copy(rt[:], pt[0:rt.shape[0], 0:B])
                    last.then_inc(rows_t, 1)


def store_rows(nc, name, table, rows):
    with cleared_semaphores(nc, name, "stored") as (stored,), nc.Block() as block:
        @block.sync
        def _(sp):
            sp.dma_start(table.rearrange("(b p) d -> p b d", p=B), rows).then_inc(stored, 16)
            sp.wait_ge(stored, 16)


def add_and_normalize(nc, name, c, g, x, y):
    with ExitStack() as s:
        step, var, root = s.enter_context(cleared_semaphores(nc, name, "norm_step", "var_ready", "std_ready"))
        with nc.Block() as block:
            @block.vector
            def _(dve):
                S = Steps(dve, step)
                S(nc.vector.tensor_tensor(y[:], y[:], x[:], ALU.add))
                normalize(nc, dve, S, y, g.bn, g.mv, g.std, g.rstd, x[:], var, root).then_inc(root, 1)

            @block.scalar
            def _(act):
                roots(nc, act, c, g.mv, g.std, var, root)


def any_order(nc, a, c, x, y, out):
    with ExitStack() as s:
        sb = lambda n, sh, d: s.enter_context(nc.sbuf_tensor(f"any_{n}", sh, d))
        g = Bag()
        g.src_i, g.dst_i = sb("src_i", [B, CH], I32), sb("dst_i", [B, CH], I32)
        g.src_f, g.dst_f = sb("src_f", [B, CH], F32), sb("dst_f", [B, CH], F32)
        g.w1, g.own, w = sb("w1", [B, CH], F32), sb("own", [B, CH, 3], F32), sb("w", [B, 2 * CH], F32)
        edges = sb("edges", [B, 2 * CH], I32)
        g.nodes, g.hot = sb("nodes", [B, V], F32), sb("hot", [B, V], F32)
        g.ident = c.ident
        g.bn, g.mv, g.std, g.rstd = norm_buffers(sb)
        acc = sb("acc", [B, NB, D + 3], F32)
        agg, z, z_out = sb("agg", [B, NB, H], F32), sb("z", [B, NB, H], F32), sb("z_out", [B, NB, H], F32)
        hx, hmu = sb("hx", [B, NB, D], F32), sb("hmu", [B, NB, D], F32)
        nothing = sb("nothing", [B, H], F32)
        nv = sb("nv", [B, NB], F32)
        table = nc.dram_tensor("any_table", [V, D], F32).ap()
        p_table, q_table = nc.dram_tensor("any_p", [V, H], F32).ap(), nc.dram_tensor("any_q", [V, H], F32).ap()
        n0, n1, n2, n3 = "L0_gnn_", "L1_gnn_", "L2_gnn_", "L3_gnn_"
        tables = {}
        for k, ap, sh in (("W1", a[n0 + "W1"], [D, D]), ("W2", a[n0 + "W2"], [D, D]),
                          ("eWa", a[n1 + "eW1"][0:D], [D, H]), ("eWb", a[n1 + "eW1"][D:2 * D], [D, H]),
                          ("eW2", a[n1 + "eW2"], [H, H]), ("nWa", a[n1 + "nW1"][0:D], [D, H]),
                          ("nWb", a[n1 + "nW1"][D:D + H], [H, H]), ("nW2", a[n1 + "nW2"], [H, D]),
                          ("W3T", a["W3T"], [D, D]), ("W4a", a["W4T"][0:D], [D, D]),
                          ("W4b", a["W4T"][D:2 * D], [D, D]), ("W4c", a["W4T"][2 * D:3 * D], [D, D]),
                          ("Wk", a[n3 + "W"].rearrange("k i o -> i k o"), [D, KMAX + 1, D])):
            tables[k] = (sb(k, sh, F32), ap)
        for k, ap, width in (("b1", a[n0 + "b1"], D), ("b2", a[n0 + "b2"], D), ("eb1", a[n1 + "eb1"], H),
                             ("wd", a[n1 + "eW1"][2 * D], H), ("eb2", a[n1 + "eb2"], H), ("nb1", a[n1 + "nb1"], H),
                             ("nb2", a[n1 + "nb2"], D), ("w1r", a[n2 + "W1"].rearrange("d o -> (d o)"), D),
                             ("w2r", a[n2 + "W2"].rearrange("d o -> (d o)"), D), ("bias", a[n3 + "bias"], D)):
            tables[k] = (sb(k, [B, width], F32), ap.partition_broadcast(B))
        tb = lambda k: tables[k][0]
        wide = lambda ap: ap.unsqueeze(1).broadcast_to([B, NB, ap.shape[1]])
        loaded, = s.enter_context(cleared_semaphores(nc, "any", "loaded"))
        LOADS = len(tables) + 4
        with nc.Block() as block:
            @block.sync
            def _(sp):
                sp.dma_start(edges[:], a["edges"].rearrange("(p j) -> p j", p=B)).then_inc(loaded, 16)
                sp.dma_start(w[:], a["weights"].rearrange("(p j) -> p j", p=B)).then_inc(loaded, 16)
                sp.dma_start(x[:], a["x"].rearrange("(b p) d -> p b d", p=B)).then_inc(loaded, 16)
                with nc.allow_non_contiguous_dma("one load of a column"):
                    sp.dma_start(nv[:], a["node_vec1"].rearrange("(b p) -> p b", p=B)).then_inc(loaded, 16)
                for k in tables:
                    sp.dma_start(tables[k][0][:], tables[k][1]).then_inc(loaded, 16)

            @block.gpsimd
            def _(pool):
                nc.gpsimd.iota(g.nodes[:], [[1, V]], base=0, channel_multiplier=0,
                               allow_small_or_imprecise_dtypes=True)
                nc.gpsimd.memset(nothing[:], 0.0)
                nc.gpsimd.memset(g.own[:, :, 2], 1.0)

            @block.vector
            def _(dve):
                v = nc.vector
                dve.wait_ge(loaded, 16 * LOADS)
                e2, w2 = (t[:].rearrange("p (j k) -> p j k", k=2) for t in (edges, w))
                v.tensor_copy(g.src_i[:], e2[:, :, 0])
                v.tensor_copy(g.dst_i[:], e2[:, :, 1])
                v.tensor_copy(g.src_f[:], e2[:, :, 0])
                v.tensor_copy(g.dst_f[:], e2[:, :, 1])
                v.tensor_copy(g.w1[:], w2[:, :, 0])
                v.tensor_scalar(g.own[:, :, 0], w2[:, :, 1], 0.0, None, ALU.max)
                v.tensor_scalar(g.own[:, :, 1], w2[:, :, 1], -1.0, 0.0, ALU.mult, ALU.max)
                inv = 1.0
                for k in range(1, KMAX + 1):
                    inv /= k
                    v.tensor_scalar(tb("Wk")[:, k, :], tb("Wk")[:, k, :], inv, None, ALU.mult)

        store_rows(nc, "any_x", table, x[:])
        edge_sums(nc, "any_L0a", g, table, g.src_i, g.dst_f, acc)
        node_product(nc, "any_L0h", g, [(acc, tb("W1")[:])], y, tb("b1")[:])
        with nc.Block() as block:
            @block.vector
            def _(dve):
                nc.vector.tensor_scalar(y[:], y[:], 0.0, None, ALU.max)
        store_rows(nc, "any_h", table, y[:])
        edge_sums(nc, "any_L0b", g, table, g.src_i, g.dst_f, acc)
        node_product(nc, "any_L0y", g, [(acc, tb("W2")[:])], y, tb("b2")[:])
        add_and_normalize(nc, "any_L0n", c, g, x, y)

        node_product(nc, "any_L1p", g, [(x, tb("eWa")[:])], z, nothing[:])
        store_rows(nc, "any_p", p_table, z[:])
        node_product(nc, "any_L1q", g, [(x, tb("eWb")[:])], z, nothing[:])
        store_rows(nc, "any_q", q_table, z[:])
        edge_network_sums(nc, g, p_table, q_table, tb("wd"), tb("eb1"), tb("eb2"), tb("eW2"), agg)
        node_product(nc, "any_L1z", g, [(x, tb("nWa")[:]), (agg, tb("nWb")[:])], z, tb("nb1")[:])
        with nc.Block() as block:
            @block.scalar
            def _(act):
                nc.scalar.activation(z_out[:], z[:], ACT.Silu)
        node_product(nc, "any_L1y", g, [(z_out, tb("nW2")[:])], y, tb("nb2")[:])
        add_and_normalize(nc, "any_L1n", c, g, x, y)

        he, side = z[:, :, 0:D], z[:, :, D:H]
        node_product(nc, "any_L2m", g, [(x, tb("W3T")[:])], hmu, nothing[:, 0:D])
        w2pm = sb("w2pm", [B, 2, D], F32)
        with cleared_semaphores(nc, "any_L2_step", "step") as (step,), nc.Block() as block:
            @block.vector
            def _(dve):
                S, v = Steps(dve, step), nc.vector
                S(v.tensor_scalar(hmu[:], hmu[:], 0.0, None, ALU.max))
                S(v.tensor_tensor(hx[:], nv[:].unsqueeze(2).broadcast_to([B, NB, D]), wide(tb("w1r")[:]), ALU.mult))
                S(v.tensor_scalar(w2pm[:, 0, :], tb("w2r")[:], 0.0, None, ALU.max))
                S(v.tensor_scalar(w2pm[:, 1, :], tb("w2r")[:], -1.0, 0.0, ALU.mult, ALU.max))
                S.wait()
                v.tensor_scalar(hx[:], hx[:], 0.0, None, ALU.max)
        node_product(nc, "any_L2z", g, [(hx, tb("W4a")[:]), (hmu, tb("W4c")[:])], y, nothing[:, 0:D])
        store_rows(nc, "any_z", table, y[:])
        edge_sums(nc, "any_L2s", g, table, g.dst_i, g.src_f, acc)
        with cleared_semaphores(nc, "any_he_step", "step") as (step,), nc.Block() as block:
            @block.vector
            def _(dve):
                S, v = Steps(dve, step), nc.vector
                for i, to in enumerate((he, side)):
                    S(v.tensor_tensor(to, acc[:, :, D + i:D + i + 1].broadcast_to([B, NB, D]), wide(w2pm[:, i, :]),
                                      ALU.mult))
                S.wait()
                v.tensor_tensor(he, he, side, ALU.add)
        node_product(nc, "any_L2e", g, [(z, tb("W4b")[:])], y, nothing[:, 0:D])
        some, dinv = sb("some", [B, NB], F32), sb("dinv", [B, NB], F32)
        root_deg = sb("root_deg", [B, NB], F32)
        with cleared_semaphores(nc, "any_msg", "step", "root") as (step, droot), nc.Block() as block:
            @block.vector
            def _(dve):
                S, v = Steps(dve, step), nc.vector
                deg = acc[:, :, D + 2]
                S(v.tensor_scalar(dinv[:], deg, 1.0, None, ALU.max))
                S(v.tensor_scalar(some[:], deg, 0.0, None, ALU.is_gt))
                S(v.tensor_tensor(y[:], y[:], acc[:, :, 0:D], ALU.add))
                S.wait()
                S(v.scalar_tensor_tensor(y[:], y[:], 0.0, hx[:], ALU.max, ALU.add))
                S.wait()
                S(v.tensor_tensor(y[:], y[:], hmu[:], ALU.add))
                S.wait()
                S(v.tensor_scalar(y[:], y[:], 0.0, None, ALU.max))
                dve.wait_ge(droot, 1)
                S(v.reciprocal(dinv[:], root_deg[:]))
                S.wait()
                v.tensor_tensor(dinv[:], dinv[:], some[:], ALU.mult)

            @block.scalar
            def _(act):
                act.wait_ge(step, 1)
                nc.scalar.activation(root_deg[:], dinv[:], ACT.Sqrt).then_inc(droot, 1)
        add_and_normalize(nc, "any_L2n", c, g, x, y)

        each = dinv[:].unsqueeze(2).broadcast_to([B, NB, D])
        node_product(nc, "any_L3y", g, [(x, tb("Wk")[:, KMAX, :])], y, nothing[:, 0:D])
        for k in range(KMAX - 1, -1, -1):
            with nc.Block() as block:
                @block.vector
                def _(dve):
                    nc.vector.tensor_tensor(hx[:], y[:], each, ALU.mult)
            store_rows(nc, f"any_y{k}", table, hx[:])
            edge_sums(nc, f"any_L3s{k}", g, table, g.dst_i, g.src_f, acc)
            node_product(nc, f"any_L3x{k}", g, [(x, tb("Wk")[:, k, :])], hmu, nothing[:, 0:D])
            with cleared_semaphores(nc, f"any_term{k}", "step") as (step,), nc.Block() as block:
                @block.vector
                def _(dve):
                    S, v = Steps(dve, step), nc.vector
                    S(v.tensor_tensor(hx[:], acc[:, :, 0:D], each, ALU.mult))
                    S(v.tensor_tensor(hmu[:], hmu[:], y[:], ALU.subtract))
                    S.wait()
                    v.tensor_tensor(y[:], hx[:], hmu[:], ALU.add)
        with nc.Block() as block:
            @block.vector
            def _(dve):
                nc.vector.tensor_tensor(y[:], y[:], wide(tb("bias")[:]), ALU.add)
        add_and_normalize(nc, "any_L3n", c, g, x, y)
        store_rows(nc, "any_out", out, x[:])


class Bag:
    pass


def program(nc, a, out):
    with ExitStack() as ctx:
        sb = lambda n, sh, d: ctx.enter_context(nc.sbuf_tensor(n, sh, d))
        c, t = Bag(), Bag()
        c.ones, c.ones_bf = sb("ones", [P, P], F32), sb("ones_bf", [P, P], BF16)
        c.iota1, c.iota1_bf = sb("iota1", [P, P], F32), sb("iota1_bf", [P, P], BF16)
        c.row1, c.sign = sb("row1", [P, 1], F32), sb("sign", [P, 1], F32)
        c.ident, c.ident_bf = sb("ident", [P, P], F32), sb("ident_bf", [P, P], BF16)
        c.placed_i = sb("placed_i", [1, 1], I32)
        c.eps = sb("eps", [P, 1], F32)
        t.src1 = sb("src1", [P, NT], F32)
        t.wsum = sb("wsum", [B, NB, WP], F32)
        rows_d = nc.dram_tensor("rows_d", [5 * NT * P], BF16).ap()
        m2_d = nc.dram_tensor("m2_d", [NB, B, MW], BF16).ap()
        t.xa, t.xb = sb("xa", [B, NB, D], F32), sb("xb", [B, NB, D], F32)
        with ExitStack() as right:
            t.dst1 = right.enter_context(nc.sbuf_tensor("dst1", [P, NT], F32, side="right"))
            t.wparts = right.enter_context(nc.sbuf_tensor("wparts", [P, NT, WP], BF16, side="right"))
            with nc.sbuf_tensor("slots", [P, REC, NC, NB], F32) as slots:
                t.slots = slots
                place_edges(nc, a, c, t)
                edge_tables(nc, c, t, slots, rows_d)
            placed = nc.values_load(c.placed_i[0:1, 0:1], min_val=0, max_val=E)
            with nc.If(placed == E):
                with ExitStack() as fast:
                    t.mat = fast.enter_context(nc.sbuf_tensor("mat", [P, NB, MW], BF16))
                    count_matrices(nc, c, t, m2_d)
                    right.close()
                    gcn_layers(nc, a, c, t)
                    edge_network(nc, a, c, t, rows_d, m2_d)
                    message_layer(nc, a, c, t, m2_d)
                    polynomial_layer(nc, a, c, t, out)
            with nc.Else():
                any_order(nc, a, c, t.xb, t.xa, out)


_WEIGHTS = ["L0_gnn_W1", "L0_gnn_b1", "L0_gnn_W2", "L0_gnn_b2", "L1_gnn_eW1", "L1_gnn_eb1", "L1_gnn_eW2", "L1_gnn_eb2",
            "L1_gnn_nW1", "L1_gnn_nb1", "L1_gnn_nW2", "L1_gnn_nb2", "L2_gnn_W1", "L2_gnn_W2", "L3_gnn_W",
            "L3_gnn_bias"]


def kernel(**inputs):
    import concourse.bacc as _bacc
    from concourse.bass_utils import run_bass_kernel_spmd as _run

    put = {k: np.ascontiguousarray(inputs[k]) for k in ["x"] + _WEIGHTS}
    src, dst = np.asarray(inputs["src"]), np.asarray(inputs["dst"])
    put["dst"] = np.ascontiguousarray(dst)
    put["edges"] = np.stack([src, dst], -1).reshape(-1)
    put["weights"] = np.stack([np.asarray(inputs["edge_weight1"])[:, 0], np.asarray(inputs["edge_weight"])],
                              -1).reshape(-1)
    put["node_vec1"] = np.asarray(inputs["node_vec1"]).reshape(-1)
    put["xT"] = np.ascontiguousarray(np.asarray(inputs["x"]).T)
    put["W3T"] = np.ascontiguousarray(np.asarray(inputs["L2_gnn_W3"]).T)
    put["W4T"] = np.ascontiguousarray(np.asarray(inputs["L2_gnn_W4"]).T)

    nc = _bacc.Bacc("TRN2", target_bir_lowering=False, num_devices=1)
    a = {n: nc.dram_tensor(f"in_{n}", v.shape, mybir.dt.from_np(v.dtype), kind="ExternalInput").ap()
         for n, v in put.items()}
    out = nc.dram_tensor("out", [V, D], F32, kind="ExternalOutput").ap()
    program(nc, a, out)
    r = _run(nc, [{f"in_{n}": v for n, v in put.items()}], core_ids=[0])
    return r.results[0]["out"]
```

```python
import numpy as np
import concourse.bass as bass
from concourse import mybir
from contextlib import ExitStack, contextmanager

F32, BF16, I32 = mybir.dt.float32, mybir.dt.bfloat16, mybir.dt.int32
ALU = mybir.AluOpType
ACT = mybir.ActivationFunctionType
X = mybir.AxisListType.X

P = 128
V, E, D, H = 3125, 53125, 64, 128
NB = 25
B = V // NB
CH = E // B
W = 18
WIN = P * W
CAP = P
NC = NB + 1
NT = NB * NC
MW = 3128
KMAX = 10
REC = 8
WP = 7
GROUPS = [list(range(g, min(g + 4, NC))) for g in range(0, NC, 4)]
EPS = 1e-5


class Steps:

    def __init__(self, eng, sem):
        self.eng, self.sem, self.base, self.n = eng, sem, 0, 0

    def __call__(self, ins):
        ins.then_inc(self.sem, 1)
        self.n += 1
        return ins

    def wait(self):
        self.eng.wait_ge(self.sem, self.base + self.n)


def in_pairs(eng, count, body, last=0):
    body(0, 0)
    end = count - last
    with eng.Fori(1, end, 2) as i:
        i = i.with_bounds(min_val=1, max_val=end - 2)
        body(i, 1)
        body((i + 1).with_bounds(min_val=2, max_val=end - 1), 0)
    for i in range(end, count):
        body(i, i % 2)


def place_edges(nc, a, c, t):
    with ExitStack() as s:
        sb = lambda n, sh, d: s.enter_context(nc.sbuf_tensor(n, sh, d))
        sem = lambda n: s.enter_context(nc.semaphore(n))
        dst_i = sb("dst_i", [B, CH], I32)
        dst_f = sb("dst_f", [B, CH], F32)
        below = sb("below", [B, NB, CH], BF16)
        cnt = sb("cnt", [B, NB], F32)
        start_f = sb("start_f", [1, NB], F32)
        start_i = sb("start_i", [1, NB], I32)
        ew = sb("ew", [P, NB, W, 2], I32)
        ww = sb("ww", [P, NB, W, 2], F32)
        bcol = sb("bcol", [P, NB, W], F32)
        bsb = sb("bsb", [P, NB, W], F32)
        keep = sb("keep", [P, NB * W], BF16)
        tri = sb("tri", [P, P], BF16)
        ps_cnt = s.enter_context(nc.psum_tensor("ps_cnt", [P, 512], F32))
        ps_cross = s.enter_context(nc.psum_tensor("ps_cross", [P, 1024], F32))
        ps_slot = [s.enter_context(nc.psum_tensor(f"ps_slot{i}", [P, 512], F32)) for i in range(2)]

        dst_in, counted, start_sum, start_ready = map(sem, ("dst_in", "counted", "start_sum", "start_ready"))
        edges_in, weights_in, consts = map(sem, ("edges_in", "weights_in", "consts"))
        HALF = (NB + 1) // 2

        def load_windows(eng, to, pairs, lo, hi, done):
            with eng.Fori(lo, hi) as b:
                b = b.with_bounds(min_val=lo, max_val=hi - 1)
                first = eng.value_load(start_i[0:1, bass.ds(b, 1)], min_val=0, max_val=E - WIN)
                eng.dma_start(to[:, bass.ds(b, 1), :, :].rearrange("p o j k -> p (o j k)"),
                              pairs[bass.ds(first * 2, WIN * 2)].rearrange("(p j) -> p j", p=P)).then_inc(done, 16)

        with nc.Block() as block:
            @block.sync
            def _(sp):
                sp.dma_start(dst_i[:], a["dst"].rearrange("(p j) -> p j", p=B)).then_inc(dst_in, 16)
                sp.wait_ge(start_ready, 1)
                load_windows(sp, ew, a["edges"], 0, HALF, edges_in)
                sp.wait_ge(edges_in, 16 * NB)

            @block.scalar
            def _(act):
                act.wait_ge(start_ready, 1)
                load_windows(act, ew, a["edges"], HALF, NB, edges_in)

            @block.gpsimd
            def _(pool):
                nc.gpsimd.memset(c.ones[:], 1.0)
                nc.gpsimd.memset(c.ones_bf[:], 1.0)
                nc.gpsimd.memset(c.eps[:], EPS)
                nc.gpsimd.iota(c.sign[:], [[0, 1]], base=1 + 2 * D, channel_multiplier=-2,
                               allow_small_or_imprecise_dtypes=True)
                nc.gpsimd.iota(c.iota1[:], [[1, P]], base=1, channel_multiplier=0,
                               allow_small_or_imprecise_dtypes=True)
                nc.gpsimd.iota(c.iota1_bf[:], [[1, P]], base=1, channel_multiplier=0,
                               allow_small_or_imprecise_dtypes=True)
                nc.gpsimd.iota(c.row1[:], [[0, 1]], base=1, channel_multiplier=1,
                               allow_small_or_imprecise_dtypes=True)
                nc.gpsimd.iota(bcol[:], [[1, NB], [0, W]], base=0, channel_multiplier=0,
                               allow_small_or_imprecise_dtypes=True)
                nc.gpsimd.iota(bsb[:], [[1, NB], [0, W]], base=1, channel_multiplier=0,
                               allow_small_or_imprecise_dtypes=True)
                nc.gpsimd.memset(keep[:], 1.0).then_inc(consts, 1)
                pool.wait_ge(consts, 1)
                nc.gpsimd.memset(keep[:].rearrange("p (c j) -> p c j", j=W)[:, :, 0:1], 0.0)
                nc.gpsimd.affine_select(out=c.ident[:], in_=c.ones[:], compare_op=ALU.is_equal, fill=0.0, base=0,
                                        pattern=[[-1, P]], channel_multiplier=1)
                nc.gpsimd.affine_select(out=c.ident_bf[:], in_=c.ones_bf[:], compare_op=ALU.is_equal, fill=0.0,
                                        base=0, pattern=[[-1, P]], channel_multiplier=1)
                nc.gpsimd.affine_select(out=tri[:], in_=c.ones_bf[:], compare_op=ALU.is_gt, fill=0.0, base=0,
                                        pattern=[[1, P]], channel_multiplier=-1).then_inc(consts, 1)

            @block.vector
            def _(dve):
                nc.vector.memset(cnt[:, 0:1], 0.0)
                dve.wait_ge(dst_in, 16)
                nc.vector.tensor_copy(dst_f[:], dst_i[:]).then_inc(counted, 1)
                dve.wait_ge(counted, 1)
                for b in range(1, NB):
                    last = nc.vector.tensor_scalar(below[:, b, :], dst_f[:], float(B * b), 0.0, ALU.is_lt, ALU.add,
                                                   accum_out=cnt[:, b:b + 1])
                last.then_inc(counted, 1)
                dve.wait_ge(start_sum, 1)
                nc.vector.tensor_scalar(start_f[:], ps_cnt[0:1, 0:NB], float(E - WIN), None, ALU.min
                                        ).then_inc(counted, 1)
                dve.wait_ge(counted, 3)
                nc.vector.tensor_copy(start_i[:], start_f[:]).then_inc(start_ready, 1)

            @block.tensor
            def _(pe):
                pe.wait_ge(counted, 2)
                pe.wait_ge(consts, 2)
                nc.tensor.matmul(ps_cnt[0:1, 0:NB], c.ones[0:B, 0:1], cnt[:], start=True, stop=True
                                 ).then_inc(start_sum, 1)

        srcf = sb("srcf", [P, NB, W], F32)
        dstf = sb("dstf", [P, NB, W], F32)
        sblk_i = sb("sblk_i", [P, NB, W], I32)
        dblk_i = sb("dblk_i", [P, NB, W], I32)
        sblk = sb("sblk", [P, NB, W], F32)
        dblk = sb("dblk", [P, NB, W], F32)
        key = sb("key", [P, NB, W], F32)
        diag = sb("diag", [P, NB, W], F32)
        rank = sb("rank", [P, NB, W], F32)
        slot = sb("slot", [P, NB, W], F32)
        col = sb("col", [P, NB, W], F32)
        rec = sb("rec", [P, NB, W, REC], BF16)
        cross = sb("cross", [P, NB * NB], F32)
        w_rest = [sb(f"w_rest{i}", [P, NB, W], F32) for i in range(2)]
        tmp = sb("tmp", [P, NB, W], F32)
        oh = sb("oh", [P, NB, NB, W], BF16)
        run = sb("run", [P, NB * NB, W], BF16)
        hit = [sb(f"hit{i}", [P, NB * W], F32) for i in range(2)]
        placed = sb("placed", [P, 1], F32)
        d1, ran, crossed, cross_kept, hit_ready, hit_used, cast, cut = map(sem, (
            "place_step", "ran", "crossed", "cross_kept", "hit_ready", "hit_used", "weights_cast", "weights_cut"))
        with nc.Block() as block:
            @block.vector
            def _(dve):
                D1 = Steps(dve, d1)
                D1(nc.vector.tensor_copy(srcf[:], ew[:, :, :, 0]))
                D1(nc.vector.tensor_copy(dstf[:], ew[:, :, :, 1]))
                D1.wait()
                D1(nc.vector.tensor_scalar(sblk_i[:], srcf[:], 1.0 / B, 0.5 / B - 0.5, ALU.mult, ALU.add))
                D1(nc.vector.tensor_scalar(dblk_i[:], dstf[:], 1.0 / B, 0.5 / B - 0.5, ALU.mult, ALU.add))
                D1.wait()
                D1(nc.vector.tensor_copy(sblk[:], sblk_i[:]))
                D1(nc.vector.tensor_copy(dblk[:], dblk_i[:]))
                D1.wait()
                D1(nc.vector.tensor_tensor(tmp[:], dblk[:], bcol[:], ALU.is_equal))
                D1(nc.vector.tensor_tensor(diag[:], sblk[:], dblk[:], ALU.is_equal))
                D1(nc.vector.scalar_tensor_tensor(srcf[:], sblk[:], -float(B), srcf[:], ALU.mult, ALU.add))
                D1(nc.vector.scalar_tensor_tensor(dstf[:], dblk[:], -float(B), dstf[:], ALU.mult, ALU.add))
                D1.wait()
                D1(nc.vector.scalar_tensor_tensor(key[:], sblk[:], 1.0, tmp[:], ALU.add, ALU.mult))
                D1.wait()
                D1(nc.vector.tensor_scalar(rec[:, :, :, 0], srcf[:], 1.0, None, ALU.add))
                D1(nc.vector.tensor_scalar(rec[:, :, :, 1], dstf[:], 1.0, None, ALU.add))
                for b in range(NB):
                    D1(nc.vector.tensor_tensor(oh[:, b], key[:, b:b + 1, :].broadcast_to([P, NB, W]), bsb[:],
                                               ALU.is_equal))
                D1.wait()
                for b in range(NB):
                    last = nc.vector.tensor_tensor_scan(
                        run[:, b * NB:(b + 1) * NB, :].rearrange("p c j -> p (c j)"), keep[:],
                        oh[:, b].rearrange("p c j -> p (c j)"), 0.0, ALU.mult, ALU.add)
                last.then_inc(ran, 1)
                for b in range(NB):
                    h = hit[b % 2]
                    dve.wait_ge(hit_ready, b + 1)
                    D1(nc.vector.tensor_tensor(h[:], h[:], oh[:, b].rearrange("p c j -> p (c j)"), ALU.mult))
                    D1.wait()
                    nc.vector.reduce_sum(rank[:, b, :], h[:].rearrange("p (c j) -> p j c", j=W), X
                                         ).then_inc(hit_used, 1)
                dve.wait_ge(hit_used, NB)
                D1(nc.vector.scalar_tensor_tensor(tmp[:], rank[:], float(CAP), diag[:], ALU.is_gt, ALU.mult))
                D1(nc.vector.tensor_scalar(col[:], sblk[:], -1.0, float(NB), ALU.mult, ALU.add))
                D1.wait()
                D1(nc.vector.scalar_tensor_tensor(slot[:], tmp[:], -float(CAP), rank[:], ALU.mult, ALU.add))
                D1(nc.vector.tensor_tensor(col[:], col[:], tmp[:], ALU.mult))
                D1.wait()
                D1(nc.vector.scalar_tensor_tensor(col[:], col[:], 1.0, sblk[:], ALU.add, ALU.add))
                D1(nc.vector.tensor_scalar(tmp[:], slot[:], 1.0, None, ALU.is_ge))
                D1.wait()
                D1(nc.vector.scalar_tensor_tensor(diag[:], slot[:], float(CAP), tmp[:], ALU.is_le, ALU.mult))
                D1.wait()
                nc.vector.reduce_sum(placed[:], diag[:].rearrange("p b j -> p (b j)"), X).then_inc(ran, 1)

            @block.tensor
            def _(pe):
                pe.wait_ge(ran, 1)
                nc.tensor.matmul(ps_cross[:, 0:500], tri[:], run[:, 0:500, W - 1], start=True, stop=True)
                nc.tensor.matmul(ps_cross[:, 512:637], tri[:], run[:, 500:625, W - 1], start=True, stop=True
                                 ).then_inc(crossed, 1)
                pe.wait_ge(ran, 2)
                nc.tensor.matmul(ps_cnt[0:1, 0:1], placed[:], c.ones[:, 0:1], start=True, stop=True
                                 ).then_inc(crossed, 1)

            @block.gpsimd
            def _(pool):
                pool.wait_ge(cast, 2)
                for i in range(2):
                    nc.gpsimd.tensor_tensor(w_rest[i][:], ww[:, :, :, i], rec[:, :, :, 2 + 3 * i], ALU.subtract
                                            ).then_inc(cut, 1)
                pool.wait_ge(cast, 4)
                for i in range(2):
                    nc.gpsimd.tensor_tensor(rec[:, :, :, 4 + 3 * i], w_rest[i][:], rec[:, :, :, 3 + 3 * i],
                                            ALU.subtract)
                pool.wait_ge(cross_kept, 1)
                for b in range(NB):
                    if b >= 2:
                        pool.wait_ge(hit_used, b - 1)
                    nc.gpsimd.tensor_tensor(
                        hit[b % 2][:].rearrange("p (c j) -> p c j", j=W), run[:, b * NB:(b + 1) * NB, :],
                        cross[:, b * NB:(b + 1) * NB].unsqueeze(2).broadcast_to([P, NB, W]), ALU.add).then_inc(hit_ready, 1)

            @block.sync
            def _(sp):
                load_windows(sp, ww, a["weights"], 0, HALF, weights_in)
                sp.wait_ge(weights_in, 16 * NB)

            @block.scalar
            def _(act):
                load_windows(act, ww, a["weights"], HALF, NB, weights_in)
                act.wait_ge(weights_in, 16 * NB)
                for i in range(2):
                    nc.scalar.copy(rec[:, :, :, 2 + 3 * i], ww[:, :, :, i]).then_inc(cast, 1)
                act.wait_ge(cut, 2)
                for i in range(2):
                    nc.scalar.copy(rec[:, :, :, 3 + 3 * i], w_rest[i][:]).then_inc(cast, 1)
                act.wait_ge(crossed, 1)
                nc.scalar.copy(cross[:, 0:500], ps_cross[:, 0:500])
                nc.scalar.copy(cross[:, 500:625], ps_cross[:, 512:637]).then_inc(cross_kept, 1)
                act.wait_ge(crossed, 2)
                nc.scalar.copy(c.placed_i[:], ps_cnt[0:1, 0:1])

        HOT = W // 2
        DR = 4
        ohr = sb("ohr", [P, 2, W, P], BF16)
        away = sb("away", [P, W - HOT, P], BF16)
        ohc = sb("ohc", [P, 2, W, NC], BF16)
        rows = sb("rows", [P, 2, W, NC * REC], BF16)
        iotac = sb("iotac", [P, W, NC], F32)
        stage = sb("stage", [P, 2, W], F32)
        srec = sb("srec", [P, 2, W, REC], BF16)
        (iotac_set, stage_set, ohc_ready, dve_ready, pool_ready, away_ready, act_ready, win_used, slot_used) = map(sem, (
            "iotac_set", "stage_set", "ohc_ready", "dve_part_ready", "pool_part_ready", "away_ready", "act_part_ready",
            "win_used", "slot_used"))
        with nc.Block() as block:
            @block.gpsimd
            def _(pool):
                nc.gpsimd.iota(iotac[:], [[0, W], [1, NC]], base=1, channel_multiplier=0,
                               allow_small_or_imprecise_dtypes=True).then_inc(iotac_set, 1)

                def body(b, k):
                    pool.wait_ge(ohc_ready, b + 1)
                    nc.gpsimd.tensor_tensor(
                        rows[:, k].rearrange("p j (c r) -> p j c r", r=REC)[:, :, :, DR:REC],
                        ohc[:, k].unsqueeze(3).broadcast_to([P, W, NC, REC - DR]),
                        srec[:, k, :, DR:REC].unsqueeze(2).broadcast_to([P, W, NC, REC - DR]), ALU.mult
                        ).then_inc(pool_ready, 1)
                in_pairs(pool, NB, body)

            @block.vector
            def _(dve):
                dve.wait_ge(iotac_set, 1)

                def body(b, k):
                    dve.wait_ge(win_used, b + 1)
                    nc.vector.tensor_copy(stage[:, k, :], slot[:, bass.ds(b, 1), :].rearrange("p o j -> p (o j)"))
                    nc.vector.tensor_copy(srec[:, k], rec[:, bass.ds(b, 1), :, :].rearrange("p o j r -> p (o j) r")
                                          ).then_inc(stage_set, 1)
                    nc.vector.tensor_tensor(
                        ohc[:, k], col[:, bass.ds(b, 1), :].rearrange("p o j -> p j o").broadcast_to([P, W, NC]),
                        iotac[:], ALU.is_equal).then_inc(ohc_ready, 1)
                    dve.wait_ge(stage_set, b + 1)
                    nc.vector.tensor_tensor(
                        ohr[:, k, 0:HOT, :], c.iota1_bf[:].unsqueeze(1).broadcast_to([P, HOT, P]),
                        stage[:, k, 0:HOT].unsqueeze(2).broadcast_to([P, HOT, P]), ALU.is_equal)
                    dve.wait_ge(ohc_ready, b + 1)
                    nc.vector.tensor_tensor(
                        rows[:, k].rearrange("p j (c r) -> p j c r", r=REC)[:, :, :, 0:DR],
                        ohc[:, k].unsqueeze(3).broadcast_to([P, W, NC, DR]),
                        srec[:, k, :, 0:DR].unsqueeze(2).broadcast_to([P, W, NC, DR]), ALU.mult
                        ).then_inc(dve_ready, 1)
                in_pairs(dve, NB, body)

            @block.tensor
            def _(pe):
                pe.sem_inc(win_used, 2)

                def body(b, k):
                    pe.wait_ge(dve_ready, b + 1)
                    pe.wait_ge(pool_ready, b + 1)
                    pe.wait_ge(act_ready, b + 1)
                    pe.wait_ge(slot_used, b + 1)
                    for j in range(W):
                        last = nc.tensor.matmul(ps_slot[k][:, 0:NC * REC], ohr[:, k, j, :], rows[:, k, j, :],
                                                start=(j == 0), stop=(j == W - 1))
                    last.then_inc(win_used, 1)
                in_pairs(pe, NB, body)

            @block.scalar
            def _(act):
                act.sem_inc(slot_used, 2)

                def keep_slots(b, k):
                    act.wait_ge(win_used, b + 3)
                    nc.scalar.copy(t.slots[:, :, :, bass.ds(b, 1)].rearrange("p r c o -> p r (c o)"),
                                   ps_slot[k][:, 0:NC * REC].rearrange("p (c r) -> p r c", r=REC)
                                   ).then_inc(slot_used, 1)

                def body(b, k):
                    act.wait_ge(stage_set, b + 1)
                    act.wait_ge(act_ready, b)
                    for j in range(HOT, W):
                        last = nc.scalar.activation(away[:, j - HOT, :], c.iota1_bf[:], ACT.Abs,
                                                    bias=stage[:, k, j:j + 1], scale=-1.0)
                    last.then_inc(away_ready, 1)
                    act.wait_ge(away_ready, b + 1)
                    nc.scalar.activation(ohr[:, k, HOT:W, :], away[:], ACT.Relu, bias=1.0, scale=-1.0
                                         ).then_inc(act_ready, 1)
                    if not (isinstance(b, int) and b == 0):
                        keep_slots(b - 1, 1 - k)
                in_pairs(act, NB, body)
                keep_slots(NB - 1, 0)


def edge_tables(nc, c, t, slots, rows_d):
    with ExitStack() as s:
        sb = lambda n, sh, d: s.enter_context(nc.sbuf_tensor(n, sh, d))
        sem = lambda n: s.enter_context(nc.semaphore(n))
        minus = sb("minus", [P, NT], F32)
        row_sb = sb("row_sb", [B, NC, P], BF16)
        ps = [s.enter_context(nc.psum_tensor(f"ps_row{i}", [P, 8, P], BF16)) for i in range(4)]
        done, rowed, row_out, rows_out = map(sem, ("table_step", "rowed", "row_out", "rows_out"))
        wv = lambda k: t.wparts[:, :, k]
        field = [slots[:, r].rearrange("p c b -> p (c b)") for r in range(REC)]
        w = field[5:8]
        with nc.Block() as block:
            @block.vector
            def _(dve):
                v = nc.vector
                v.tensor_copy(t.src1[:], field[0])
                v.tensor_copy(t.dst1[:], field[1])
                v.tensor_scalar(minus[:], w[0], 0.0, -1.0, ALU.is_lt, ALU.mult).then_inc(done, 1)
                for r in range(3):
                    v.scalar_tensor_tensor(wv(r), w[0], 0.0, w[r], ALU.is_gt, ALU.mult)
                dve.wait_ge(done, 1)
                for r in range(3):
                    v.tensor_tensor(wv(3 + r), minus[:], w[r], ALU.mult)

            @block.gpsimd
            def _(pool):
                nc.gpsimd.memset(wv(6), 1.0)

            @block.tensor
            def _(pe):
                flat = slots[:, 0:5].rearrange("p r c b -> p (r c b)")
                for i in range(NC):
                    last = nc.tensor.transpose(ps[i // 8][0:B, i % 8, :], flat[:, i * B:(i + 1) * B], c.ident_bf[:])
                    if i % 8 == 7 or i == NC - 1:
                        last.then_inc(rowed, 1)

            @block.scalar
            def _(act):
                for g in range(4):
                    n = min(8, NC - 8 * g)
                    act.wait_ge(rowed, g + 1)
                    nc.scalar.copy(row_sb[:, 8 * g:8 * g + n, :], ps[g][0:B, 0:n, :]).then_inc(row_out, 1)

            @block.sync
            def _(sp):
                sp.wait_ge(row_out, 4)
                sp.dma_start(rows_d.rearrange("(n p r) -> p n r", p=B, r=P), row_sb[:]).then_inc(rows_out, 16)
                sp.wait_ge(rows_out, 16)


def l0_inputs(nc, ctx, t):
    sb = lambda n, sh, d: ctx.enter_context(nc.sbuf_tensor(f"L0_{n}", sh, d))
    sem = lambda n: ctx.enter_context(nc.semaphore(f"L0_{n}"))
    l = Bag()
    l.W1, l.W2, l.b1, l.b2 = sb("W1", [D, D], F32), sb("W2", [D, D], F32), sb("b1", [D, 1], F32), sb("b2", [B, D], F32)
    l.groups = [range(g, min(g + 6, NB)) for g in range(0, NB, 6)]
    xa = t.xa[0:D].rearrange("p b d -> p (b d)")
    l.xT = [xa[:, i * 6 * B:(i + 1) * 6 * B] for i in range(2)]
    l.small_in, l.x_in, l.xT_in = sem("small_in"), sem("x_in"), [sem("xT0_in"), sem("xT1_in")]
    return l


def load_xT(sp, a, l, g):
    lo, hi = l.groups[g][0] * B, (l.groups[g][-1] + 1) * B
    sp.dma_start(l.xT[g % 2][:, 0:hi - lo], a["xT"][:, lo:hi]).then_inc(l.xT_in[g % 2], 16)


def l1_weights(nc, ctx):
    sb = lambda n, sh, d: ctx.enter_context(nc.sbuf_tensor(f"L1_{n}", sh, d))
    w = Bag()
    w.eWa, w.eWb, w.eW2 = sb("eWa", [D, H], F32), sb("eWb", [D, H], F32), sb("eW2", [H, H], F32)
    w.nWa, w.nWb, w.nW2 = sb("nWa", [D, H], F32), sb("nWb", [H, H], F32), sb("nW2", [H, D], F32)
    w.eb1, w.nb1, w.nb2 = sb("eb1", [H, 1], F32), sb("nb1", [H, 1], F32), sb("nb2", [B, D], F32)
    w.wd, w.eb2 = sb("wd", [P, H], F32), sb("eb2", [P, H], F32)
    w.w_in = ctx.enter_context(nc.semaphore("L1_weights_in"))
    return w


def load_l1_weights(sp, a, w):
    n = "L1_gnn_"
    for out_, in_ in ((w.eWa[:], a[n + "eW1"][0:D]), (w.eWb[:], a[n + "eW1"][D:2 * D]), (w.eW2[:], a[n + "eW2"]),
                      (w.nWa[:], a[n + "nW1"][0:D]), (w.nWb[:], a[n + "nW1"][D:D + H]), (w.nW2[:], a[n + "nW2"]),
                      (w.eb1[:], a[n + "eb1"].rearrange("(d o) -> d o", o=1)),
                      (w.nb1[:], a[n + "nb1"].rearrange("(d o) -> d o", o=1)),
                      (w.nb2[:], a[n + "nb2"].partition_broadcast(B)),
                      (w.wd[:], a[n + "eW1"][2 * D].partition_broadcast(P)),
                      (w.eb2[:], a[n + "eb2"].partition_broadcast(P))):
        sp.dma_start(out_, in_).then_inc(w.w_in, 16)


def count_matrices(nc, a, c, t, m2_d, l0):
    with ExitStack() as s:
        sb = lambda n, sh, d: s.enter_context(nc.sbuf_tensor(n, sh, d))
        sem = lambda n: s.enter_context(nc.semaphore(n))
        pb = lambda n: s.enter_context(nc.psum_tensor(n, [P, 512], F32))
        POOL = [2, 6]
        DVE = [g for g in range(len(GROUPS)) if g not in POOL]
        dve_hot = [sb(f"onehot{i}", [P, 4, 2, P], BF16) for i in range(2)]
        pool_hot = [sb(f"pool_onehot{i}", [P, 4, 2, P], BF16) for i in range(2)]
        hot_of = lambda k, g: (pool_hot[POOL.index(g)] if g in POOL else dve_hot[(len(DVE) * k + DVE.index(g)) % 2])
        stage = [sb(f"codes{i}", [P, NC, 2], F32) for i in range(2)]
        panel = [sb(f"panel{i}", [B, MW], BF16) for i in range(2)]
        extra = sb("w_extra", [B, NB, WP], F32)
        A2, A1, WS = ([pb(f"{n}{i}") for i in range(2)] for n in ("ps_dst", "ps_src", "ps_w"))
        NG = len(GROUPS)
        stored = [sem("panel0_stored"), sem("panel1_stored")]
        turn = sb("pool_turn", [P, len(POOL)], F32)
        padded, staged, turns, dve_ready, pool_ready, counted, moved, added, wdone = map(sem, (
            "padded", "codes_staged", "pool_turns", "dve_onehots_ready", "pool_onehots_ready", "counted", "blocks_moved",
            "extras_added", "w_summed"))

        src1 = t.src1[:].rearrange("p (c b) -> p c b", b=NB)
        dst1 = t.dst1[:].rearrange("p (c b) -> p c b", b=NB)
        wparts = t.wparts[:].rearrange("p (c b) k -> p c b k", b=NB)
        with nc.Block() as block:
            @block.gpsimd
            def _(pool):
                nc.gpsimd.memset(t.mat[0:B, :, V:MW], 0.0)
                for k in range(2):
                    nc.gpsimd.memset(panel[k][:, V:MW], 0.0)
                nc.gpsimd.memset(t.wsum[:], 0.0).then_inc(padded, 1)
                pool.sem_inc(pool_ready, 1)

                def body(b, k):
                    pool.wait_ge(staged, b + 1)
                    for j, g in enumerate(POOL):
                        if not (isinstance(b, int) and b == 0):
                            pool.wait_ge(counted, NG * (b - 1) + g + 3)
                        nc.gpsimd.tensor_tensor(turn[:, j:j + 1], c.ones[:, 0:1], c.ones[:, 0:1], ALU.add
                                                ).then_inc(turns, 1)
                        for i, cc in enumerate(GROUPS[g]):
                            for e in range(2):
                                last = nc.gpsimd.tensor_scalar(hot_of(k, g)[:, i, e, :], c.iota1_bf[:],
                                                               stage[k][:, cc, e:e + 1], None, ALU.is_equal)
                        last.then_inc(pool_ready, 1)
                in_pairs(pool, NB, body)

            @block.vector
            def _(dve):
                dve.wait_ge(padded, 1)
                dve.sem_inc(added, 1)

                def add_extras(b, k):
                    bank = (k * NG + NG - 1) % 2
                    dve.wait_ge(moved, NG * b + NG)
                    v = panel[k][:, bass.ds(b * B, B)]
                    nc.vector.tensor_tensor(v, v, A2[bank][0:B, 128:128 + B], ALU.add)
                    m = t.mat[0:B, bass.ds(b, 1), bass.ds(b * B, B)].rearrange("p o n -> p (o n)")
                    nc.vector.tensor_tensor(m, m, A1[bank][0:B, 128:128 + B], ALU.add)
                    nc.vector.tensor_copy(extra[:, bass.ds(b, 1), :].rearrange("p o w -> p (o w)"),
                                          WS[k][0:B, NB * WP:NC * WP])
                    w = t.wsum[:].rearrange("p b w -> p (b w)")
                    nc.vector.tensor_tensor(w, w, WS[k][0:B, 0:NB * WP], ALU.add).then_inc(added, 1)

                def stage_codes(b, k):
                    if not (isinstance(b, int) and b == 0):
                        dve.wait_ge(dve_ready, len(DVE) * (b - 1))
                        dve.wait_ge(pool_ready, len(POOL) * (b - 1) + 1)
                        dve.wait_ge(turns, len(POOL) * (b - 1))
                    nc.vector.tensor_copy(stage[k][:, :, 0], src1[:, :, bass.ds(b, 1)].rearrange("p c o -> p (c o)"))
                    nc.vector.tensor_copy(stage[k][:, :, 1], dst1[:, :, bass.ds(b, 1)].rearrange("p c o -> p (c o)")
                                          ).then_inc(staged, 1)

                def body(b, k):
                    for j, g in enumerate(DVE):
                        before = NG * b + DVE[j - 2] - (0 if j >= 2 else NG)
                        if not (isinstance(b, int) and b == 0 and j < 2):
                            dve.wait_ge(counted, before + 3)
                        if j == 0:
                            dve.wait_ge(staged, b + 1)
                        lo, n = GROUPS[g][0], len(GROUPS[g])
                        nc.vector.tensor_tensor(
                            hot_of(k, g)[:, 0:n], c.iota1_bf[:].unsqueeze(1).unsqueeze(1).broadcast_to([P, n, 2, P]),
                            stage[k][:, lo:lo + n, :].unsqueeze(3).broadcast_to([P, n, 2, P]), ALU.is_equal
                            ).then_inc(dve_ready, 1)
                        if j == 2 and not (isinstance(b, int) and b == NB - 1):
                            stage_codes(b + 1, 1 - k)
                        if g == 1 and not (isinstance(b, int) and b == 0):
                            dve.wait_ge(added, b)
                            add_extras(b - 1, 1 - k)
                stage_codes(0, 0)
                in_pairs(dve, NB, body, last=2)
                dve.wait_ge(added, NB)
                add_extras(NB - 1, 0)
                dve.wait_ge(added, NB + 1)
                nc.vector.tensor_tensor(t.wsum[:], t.wsum[:], extra[:], ALU.add).then_inc(wdone, 1)

            @block.tensor
            def _(pe):
                pe.sem_inc(counted, 2)

                def body(b, k):
                    for g, tiles in enumerate(GROUPS):
                        bank = (k * NG + g) % 2
                        if g in POOL:
                            pe.wait_ge(pool_ready, len(POOL) * b + POOL.index(g) + 2)
                        else:
                            pe.wait_ge(dve_ready, len(DVE) * b + DVE.index(g) + 1)
                        if not (isinstance(b, int) and b == 0 and g < 2):
                            pe.wait_ge(moved, NG * b + g - 1)
                        if g == 1 and not (isinstance(b, int) and b == 0):
                            pe.wait_ge(added, b + 1)
                        for i, cc in enumerate(tiles):
                            s1, d1 = hot_of(k, g)[:, i, 0, :], hot_of(k, g)[:, i, 1, :]
                            o = slice(i * B, i * B + B) if cc < NB else slice(128, 128 + B)
                            nc.tensor.matmul(A2[bank][:, o], d1, s1[:, 0:B], start=True, stop=True)
                            nc.tensor.matmul(A1[bank][:, o], s1, d1[:, 0:B], start=True, stop=True)
                            last = nc.tensor.matmul(
                                WS[k][:, cc * WP:(cc + 1) * WP], s1,
                                wparts[:, cc, bass.ds(b, 1), :].rearrange("p o w -> p (o w)"), start=True, stop=True)
                        last.then_inc(counted, 1)
                in_pairs(pe, NB, body)

            @block.scalar
            def _(act):
                act.wait_ge(padded, 1)

                def body(b, k):
                    for g, tiles in enumerate(GROUPS):
                        bank, n = (k * NG + g) % 2, min(len(tiles), NB - tiles[0])
                        act.wait_ge(counted, NG * b + g + 3)
                        if g == 0 and not (isinstance(b, int) and b == 0):
                            act.wait_ge(stored[k], 8 * (b - k) + 16)
                        nc.scalar.copy(panel[k][:, tiles[0] * B:(tiles[0] + n) * B], A2[bank][0:B, 0:n * B])
                        nc.scalar.copy(t.mat[0:B, tiles[0]:tiles[0] + n, bass.ds(b * B, B)],
                                       A1[bank][0:B, 0:n * B].rearrange("p (c n) -> p c n", n=B)).then_inc(moved, 1)
                in_pairs(act, NB, body)

            @block.sync
            def _(sp):
                sp.dma_start(l0.W1[:], a["L0_gnn_W1"]).then_inc(l0.small_in, 16)
                sp.dma_start(l0.W2[:], a["L0_gnn_W2"]).then_inc(l0.small_in, 16)
                sp.dma_start(l0.b1[:], a["L0_gnn_b1"].rearrange("(d o) -> d o", o=1)).then_inc(l0.small_in, 16)
                sp.dma_start(l0.b2[:], a["L0_gnn_b2"].partition_broadcast(B)).then_inc(l0.small_in, 16)
                sp.dma_start(t.xb[:], a["x"].rearrange("(b p) d -> p b d", p=B)).then_inc(l0.x_in, 16)
                for g in range(2):
                    load_xT(sp, a, l0, g)
                for k in range(2):
                    sp.sem_inc(stored[k], 16)

                def body(b, k):
                    sp.wait_ge(added, b + 2)
                    sp.dma_start(m2_d[bass.ds(b, 1)].rearrange("o p n -> p (o n)"), panel[k][:]).then_inc(stored[k], 16)
                in_pairs(sp, NB, body)
                sp.wait_ge(stored[0], 16 * ((NB + 1) // 2) + 16)
                sp.wait_ge(stored[1], 16 * (NB // 2) + 16)


def spread(pe, nc, mat, ob, parts, ps):
    for kb in range(NB):
        last = nc.tensor.matmul(ps[:, 0:3 * D], mat[0:B, kb, ob * B:ob * B + P],
                                parts[:, kb].rearrange("p r d -> p (r d)"), start=(kb == 0), stop=(kb == NB - 1))
    return last


def split(nc, S, parts, src, rest):
    S(nc.vector.tensor_copy(parts(0), src))
    S.wait()
    S(nc.vector.tensor_tensor(rest, src, parts(0), ALU.subtract))
    S.wait()
    S(nc.vector.tensor_copy(parts(1), rest))
    S.wait()
    return nc.vector.tensor_tensor(parts(2), rest, parts(1), ALU.subtract)


def normalize(nc, dve, S, y, stats, mv, std, rstd, out, var_ready, std_ready, blocks=range(NB)):
    S.wait()
    for b in blocks:
        last = S(nc.vector.bn_stats(stats[:, b, :], y[:, b, :]))
    S.wait()
    for b in range(NB):
        last = nc.vector.bn_aggr(mv[:, b, :], stats[:, b, :])
    last.then_inc(var_ready, 1)
    dve.wait_ge(std_ready, 1)
    S(nc.vector.reciprocal(rstd[:], std[:]))
    S(nc.vector.tensor_tensor(y[:], y[:], mv[:, :, 0:1].broadcast_to([B, NB, D]), ALU.subtract))
    S.wait()
    return nc.vector.tensor_tensor(out, y[:], rstd[:].unsqueeze(2).broadcast_to([B, NB, D]), ALU.mult)


def roots(nc, act, c, mv, std, var_ready, std_ready):
    act.wait_ge(var_ready, 1)
    nc.scalar.activation(std[:], mv[:, :, 1], ACT.Sqrt, bias=c.eps[0:B, :]).then_inc(std_ready, 1)


def norm_buffers(sb):
    return (sb("bn", [B, NB, 6], F32), sb("mean_var", [B, NB, 2], F32), sb("std", [B, NB], F32),
            sb("rstd", [B, NB], F32))


def gcn_layers(nc, a, c, t, l0, l1):
    with ExitStack() as s:
        sb = lambda n, sh, d: s.enter_context(nc.sbuf_tensor(f"L0_{n}", sh, d))
        sem = lambda n: s.enter_context(nc.semaphore(f"L0_{n}"))
        pb = lambda n: s.enter_context(nc.psum_tensor(f"L0_{n}", [P, 512], F32))
        parts = [sb(f"gparts{i}", [B, NB, 3, D], BF16) for i in range(2)]
        xT, W1, W2, b1, b2, groups = l0.xT, l0.W1, l0.W2, l0.b1, l0.b2, l0.groups
        small_in, x_in, xT_in = l0.small_in, l0.x_in, l0.xT_in
        rest = sb("rest", [B, 6, D], F32)
        sumr = [sb(f"sumr{i}", [B, D], F32) for i in range(2)]
        hT = [sb(f"hT{i}", [D, B], F32) for i in range(2)]
        bn, mv, std, rstd = norm_buffers(sb)
        psA, psT, psZ = ([pb(f"{n}{i}") for i in range(2)] for n in ("psA", "psT", "psZ"))
        h_ready, parts_ready, sums, summed, turned, relued, z_ready, step, xb, y2, var, root = map(
            sem, ("h_ready", "parts_ready", "sums_ready", "sum_kept",
                  "turned", "hidden_ready", "z_ready", "gcn_step", "x_bias", "rows_done", "var_ready", "std_ready"))
        y = t.xa
        with nc.Block() as block:
            @block.sync
            def _(sp):
                for g in range(2, len(groups)):
                    sp.wait_ge(h_ready, g - 1)
                    load_xT(sp, a, l0, g)
                load_l1_weights(sp, a, l1)

            @block.tensor
            def _(pe):
                pe.wait_ge(small_in, 64)
                for g, blocks in enumerate(groups):
                    pe.wait_ge(xT_in[g % 2], 16 * (g // 2 + 1))
                    if g >= 2:
                        pe.wait_ge(parts_ready, g - 1)
                    for b in blocks:
                        last = nc.tensor.matmul(psZ[g % 2][0:B, (b % 6) * D:(b % 6 + 1) * D], xT[g % 2][:, b % 6 * B:(b % 6 + 1) * B],
                                                W1[:], start=True, stop=True)
                    last.then_inc(h_ready, 1)
                pe.wait_ge(parts_ready, len(groups))

                def turn(b):
                    pe.wait_ge(summed, b + 1)
                    if b >= 2:
                        pe.wait_ge(relued, b - 1)
                    nc.tensor.transpose(psT[b % 2][0:D, 0:B], sumr[b % 2][:], c.ident[0:B, 0:B]).then_inc(turned, 1)

                def times_w2(b):
                    pe.wait_ge(relued, b + 1)
                    if b >= 2:
                        pe.wait_ge(parts_ready, len(groups) + b - 1)
                    nc.tensor.matmul(psZ[b % 2][0:B, 0:D], hT[b % 2][:], W2[:], start=True, stop=True
                                     ).then_inc(z_ready, 1)

                for b in range(NB):
                    if b >= 2:
                        pe.wait_ge(summed, b - 1)
                    spread(pe, nc, t.mat, b, parts[0], psA[b % 2]).then_inc(sums, 1)
                    if b >= 1:
                        turn(b - 1)
                    if b >= 2:
                        times_w2(b - 2)
                turn(NB - 1)
                times_w2(NB - 2)
                times_w2(NB - 1)
                pe.wait_ge(parts_ready, len(groups) + NB)
                for b in range(NB):
                    if b >= 2:
                        pe.wait_ge(y2, b - 1)
                    spread(pe, nc, t.mat, b, parts[1], psA[b % 2]).then_inc(sums, 1)

            @block.scalar
            def _(act):
                act.wait_ge(small_in, 64)
                for b in range(NB):
                    act.wait_ge(turned, b + 1)
                    if b >= 2:
                        act.wait_ge(z_ready, b - 1)
                    nc.scalar.activation(hT[b % 2][:], psT[b % 2][0:D, 0:B], ACT.Relu, bias=b1[:]).then_inc(relued, 1)
                roots(nc, act, c, mv, std, var, root)

            @block.vector
            def _(dve):
                S = Steps(dve, step)

                def hidden_parts(b):
                    dve.wait_ge(z_ready, b + 1)
                    dve.wait_ge(parts_ready, len(groups) + b)
                    split(nc, S, lambda r: parts[1][:, b, r, :], psZ[b % 2][0:B, 0:D], rest[:, 0, :]
                          ).then_inc(parts_ready, 1)

                dve.wait_ge(small_in, 64)
                dve.wait_ge(x_in, 16)
                nc.vector.tensor_tensor(t.xb[:], t.xb[:], b2[:].unsqueeze(1).broadcast_to([B, NB, D]), ALU.add
                                        ).then_inc(xb, 1)
                for g, blocks in enumerate(groups):
                    n, b = len(blocks), blocks[0]
                    src = psZ[g % 2][0:B, 0:n * D].rearrange("p (b d) -> p b d", d=D)
                    dve.wait_ge(h_ready, g + 1)
                    if g:
                        dve.wait_ge(parts_ready, g)
                    split(nc, S, lambda r: parts[0][:, b:b + n, r, :], src, rest[:, 0:n, :]).then_inc(parts_ready, 1)
                for b in range(NB):
                    dve.wait_ge(sums, b + 1)
                    if b >= 2:
                        dve.wait_ge(turned, b - 1)
                    nc.vector.reduce_sum(sumr[b % 2][:], psA[b % 2][0:B, 0:3 * D].rearrange("p (r d) -> p d r", r=3),
                                         X).then_inc(summed, 1)
                    if b >= 2:
                        hidden_parts(b - 2)
                hidden_parts(NB - 2)
                hidden_parts(NB - 1)
                dve.wait_ge(xb, 1)
                for b in range(NB):
                    k = b % 2
                    dve.wait_ge(sums, NB + b + 1)
                    if b == 0:
                        S.wait()
                        dve.wait_ge(summed, NB)
                    else:
                        dve.wait_ge(y2, b)
                    S(nc.vector.reduce_sum(sumr[k][:], psA[k][0:B, 0:3 * D].rearrange("p (r d) -> p d r", r=3), X))
                    S.wait()
                    nc.vector.tensor_tensor(y[:, b, :], sumr[k][:], t.xb[:, b, :], ALU.add).then_inc(y2, 1)
                    if b >= 1:
                        S(nc.vector.bn_stats(bn[:, b - 1, :], y[:, b - 1, :]))
                dve.wait_ge(y2, NB)
                normalize(nc, dve, S, y, bn, mv, std, rstd, t.xb[:], var, root, range(NB - 1, NB)).then_inc(xb, 1)


def edge_network(nc, a, c, t, rows_d, m2_d, w):
    HEAD = 17
    HOT = NC * P
    with ExitStack() as s:
        sb = lambda n, sh, d: s.enter_context(nc.sbuf_tensor(f"L1_{n}", sh, d))
        sem = lambda n: s.enter_context(nc.semaphore(f"L1_{n}"))
        pb = lambda n: s.enter_context(nc.psum_tensor(f"L1_{n}", [P, 512], F32))
        room = t.mat[:, HEAD:NB, :].rearrange("p a b -> p (a b)")
        q = room[:, 0:NB * 3 * H].rearrange("p (b r h) -> p b r h", r=3, h=H)
        o = NB * 3 * H
        x1T = room[0:D, o:o + 2 * (NB + 1) * B].bitcast(F32)
        o += 2 * (NB + 1) * B
        srow = [room[:, o + i * HOT:o + (i + 1) * HOT] for i in range(2)]
        drow = [sb(f"drow{i}", [P, HOT], BF16) for i in range(2)]
        eWa, eWb, eW2, nWa, nWb, nW2 = w.eWa, w.eWb, w.eW2, w.nWa, w.nWb, w.nW2
        eb1, nb1, nb2, wd, eb2, w_in = w.eb1, w.nb1, w.nb2, w.wd, w.eb2, w.w_in
        wd3 = sb("wd3", [P, 3, H], BF16)
        o += 2 * HOT
        rest = room[:, o:o + 8 * H].bitcast(F32)
        rest2 = room[:, o + 8 * H:o + 16 * H].bitcast(F32)
        pp = [sb(f"pp{i}", [B, 3, H], BF16) for i in range(2)]
        xs = [sb(f"xs{i}", [D, B], F32) for i in range(2)]
        codes = [sb(f"scodes{i}", [P, NC], F32) for i in range(2)]
        hot = [sb(f"hot{i}", [P, 4, B], F32) for i in range(2)]
        e1 = [sb("e1", [H, 4 * P], F32), rest2]
        e2 = [sb(f"e2_{i}", [P, 4 * H], F32) for i in range(2)]
        aggs = [sb(f"aggs{i}", [H, B], F32) for i in range(2)]
        z1 = sb("z1", [H, B], F32)
        bn, mv, std, rstd = norm_buffers(sb)
        ps_pre, ps_z2, ps_agg = ([pb(f"{n}{i}") for i in range(2)] for n in ("ps_pre", "ps_z2", "ps_agg"))
        ps_n, ps_p = pb("ps_n"), pb("ps_p")
        turned, x1t_ready, q_ps, q_cast, q_cut, q_done, prep, wd_set, q_tail = map(sem, (
            "x1_turned", "x1T_ready", "q_ready", "q_cast", "q_cut", "q_split", "prep_step", "wd_parts", "q_tail"))
        rows_in = [sem("rows0_in"), sem("rows1_in")]
        rows = rows_d.rearrange("(f c b r) -> f c b r", f=5, c=NC, r=P)
        one = lambda ap: ap.rearrange("o n -> (o n)")

        def load_rows(sp, b, k):
            for buf, f in ((srow, 0), (drow, 1)):
                sp.dma_start(buf[k][0:B, 0:NB * P],
                             one(rows[f, bass.ds(b, 1)].rearrange("o b r -> o (b r)")).partition_broadcast(B)
                             ).then_inc(rows_in[k], 16)
                sp.dma_start(buf[k][0:B, NB * P:HOT],
                             one(rows[f, NB, bass.ds(b, 1)]).partition_broadcast(B)).then_inc(rows_in[k], 16)
            sp.dma_start(drow[k][B:P, 0:NB * P], rows[2:5, bass.ds(b, 1)].rearrange("f o b r -> f (o b r)")
                         ).then_inc(rows_in[k], 16)
            sp.dma_start(drow[k][B:P, NB * P:HOT], rows[2:5, NB, bass.ds(b, 1)].rearrange("f o r -> f (o r)")
                         ).then_inc(rows_in[k], 16)

        NG = len(GROUPS)
        tile_groups = [range(g, min(g + 4, NB)) for g in range(0, NB, 4)]
        q_part = lambda g, r: q[0:B, tile_groups[g][0]:tile_groups[g][-1] + 1, r, :]
        by_block = lambda ap, g: ap[0:B, 0:len(tile_groups[g]) * H].rearrange("p (b h) -> p b h", h=H)
        q_sum = lambda g: by_block(ps_z2[g % 2], g)
        q_rest = lambda g: by_block((rest, rest2)[g % 2], g)
        with nc.Block() as block:
            @block.sync
            def _(sp):
                load_rows(sp, 0, 0)
                sp.wait_ge(wd_set, 1)
                sp.dma_start(q[B:P], wd3[B:P].unsqueeze(1).broadcast_to([3, NB, 3, H])).then_inc(q_tail, 16)
                sp.wait_ge(q_tail, 16)

            @block.gpsimd
            def _(pool):
                nc.gpsimd.memset(x1T[:, NB * B:], 0.0)

            @block.tensor
            def _(pe):
                for g, blocks in enumerate(tile_groups):
                    if g >= 2:
                        pe.wait_ge(x1t_ready, g - 1)
                    for i, b in enumerate(blocks):
                        last = nc.tensor.transpose(ps_pre[g % 2][0:D, i * P:i * P + B], t.xb[:, b, :],
                                                   c.ident[0:B, 0:B])
                    last.then_inc(turned, 1)
                pe.wait_ge(w_in, 16 * 11)
                for g, blocks in enumerate(tile_groups):
                    pe.wait_ge(x1t_ready, g + 1)
                    if g >= 2:
                        pe.wait_ge(q_cut, g - 1)
                    for i, b in enumerate(blocks):
                        last = nc.tensor.matmul(ps_z2[g % 2][0:B, i * H:(i + 1) * H], x1T[:, b * B:(b + 1) * B],
                                                eWb[:], start=True, stop=True)
                    last.then_inc(q_ps, 1)

            @block.scalar
            def _(act):
                for g, blocks in enumerate(tile_groups):
                    act.wait_ge(turned, g + 1)
                    n = len(blocks)
                    nc.scalar.copy(x1T[:, 4 * g * B:(4 * g + n) * B].rearrange("p (b n) -> p b n", n=B),
                                   ps_pre[g % 2][0:D, 0:n * P].rearrange("p (b n) -> p b n", n=P)[:, :, 0:B]
                                   ).then_inc(x1t_ready, 1)
                for g in range(len(tile_groups) + 1):
                    if g < len(tile_groups):
                        act.wait_ge(q_ps, g + 1)
                        nc.scalar.copy(q_part(g, 0), q_sum(g)).then_inc(q_cast, 1)
                    if g >= 1:
                        act.wait_ge(q_cut, g)
                        nc.scalar.copy(q_part(g - 1, 1), q_rest(g - 1)).then_inc(q_cast, 1)

            @block.vector
            def _(dve):
                S = Steps(dve, prep)
                dve.wait_ge(w_in, 16 * 11)
                split(nc, S, lambda r: wd3[:, r, :], wd[:], rest[:, 0:H]).then_inc(wd_set, 1)
                dve.wait_ge(turned, len(tile_groups))
                S(nc.vector.tensor_tensor(t.xb[:], t.xb[:], nb2[:].unsqueeze(1).broadcast_to([B, NB, D]), ALU.add))
                dve.wait_ge(wd_set, 1)
                for g in range(len(tile_groups) + 1):
                    if g < len(tile_groups):
                        dve.wait_ge(q_cast, max(1, 2 * g))
                        if g >= 2:
                            dve.wait_ge(q_done, g - 1)
                        nc.vector.tensor_tensor(q_rest(g), q_sum(g), q_part(g, 0), ALU.subtract).then_inc(q_cut, 1)
                    if g >= 1:
                        dve.wait_ge(q_cast, 2 * g + 1 if g < len(tile_groups) else 2 * g)
                        nc.vector.tensor_tensor(q_part(g - 1, 2), q_rest(g - 1), q_part(g - 1, 1), ALU.subtract
                                                ).then_inc(q_done, 1)

        (panels_in, rows_hot, staged, pre_done, e1_ready, z2_done, biased, e2_ready, hot_ready, seg_done, agg_ready, n1_ready,
         z1_ready, out_ready, out_kept, xs_ready, p_ps, p_ready, var, root, step) = map(sem, (
             "panels_in", "rows_hot", "codes_staged", "pre_done", "e1_ready", "z2_done", "biased", "e2_ready", "onehots_ready",
             "seg_done", "agg_ready", "n1_ready", "z1_ready", "out_ready", "out_kept", "xs_ready", "p_product",
             "p_ready", "var_ready", "std_ready", "net_step"))
        first = lambda b: isinstance(b, int) and b == 0
        with nc.Block() as block:
            @block.sync
            def _(sp):
                def body(b, k):
                    if not first(b):
                        sp.wait_ge(pre_done, NG * (b - 1) + 1)
                        load_rows(sp, b, k)
                in_pairs(sp, NB, body)
                sp.wait_ge(panels_in, 16 * HEAD)

            @block.gpsimd
            def _(pool):
                with pool.Fori(0, HEAD) as i:
                    pool.wait_ge(pre_done, NG * i + 1)
                    pool.wait_ge(xs_ready, 1)
                    pool.dma_start(t.mat[0:B, bass.ds(i, 1), :].rearrange("p o n -> p (o n)"),
                                   m2_d[bass.ds(i, 1)].rearrange("o p n -> p (o n)")).then_inc(panels_in, 16)

            @block.tensor
            def _(pe):
                def product_p(b, k):
                    pe.wait_ge(xs_ready, b + 1)
                    nc.tensor.matmul(ps_p[0:B, 0:H], xs[k][:], eWa[:], start=True, stop=True).then_inc(p_ps, 1)

                def layer1(b, k, g):
                    bank, tiles = (k * NG + g) % 2, GROUPS[g]
                    lo, hi = tiles[0] * P, (tiles[-1] + 1) * P
                    if g == 0:
                        pe.wait_ge(rows_hot, b + 1)
                        pe.wait_ge(p_ready, b + 1)
                    if not (first(b) and g < 2):
                        pe.wait_ge(e1_ready, NG * b + g - 1)
                    for r in range(3):
                        nc.tensor.matmul(ps_pre[bank][:, 0:hi - lo], pp[k][:, r, :], srow[k][0:B, lo:hi],
                                         start=(r == 0), stop=False)
                    for i, cc in enumerate(tiles):
                        for r in range(3):
                            w = (q[:, cc, r, :] if cc < NB else
                                 q[:, bass.ds(b, 1), r, :].rearrange("p o h -> p (o h)"))
                            last = nc.tensor.matmul(ps_pre[bank][:, i * P:(i + 1) * P], w,
                                                    drow[k][:, cc * P:(cc + 1) * P], start=False,
                                                    stop=(r == 2 and cc == tiles[-1]))
                    last.then_inc(pre_done, 1)

                def layer2(b, k, g):
                    bank, tiles = (k * NG + g) % 2, GROUPS[g]
                    pe.wait_ge(e1_ready, NG * b + g + 1)
                    if not (first(b) and g < 2):
                        pe.wait_ge(biased, NG * b + g - 1)
                    for i, cc in enumerate(tiles):
                        last = nc.tensor.matmul(ps_z2[bank][:, i * H:(i + 1) * H], e1[bank][:, i * P:(i + 1) * P],
                                                eW2[:], start=True, stop=True)
                    last.then_inc(z2_done, 1)

                def by_src(b, k, g):
                    bank, tiles = (k * NG + g) % 2, GROUPS[g]
                    pe.wait_ge(e2_ready, NG * b + g + 1)
                    pe.wait_ge(hot_ready, NG * b + g + 2)
                    if g == 0 and not first(b):
                        pe.wait_ge(agg_ready, b)
                    for i, cc in enumerate(tiles):
                        last = nc.tensor.matmul(ps_agg[k][:, 0:B], e2[bank][:, i * H:(i + 1) * H], hot[bank][:, i, :],
                                                start=(cc == 0), stop=(cc == NC - 1))
                    last.then_inc(seg_done, 1)

                def node1(b, k):
                    pe.wait_ge(agg_ready, b + 2)
                    if not first(b):
                        pe.wait_ge(out_kept, b + 1)
                    nc.tensor.matmul(ps_n[:, 0:B], nWa[:], xs[k][:], start=True, stop=False)
                    nc.tensor.matmul(ps_n[:, 0:B], nWb[:], aggs[k][:], start=False, stop=True).then_inc(n1_ready, 1)

                def node2(b, k):
                    pe.wait_ge(z1_ready, b + 1)
                    nc.tensor.matmul(ps_n[0:B, 256:256 + D], z1[:], nW2[:], start=True, stop=True
                                     ).then_inc(out_ready, 1)

                def body(b, k):
                    was = None if first(b) else (b - 1, 1 - k)
                    for g in range(NG):
                        layer1(b, k, g)
                        if g >= 1:
                            layer2(b, k, g - 1)
                        elif was:
                            layer2(*was, NG - 1)
                        if g >= 2:
                            by_src(b, k, g - 2)
                        elif was:
                            by_src(*was, NG - 2 + g)
                        if was and g == 2:
                            node1(*was)
                        if was and g == 3:
                            node2(*was)
                        if g == 4:
                            product_p(b + 1, 1 - k)
                for count in (pre_done, n1_ready, out_ready):
                    pe.sem_inc(count, 1)
                product_p(0, 0)
                in_pairs(pe, NB, body)
                z = NB - 1
                layer2(z, 0, NG - 1)
                by_src(z, 0, NG - 2)
                by_src(z, 0, NG - 1)
                node1(z, 0)
                node2(z, 0)

            @block.scalar
            def _(act):
                def stage_x(b, k):
                    nc.scalar.copy(xs[k][:], x1T[:, bass.ds(b * B, B)]).then_inc(xs_ready, 1)

                def silu1(b, k, g):
                    bank, n = (k * NG + g) % 2, len(GROUPS[g]) * P
                    act.wait_ge(pre_done, NG * b + g + 2)
                    if not (first(b) and g < 2):
                        act.wait_ge(z2_done, NG * b + g - 1)
                    nc.scalar.activation(e1[bank][:, 0:n], ps_pre[bank][:, 0:n], ACT.Silu, bias=eb1[:]
                                         ).then_inc(e1_ready, 1)

                def silu2(b, k, g):
                    bank, n = (k * NG + g) % 2, len(GROUPS[g]) * H
                    act.wait_ge(biased, NG * b + g + 1)
                    nc.scalar.activation(e2[bank][:, 0:n], e2[bank][:, 0:n], ACT.Silu).then_inc(e2_ready, 1)

                def keep_agg(b, k):
                    act.wait_ge(seg_done, NG * b + NG)
                    act.wait_ge(n1_ready, b + 1)
                    nc.scalar.copy(aggs[k][:], ps_agg[k][:, 0:B]).then_inc(agg_ready, 1)

                def node_silu(b, k):
                    act.wait_ge(n1_ready, b + 2)
                    if not first(b):
                        act.wait_ge(out_ready, b + 1)
                    nc.scalar.activation(z1[:], ps_n[:, 0:B], ACT.Silu, bias=nb1[:]).then_inc(z1_ready, 1)

                def body(b, k):
                    was = None if first(b) else (b - 1, 1 - k)
                    for g in range(NG):
                        silu1(b, k, g)
                        if g >= 1:
                            silu2(b, k, g - 1)
                        elif was:
                            silu2(*was, NG - 1)
                        if was and g == 1:
                            keep_agg(*was)
                        if was and g == 2:
                            node_silu(*was)
                        if g == 3:
                            act.wait_ge(p_ps, b + 1)
                            stage_x(b + 1, 1 - k)
                act.sem_inc(agg_ready, 1)
                stage_x(0, 0)
                in_pairs(act, NB, body)
                z = NB - 1
                silu2(z, 0, NG - 1)
                keep_agg(z, 0)
                node_silu(z, 0)
                roots(nc, act, c, mv, std, var, root)

            @block.vector
            def _(dve):
                S = Steps(dve, step)

                def split_p(b, k):
                    dve.wait_ge(p_ps, b + 1)
                    if not first(b):
                        dve.wait_ge(p_ready, b)
                        dve.wait_ge(pre_done, NG * (b - 1) + 1)
                    dve.wait_ge(step, 3 * b if not isinstance(b, int) else 3 * b)
                    v = nc.vector
                    v.tensor_copy(pp[k][:, 0, :], ps_p[0:B, 0:H]).then_inc(step, 1)
                    dve.wait_ge(step, 3 * b + 1)
                    v.tensor_tensor(rest[0:B, 0:H], ps_p[0:B, 0:H], pp[k][:, 0, :], ALU.subtract).then_inc(step, 1)
                    dve.wait_ge(step, 3 * b + 2)
                    v.tensor_copy(pp[k][:, 1, :], rest[0:B, 0:H]).then_inc(step, 1)
                    dve.wait_ge(step, 3 * b + 3)
                    v.tensor_tensor(pp[k][:, 2, :], rest[0:B, 0:H], pp[k][:, 1, :], ALU.subtract).then_inc(p_ready, 1)

                def keep_out(b, k):
                    dve.wait_ge(out_ready, b + 2)
                    nc.vector.tensor_tensor(t.xa[:, bass.ds(b, 1), :].rearrange("p o d -> p (o d)"),
                                            ps_n[0:B, 256:256 + D],
                                            t.xb[:, bass.ds(b, 1), :].rearrange("p o d -> p (o d)"), ALU.add
                                            ).then_inc(out_kept, 1)

                def rows_to_hot(b, k):
                    if not first(b):
                        dve.wait_ge(hot_ready, NG * (b - 1) + 1)
                    nc.vector.tensor_copy(codes[k][:, 0:NB], t.src1[:, bass.ds(b * NB, NB)])
                    nc.vector.tensor_copy(codes[k][:, NB:NC], t.src1[:, bass.ds(b + NB * NB, 1)]).then_inc(staged, 1)
                    dve.wait_ge(rows_in[k], 48 * (b - k) + 96)
                    nc.vector.tensor_scalar(srow[k][0:B, :], srow[k][0:B, :], c.row1[0:B, :], None, ALU.is_equal)

                def dst_rows_to_hot(b, k):
                    nc.vector.tensor_scalar(drow[k][0:B, :], drow[k][0:B, :], c.row1[0:B, :], None, ALU.is_equal
                                            ).then_inc(rows_hot, 1)

                def add_bias(b, k, g):
                    bank, tiles = (k * NG + g) % 2, GROUPS[g]
                    dve.wait_ge(z2_done, NG * b + g + 1)
                    if not (first(b) and g < 2):
                        dve.wait_ge(seg_done, NG * b + g - 1)
                    grp = lambda t: t[:, 0:len(tiles) * H].rearrange("p (i h) -> p i h", h=H)
                    nc.vector.tensor_tensor(grp(e2[bank]), grp(ps_z2[bank]),
                                            eb2[:].unsqueeze(1).broadcast_to([P, len(tiles), H]), ALU.add
                                            ).then_inc(biased, 1)

                def body(b, k):
                    dve.wait_ge(staged, b + 1)
                    for g, tiles in enumerate(GROUPS):
                        bank = (k * NG + g) % 2
                        if g >= 1:
                            add_bias(b, k, g - 1)
                        elif not first(b):
                            add_bias(b - 1, 1 - k, NG - 1)
                        if not (first(b) and g < 2):
                            dve.wait_ge(seg_done, NG * b + g - 1)
                        for i, cc in enumerate(tiles):
                            last = nc.vector.tensor_scalar(hot[bank][:, i, :], c.iota1[:, 0:B],
                                                           codes[k][:, cc:cc + 1], None, ALU.is_equal)
                        last.then_inc(hot_ready, 1)
                        if g == 4 and not first(b):
                            keep_out(b - 1, 1 - k)
                        if g == 5:
                            split_p(b + 1, 1 - k)
                        if not (isinstance(b, int) and b == NB - 1):
                            if g == 3:
                                rows_to_hot(b + 1, 1 - k)
                            if g == 4:
                                dst_rows_to_hot(b + 1, 1 - k)
                for count in (hot_ready, out_kept):
                    dve.sem_inc(count, 1)
                rows_to_hot(0, 0)
                dst_rows_to_hot(0, 0)
                split_p(0, 0)
                in_pairs(dve, NB, body, last=2)
                add_bias(NB - 1, 0, NG - 1)
                keep_out(NB - 1, 0)
                dve.wait_ge(out_kept, NB + 1)
                S.n = 3 * (NB + 1)
                normalize(nc, dve, S, t.xa, bn, mv, std, rstd, t.xb[:], var, root)


def message_layer(nc, a, c, t, m2_d, HEAD=17):
    with ExitStack() as s:
        sb = lambda n, sh, d: s.enter_context(nc.sbuf_tensor(f"L2_{n}", sh, d))
        sem = lambda n: s.enter_context(nc.semaphore(f"L2_{n}"))
        pb = lambda n: s.enter_context(nc.psum_tensor(f"L2_{n}", [P, 512], F32))
        parts = sb("parts", [B, NB, 3, D], BF16)
        base = sb("base", [B, NB, D], F32)
        x2T = [sb(f"x2T{i}", [D, 4 * B], F32) for i in range(2)]
        feat = [sb(f"feat{i}", [D + 2, 4 * B], F32) for i in range(2)]
        mix = sb("mix", [D + 2, 2 * D], F32)
        W3T, W4a, W4b = (sb(n, [D, D], F32) for n in ("W3T", "W4a", "W4b"))
        w1c, w2c = sb("w1c", [D, 1], F32), sb("w2c", [D, 1], F32)
        w1pm, w2pm, ge = sb("w1pm", [D, D + 2], F32), sb("w2pm", [D, 2, B], F32), sb("ge", [B, 2, D], F32)
        we = sb("we", [B, NB, 2], F32)
        sumr = [sb(f"sumr{i}", [B, D], F32) for i in range(2)]
        rest = sb("rest", [B, 4, D], F32)
        bn, mv, std, rstd = norm_buffers(sb)
        psT, psM, psZ = ([pb(f"{n}{i}") for i in range(2)] for n in ("psT", "psM", "psZ"))
        psG = pb("psG")
        nv_in = [sem("nv0_in"), sem("nv1_in")]
        (w_in, tail_in, turned, x2t, hmu_ps, hmut, z_ps, parts_ready, nv_set, w_set, g_ps, g_set, sums, kept, var, root,
         step) = map(sem, ("weights_in", "tail_in", "x2_turned", "x2T_ready", "hmu_product", "hmuT_ready", "z_product",
                           "parts_ready", "nv_set", "w_parts", "g_product", "g_set", "sums_ready", "rows_kept",
                           "var_ready", "std_ready", "msg_step"))
        groups = [range(g, min(g + 4, NB)) for g in range(0, NB, 4)]
        with nc.Block() as block:
            @block.sync
            def _(sp):
                n = "L2_gnn_"
                for out_, in_ in ((W3T[:], a["W3T"]), (W4a[:], a["W4T"][0:D]), (W4b[:], a["W4T"][D:2 * D]),
                                  (mix[0:D, 0:D], a["W4T"][2 * D:3 * D]), (w1c[:], a[n + "W1"]), (w2c[:], a[n + "W2"]),
                                  (mix[D:D + 2, D:2 * D],
                                   a[n + "W1"].rearrange("d o -> (d o)").partition_broadcast(2))):
                    sp.dma_start(out_, in_).then_inc(w_in, 16)
                for g, blocks in enumerate(groups):
                    if g >= 2:
                        sp.wait_ge(z_ps, g - 1)
                    lo, hi = blocks[0] * B, (blocks[-1] + 1) * B
                    sp.dma_start(feat[g % 2][D:D + 2, 0:hi - lo], a["node_vec1"][lo:hi].partition_broadcast(2)
                                 ).then_inc(nv_in[g % 2], 16)

            @block.scalar
            def _(act):
                act.wait_ge(w_in, 16 * 7)
                act.dma_start(t.mat[0:B, HEAD:NB, :], m2_d[HEAD:NB].rearrange("b p n -> p b n")).then_inc(tail_in, 16)
                for g, blocks in enumerate(groups):
                    n = len(blocks)
                    act.wait_ge(turned, g + 1)
                    if g >= 2:
                        act.wait_ge(z_ps, g - 1)
                    nc.scalar.copy(x2T[g % 2][:, 0:n * B].rearrange("p (b n) -> p b n", n=B),
                                   psT[g % 2][0:D, 0:n * P].rearrange("p (b n) -> p b n", n=P)[:, :, 0:B]
                                   ).then_inc(x2t, 1)
                    act.wait_ge(hmu_ps, g + 1)
                    nc.scalar.activation(feat[g % 2][0:D, 0:n * B], psM[g % 2][0:D, 0:n * B], ACT.Relu).then_inc(hmut, 1)
                roots(nc, act, c, mv, std, var, root)

            @block.tensor
            def _(pe):
                def turn(g):
                    if g >= 2:
                        pe.wait_ge(x2t, g - 1)
                    for i, b in enumerate(groups[g]):
                        last = nc.tensor.transpose(psT[g % 2][0:D, i * P:i * P + B], t.xb[:, b, :], c.ident[0:B, 0:B])
                    last.then_inc(turned, 1)
                turn(0)
                pe.wait_ge(w_in, 16 * 7)
                pe.wait_ge(w_set, 1)
                nc.tensor.matmul(psG[0:D + 2, 128:128 + D], w1pm[:], W4a[:], start=True, stop=True)
                for i in range(2):
                    last = nc.tensor.matmul(psG[0:B, i * D:(i + 1) * D], w2pm[:, i, :], W4b[:], start=True,
                                            stop=True)
                last.then_inc(g_ps, 1)
                for g, blocks in enumerate(groups):
                    k, n = g % 2, len(blocks)
                    if g + 1 < len(groups):
                        turn(g + 1)
                    pe.wait_ge(x2t, g + 1)
                    if g >= 2:
                        pe.wait_ge(hmut, g - 1)
                    nc.tensor.matmul(psM[k][0:D, 0:n * B], W3T[:], x2T[k][:, 0:n * B], start=True, stop=True
                                     ).then_inc(hmu_ps, 1)
                    if g >= 2:
                        pe.wait_ge(parts_ready, g - 1)
                    pe.wait_ge(nv_set, g + 1)
                    pe.wait_ge(g_set, 1)
                    pe.wait_ge(hmut, g + 1)
                    for i in range(n):
                        last = nc.tensor.matmul(psZ[k][0:B, i * 2 * D:(i + 1) * 2 * D], feat[k][:, i * B:(i + 1) * B],
                                                mix[:], start=True, stop=True)
                    last.then_inc(z_ps, 1)
                pe.wait_ge(tail_in, 16)
                pe.wait_ge(parts_ready, len(groups))
                for b in range(NB):
                    if b >= 2:
                        pe.wait_ge(kept, b - 1)
                    spread(pe, nc, t.mat, b, parts, psT[b % 2]).then_inc(sums, 1)

            @block.vector
            def _(dve):
                S = Steps(dve, step)
                v = nc.vector
                dve.wait_ge(w_in, 16 * 7)
                S(v.memset(w1pm[:, 0:D], 0.0))
                S(v.tensor_copy(mix[0:D, D:2 * D], c.ident[0:D, 0:D]))
                S(v.tensor_scalar(w1pm[:, D:D + 1], w1c[:], 0.0, None, ALU.max))
                S(v.tensor_scalar(w1pm[:, D + 1:D + 2], w1c[:], -1.0, 0.0, ALU.mult, ALU.max))
                S(v.tensor_scalar(w2pm[:, 0, :], c.ones[0:D, 0:B], w2c[:], 0.0, ALU.mult, ALU.max))
                S(v.tensor_scalar(w2pm[:, 1, :], c.ones[0:D, 0:B], w2c[:], -1.0, ALU.mult, ALU.mult))
                S(v.tensor_scalar(mix[D:D + 2, D:2 * D], mix[D:D + 2, D:2 * D], c.sign[D:D + 2, :], 0.0, ALU.mult,
                                  ALU.max))
                S(v.reduce_sum(we[:], t.wsum[:, :, 0:6].rearrange("p b (s r) -> p b s r", r=3), X))
                S.wait()
                v.tensor_scalar(w2pm[:, 1, :], w2pm[:, 1, :], 0.0, None, ALU.max).then_inc(w_set, 1)
                dve.wait_ge(g_ps, 1)
                v.tensor_copy(ge[:].rearrange("p s d -> p (s d)"), psG[0:B, 0:2 * D])
                v.tensor_copy(mix[D:D + 2, 0:D], psG[D:D + 2, 128:128 + D]).then_inc(g_set, 1)
                for g, blocks in enumerate(groups):
                    k, n, b = g % 2, len(blocks), blocks[0]
                    dve.wait_ge(nv_in[k], 16 * (g // 2 + 1))
                    nv = feat[k][D:D + 2, 0:n * B]
                    v.tensor_scalar(nv, nv, c.sign[D:D + 2, :], 0.0, ALU.mult, ALU.max).then_inc(nv_set, 1)
                    dve.wait_ge(z_ps, g + 1)
                    both = psZ[k][0:B, 0:n * 2 * D].rearrange("p (b d) -> p b d", d=2 * D)
                    S(v.tensor_copy(base[:, b:b + n, :], both[:, :, D:2 * D]))
                    if g:
                        dve.wait_ge(parts_ready, g)
                    split(nc, S, lambda r: parts[:, b:b + n, r, :], both[:, :, 0:D], rest[:, 0:n, :]
                          ).then_inc(parts_ready, 1)
                dve.wait_ge(parts_ready, len(groups))
                for b in range(NB):
                    r = sumr[b % 2][:]
                    dve.wait_ge(sums, b + 1)
                    if b >= 1:
                        dve.wait_ge(kept, b)
                    S(v.reduce_sum(r, psT[b % 2][0:B, 0:3 * D].rearrange("p (r d) -> p d r", r=3), X))
                    S.wait()
                    for i in range(2):
                        S(v.scalar_tensor_tensor(r, ge[:, i, :], we[:, b, i:i + 1], r, ALU.mult, ALU.add))
                        S.wait()
                    S(v.scalar_tensor_tensor(r, r, 0.0, base[:, b, :], ALU.max, ALU.add))
                    S.wait()
                    v.scalar_tensor_tensor(t.xa[:, b, :], r, 0.0, t.xb[:, b, :], ALU.max, ALU.add).then_inc(kept, 1)
                    if b >= 1:
                        S(v.bn_stats(bn[:, b - 1, :], t.xa[:, b - 1, :]))
                dve.wait_ge(kept, NB)
                normalize(nc, dve, S, t.xa, bn, mv, std, rstd, t.xb[:], var, root, range(NB - 1, NB))


def polynomial_layer(nc, a, c, t, out):
    with ExitStack() as s:
        sb = lambda n, sh, d: s.enter_context(nc.sbuf_tensor(f"L3_{n}", sh, d))
        sem = lambda n: s.enter_context(nc.semaphore(f"L3_{n}"))
        pb = lambda n: s.enter_context(nc.psum_tensor(f"L3_{n}", [P, 512], F32))
        parts = [sb(f"parts{i}", [B, NB, 3, D], BF16) for i in range(2)]
        x3T = sb("x3T", [D, V], F32)
        Wk = sb("Wk", [D, KMAX + 1, D], F32)
        wk = [sb(f"wk{i}", [D, D], F32) for i in range(2)]
        bias = sb("bias", [B, D], F32)
        some, root_deg, dinv = sb("some", [B, NB], F32), sb("root_deg", [B, NB], F32), sb("dinv", [B, NB], F32)
        safe = sb("safe", [B, NB], F32)
        sumr, diff, rest = ([sb(f"{n}{i}", [B, D], F32) for i in range(2)] for n in ("sumr", "diff", "rest"))
        old = lambda lo, hi: t.src1[0:B, lo * NB:hi * NB].rearrange("p (b s) -> p b s", s=hi - lo)
        bn, mv = old(0, 6), old(6, 8)
        std, rstd = t.src1[0:B, 8 * NB:9 * NB], t.src1[0:B, 9 * NB:10 * NB]
        scaled = t.src1[0:B, 10 * NB:10 * NB + 4 * D].rearrange("p (b d) -> p b d", d=D)
        psT, psA, psY = ([pb(f"{n}{i}") for i in range(2)] for n in ("psT", "psA", "psY"))
        (w_in, turned, x3t, wk_set, wk_staged, deg_set, droot, y_ps, parts_ready, sums, bank_free, var, root, step, stored
         ) = map(sem, ("weights_in", "x3_turned", "x3T_ready", "Wk_scaled", "wk_staged", "deg_set", "deg_root", "y_product",
                       "parts_ready", "sums_ready", "bank_read", "var_ready", "std_ready", "poly_step", "out_stored"))
        groups = [range(g, min(g + 4, NB)) for g in range(0, NB, 4)]
        y = t.xa
        PER = 6
        with nc.Block() as block:
            @block.sync
            def _(sp):
                sp.dma_start(Wk[:], a["L3_gnn_W"].rearrange("k i o -> i k o")).then_inc(w_in, 16)
                sp.dma_start(bias[:], a["L3_gnn_bias"].partition_broadcast(B)).then_inc(w_in, 16)

            @block.scalar
            def _(act):
                act.wait_ge(w_in, 32)
                inv = 1.0
                for k in range(1, KMAX + 1):
                    inv /= k
                    last = nc.scalar.mul(Wk[:, k, :], Wk[:, k, :], inv)
                last.then_inc(wk_set, 1)
                act.wait_ge(deg_set, 1)
                nc.scalar.activation(root_deg[:], safe[:], ACT.Sqrt).then_inc(droot, 1)
                for g, blocks in enumerate(groups):
                    n = len(blocks)
                    act.wait_ge(turned, g + 1)
                    nc.scalar.copy(x3T[:, 4 * g * B:(4 * g + n) * B].rearrange("p (b n) -> p b n", n=B),
                                   psT[g % 2][0:D, 0:n * P].rearrange("p (b n) -> p b n", n=P)[:, :, 0:B]
                                   ).then_inc(x3t, 1)

                def stage(it, k):
                    act.wait_ge(sums, NB * it + 1)
                    nc.scalar.copy(wk[k][:], Wk[:, bass.ds(KMAX - 1 - it, 1), :].rearrange("p o d -> p (o d)")
                                   ).then_inc(wk_staged, 1)

                act.wait_ge(wk_set, 1)
                with act.Fori(0, KMAX, 2) as it:
                    it = it.with_bounds(min_val=0, max_val=KMAX - 2)
                    stage(it, 0)
                    stage((it + 1).with_bounds(min_val=1, max_val=KMAX - 1), 1)
                roots(nc, act, c, mv, std, var, root)

            @block.tensor
            def _(pe):
                for g, blocks in enumerate(groups):
                    if g >= 2:
                        pe.wait_ge(x3t, g - 1)
                    for i, b in enumerate(blocks):
                        last = nc.tensor.transpose(psT[g % 2][0:D, i * P:i * P + B], t.xb[:, b, :], c.ident[0:B, 0:B])
                    last.then_inc(turned, 1)
                pe.wait_ge(wk_set, 1)
                for g, blocks in enumerate(groups):
                    pe.wait_ge(x3t, g + 1)
                    if g >= 2:
                        pe.wait_ge(parts_ready, 4 * (g - 1))
                    for i, b in enumerate(blocks):
                        last = nc.tensor.matmul(psY[g % 2][0:B, i * D:(i + 1) * D], x3T[:, b * B:(b + 1) * B],
                                                Wk[:, KMAX, :], start=True, stop=True)
                    last.then_inc(y_ps, 1)

                pe.sem_inc(sums, 1)

                def term(it, src):
                    for b in range(NB):
                        ps = psA[(NB * src + b) % 2]
                        pe.wait_ge(bank_free, NB * it + b + 1)
                        if b == 0:
                            pe.wait_ge(wk_staged, it + 1)
                        nc.tensor.matmul(ps[0:B, 256:256 + D], x3T[:, b * B:(b + 1) * B], wk[src][:], start=True,
                                         stop=True)
                        for kb in range(NB):
                            if b == 0:
                                pe.wait_ge(parts_ready, NB * it + kb + 1)
                            last = nc.tensor.matmul(ps[:, 0:3 * D], t.mat[0:B, kb, b * B:b * B + P],
                                                    parts[src][:, kb].rearrange("p r d -> p (r d)"),
                                                    start=(kb == 0), stop=(kb == NB - 1))
                        last.then_inc(sums, 1)

                with pe.Fori(0, KMAX, 2) as it:
                    it = it.with_bounds(min_val=0, max_val=KMAX - 2)
                    term(it, 0)
                    term((it + 1).with_bounds(min_val=1, max_val=KMAX - 1), 1)

            @block.vector
            def _(dve):
                S = Steps(dve, step)
                v = nc.vector
                dve.sem_inc(bank_free, 2)
                deg = t.wsum[:, :, WP - 1]
                S(v.tensor_scalar(some[:], deg, 0.0, None, ALU.is_gt))
                v.tensor_scalar(safe[:], deg, 1.0, None, ALU.max).then_inc(deg_set, 1)
                dve.wait_ge(droot, 1)
                S(v.reciprocal(dinv[:], root_deg[:]))
                S.wait()
                S(v.tensor_tensor(dinv[:], dinv[:], some[:], ALU.mult))
                dve.wait_ge(w_in, 32)
                dve.wait_ge(turned, len(groups))
                S(v.tensor_tensor(t.xb[:], t.xb[:], bias[:].unsqueeze(1).broadcast_to([B, NB, D]), ALU.add))
                S.wait()
                for g, blocks in enumerate(groups):
                    n, b = len(blocks), blocks[0]
                    dve.wait_ge(y_ps, g + 1)
                    if g:
                        dve.wait_ge(parts_ready, 4 * g)
                    S(v.tensor_copy(y[:, b:b + n, :], psY[g % 2][0:B, 0:n * D].rearrange("p (b d) -> p b d", d=D)))
                    S.wait()
                    S(v.tensor_tensor(scaled[:, 0:n, :], y[:, b:b + n, :],
                                      dinv[:, b:b + n].unsqueeze(2).broadcast_to([B, n, D]), ALU.mult))
                    S.wait()
                    split(nc, S, lambda r: parts[0][:, b:b + n, r, :], scaled[:, 0:n, :], scaled[:, 0:n, :]
                          ).then_inc(parts_ready, n)
                start = S.n

                def term(it, src):
                    S.base, S.n = start + NB * PER * it, 0
                    for b in range(NB):
                        k = b % 2
                        ps, r, d, e = psA[(NB * src + b) % 2], sumr[k][:], diff[k][:], rest[k][:]
                        p = lambda i: parts[1 - src][:, b, i, :]
                        dve.wait_ge(sums, NB * it + b + 2)
                        dve.wait_ge(parts_ready, NB * it + NB + b)
                        S(v.reduce_sum(r, ps[0:B, 0:3 * D].rearrange("p (r d) -> p d r", r=3), X))
                        v.tensor_tensor(d, ps[0:B, 256:256 + D], y[:, b, :], ALU.subtract).then_inc(bank_free, 1)
                        dve.wait_ge(bank_free, NB * it + b + 3)
                        S(v.scalar_tensor_tensor(y[:, b, :], r, dinv[:, b:b + 1], d, ALU.mult, ALU.add))
                        S.wait()
                        S(v.tensor_scalar(p(0), y[:, b, :], dinv[:, b:b + 1], None, ALU.mult))
                        S(v.tensor_scalar(r, y[:, b, :], dinv[:, b:b + 1], None, ALU.mult))
                        S.wait()
                        S(v.tensor_tensor(e, r, p(0), ALU.subtract))
                        S.wait()
                        S(v.tensor_copy(p(1), e))
                        S.wait()
                        v.tensor_tensor(p(2), e, p(1), ALU.subtract).then_inc(parts_ready, 1)
                    assert S.n == NB * PER

                with dve.Fori(0, KMAX, 2) as it:
                    it = it.with_bounds(min_val=0, max_val=KMAX - 2)
                    term(it, 0)
                    term((it + 1).with_bounds(min_val=1, max_val=KMAX - 1), 1)
                S.base, S.n = start + NB * PER * KMAX, 0
                dve.wait_ge(parts_ready, NB * (KMAX + 1))
                S(v.tensor_tensor(y[:], y[:], t.xb[:], ALU.add))
                normalize(nc, dve, S, y, bn, mv, std, rstd, t.xb[:], var, root).then_inc(root, 1)

        with nc.Block() as block:
            @block.sync
            def _(sp):
                sp.dma_start(out.rearrange("(b p) d -> p b d", p=B), t.xb[:]).then_inc(stored, 16)
                sp.wait_ge(stored, 16)


@contextmanager
def cleared_semaphores(nc, prefix, *names):
    sems = [nc.alloc_semaphore(name=f"{prefix}_{n}") for n in names]
    yield sems
    nc.clear_and_free_semaphores(sems)
    nc.all_engine_barrier()


def edge_sums(nc, name, g, table, pick, node, acc):
    C = D + 3
    with ExitStack() as s:
        sb = lambda n, sh, d: s.enter_context(nc.sbuf_tensor(f"{name}_{n}", sh, d))
        pick_i, node_f, rows = sb("pick_i", [B, 1], I32), sb("node_f", [B, 1], F32), sb("rows", [B, C], F32)
        ps = s.enter_context(nc.psum_tensor(f"{name}_ps", [P, 4, 512], F32))
        turn = sb("turn", [B, 1], F32)
        cleared, staged, turns, gathered, hot_ready, product, added = s.enter_context(cleared_semaphores(
            nc, name, "cleared", "staged", "turns", "gathered", "onehot_ready", "product", "added"))
        banks = [range(lo, min(lo + 7, NB)) for lo in range(0, NB, 7)]
        with nc.Block() as block:
            @block.vector
            def _(dve):
                nc.vector.memset(acc[:], 0.0).then_inc(cleared, 1)
                dve.wait_ge(cleared, 1)
                for count in (added, turns):
                    dve.sem_inc(count, 1)
                with dve.Fori(0, CH) as it:
                    dve.wait_ge(added, it + 1)
                    dve.wait_ge(turns, it + 1)
                    nc.vector.tensor_copy(pick_i[:], pick[:, bass.ds(it, 1)])
                    nc.vector.tensor_copy(node_f[:], node[:, bass.ds(it, 1)])
                    nc.vector.tensor_copy(rows[:, D:C], g.own[:, bass.ds(it, 1), :].rearrange("p o k -> p (o k)")
                                          ).then_inc(staged, 1)
                    dve.wait_ge(staged, it + 1)
                    nc.vector.tensor_scalar(g.hot[:], g.nodes[:], node_f[:], None, ALU.is_equal
                                            ).then_inc(hot_ready, 1)
                    dve.wait_ge(product, it + 1)
                    for k, blocks in enumerate(banks):
                        n, v = len(blocks), acc[:, blocks[0]:blocks[-1] + 1, :]
                        last = nc.vector.tensor_tensor(
                            v, v, ps[0:B, k, 0:n * C].rearrange("p (b c) -> p b c", c=C), ALU.add)
                    last.then_inc(added, 1)

            @block.gpsimd
            def _(pool):
                with pool.Fori(0, CH) as it:
                    pool.wait_ge(staged, it + 1)
                    nc.gpsimd.tensor_tensor(turn[:], g.ident[0:B, 0:1], g.ident[0:B, 0:1], ALU.add
                                            ).then_inc(turns, 1)
                    nc.gpsimd.indirect_dma_start(
                        out=rows[:, 0:D], out_offset=None, in_=table,
                        in_offset=bass.IndirectOffsetOnAxis(ap=pick_i[:, 0:1], axis=0)).then_inc(gathered, 16)

            @block.tensor
            def _(pe):
                with pe.Fori(0, CH) as it:
                    pe.wait_ge(gathered, 16 * it + 16)
                    pe.wait_ge(hot_ready, it + 1)
                    for k, blocks in enumerate(banks):
                        for i, b in enumerate(blocks):
                            last = nc.tensor.matmul(ps[0:B, k, i * C:(i + 1) * C], g.hot[:, b * B:(b + 1) * B],
                                                    rows[:], start=True, stop=True)
                    last.then_inc(product, 1)


def edge_network_sums(nc, g, p_table, q_table, wd, eb1, eb2, eW2, acc):
    with ExitStack() as s:
        sb = lambda n, sh, d: s.enter_context(nc.sbuf_tensor(f"EN_{n}", sh, d))
        src_i, dst_i = sb("src_i", [B, 1], I32), sb("dst_i", [B, 1], I32)
        src_f, w1 = sb("src_f", [B, 1], F32), sb("w1", [B, 1], F32)
        pre, q, h1, h1T, z2, h2 = (sb("pre", [B, H], F32), sb("q", [B, H], F32), sb("h1", [B, H], F32),
                                   sb("h1T", [H, B], F32), sb("z2", [B, H], F32), sb("h2", [B, H], F32))
        ps = s.enter_context(nc.psum_tensor("EN_ps", [P, 4, 512], F32))
        ps_t = s.enter_context(nc.psum_tensor("EN_ps_t", [P, 512], F32))
        ps_z = s.enter_context(nc.psum_tensor("EN_ps_z", [P, 512], F32))
        turn = sb("turn", [B, 1], F32)
        (cleared, staged, turns, gathered, summed, h1_ready, turned, h1t_ready, z_ps, z2_ready, h2_ready, hot_ready, product,
         added) = s.enter_context(cleared_semaphores(
             nc, "EN", "cleared", "staged", "turns", "gathered", "summed", "h1_ready", "h1_turned", "h1T_ready", "z_product",
             "z2_ready", "h2_ready", "onehot_ready", "product", "added"))
        banks = [range(lo, min(lo + 8, NB)) for lo in range(0, NB, 8)]
        with nc.Block() as block:
            @block.vector
            def _(dve):
                nc.vector.memset(acc[:], 0.0).then_inc(cleared, 1)
                dve.wait_ge(cleared, 1)
                for count in (added, turns):
                    dve.sem_inc(count, 1)
                with dve.Fori(0, CH) as it:
                    dve.wait_ge(added, 2 * it + 1)
                    dve.wait_ge(turns, it + 1)
                    nc.vector.tensor_copy(src_i[:], g.src_i[:, bass.ds(it, 1)])
                    nc.vector.tensor_copy(dst_i[:], g.dst_i[:, bass.ds(it, 1)])
                    nc.vector.tensor_copy(src_f[:], g.src_f[:, bass.ds(it, 1)])
                    nc.vector.tensor_copy(w1[:], g.w1[:, bass.ds(it, 1)]).then_inc(staged, 1)
                    dve.wait_ge(staged, it + 1)
                    nc.vector.tensor_scalar(g.hot[:], g.nodes[:], src_f[:], None, ALU.is_equal).then_inc(hot_ready, 1)
                    dve.wait_ge(gathered, 32 * it + 32)
                    nc.vector.tensor_tensor(pre[:], pre[:], q[:], ALU.add).then_inc(summed, 1)
                    dve.wait_ge(summed, 3 * it + 1)
                    nc.vector.scalar_tensor_tensor(pre[:], wd[:], w1[:], pre[:], ALU.mult, ALU.add
                                                   ).then_inc(summed, 1)
                    dve.wait_ge(summed, 3 * it + 2)
                    nc.vector.tensor_tensor(pre[:], pre[:], eb1[:], ALU.add).then_inc(summed, 1)
                    dve.wait_ge(z_ps, it + 1)
                    nc.vector.tensor_tensor(z2[:], ps_z[0:B, 0:H], eb2[:], ALU.add).then_inc(z2_ready, 1)
                    for half in range(2):
                        dve.wait_ge(product, 2 * it + half + 1)
                        for k, blocks in enumerate(banks):
                            n, v = len(blocks), acc[:, blocks[0]:blocks[-1] + 1, half * D:(half + 1) * D]
                            last = nc.vector.tensor_tensor(
                                v, v, ps[0:B, k, 0:n * D].rearrange("p (b c) -> p b c", c=D), ALU.add)
                        last.then_inc(added, 1)

            @block.gpsimd
            def _(pool):
                with pool.Fori(0, CH) as it:
                    pool.wait_ge(staged, it + 1)
                    nc.gpsimd.tensor_tensor(turn[:], g.ident[0:B, 0:1], g.ident[0:B, 0:1], ALU.add
                                            ).then_inc(turns, 1)
                    nc.gpsimd.indirect_dma_start(
                        out=pre[:], out_offset=None, in_=p_table,
                        in_offset=bass.IndirectOffsetOnAxis(ap=src_i[:, 0:1], axis=0)).then_inc(gathered, 16)
                    nc.gpsimd.indirect_dma_start(
                        out=q[:], out_offset=None, in_=q_table,
                        in_offset=bass.IndirectOffsetOnAxis(ap=dst_i[:, 0:1], axis=0)).then_inc(gathered, 16)

            @block.scalar
            def _(act):
                with act.Fori(0, CH) as it:
                    act.wait_ge(summed, 3 * it + 3)
                    nc.scalar.activation(h1[:], pre[:], ACT.Silu).then_inc(h1_ready, 1)
                    act.wait_ge(turned, it + 1)
                    nc.scalar.copy(h1T[:], ps_t[:, 0:B]).then_inc(h1t_ready, 1)
                    act.wait_ge(z2_ready, it + 1)
                    nc.scalar.activation(h2[:], z2[:], ACT.Silu).then_inc(h2_ready, 1)

            @block.tensor
            def _(pe):
                with pe.Fori(0, CH) as it:
                    pe.wait_ge(h1_ready, it + 1)
                    nc.tensor.transpose(ps_t[:, 0:B], h1[:], g.ident[0:B, 0:B]).then_inc(turned, 1)
                    pe.wait_ge(h1t_ready, it + 1)
                    nc.tensor.matmul(ps_z[0:B, 0:H], h1T[:], eW2[:], start=True, stop=True).then_inc(z_ps, 1)
                    pe.wait_ge(h2_ready, it + 1)
                    pe.wait_ge(hot_ready, it + 1)
                    for half in range(2):
                        if half:
                            pe.wait_ge(added, 2 * it + 2)
                        for k, blocks in enumerate(banks):
                            for i, b in enumerate(blocks):
                                last = nc.tensor.matmul(ps[0:B, k, i * D:(i + 1) * D], g.hot[:, b * B:(b + 1) * B],
                                                        h2[:, half * D:(half + 1) * D], start=True, stop=True)
                        last.then_inc(product, 1)


def node_product(nc, name, g, terms, out, bias):
    with ExitStack() as s:
        N = out.shape[2]
        staged_rows = [s.enter_context(nc.sbuf_tensor(f"{name}_rows{i}", [B, w.shape[0]], F32))
                       for i, (_, w) in enumerate(terms)]
        rowsT = [s.enter_context(nc.sbuf_tensor(f"{name}_rowsT{i}", [w.shape[0], B], F32))
                 for i, (_, w) in enumerate(terms)]
        ps_t = [s.enter_context(nc.psum_tensor(f"{name}_ps_t{i}", [P, 512], F32)) for i in range(len(terms))]
        ps = s.enter_context(nc.psum_tensor(f"{name}_ps", [P, 512], F32))
        staged, turned, rows_t, product, kept = s.enter_context(cleared_semaphores(
            nc, name, "staged", "turned", "rowsT_ready", "product", "kept"))
        with nc.Block() as block:
            @block.vector
            def _(dve):
                dve.sem_inc(kept, 1)
                with dve.Fori(0, NB) as b:
                    dve.wait_ge(kept, b + 1)
                    for (rows, w), st in zip(terms, staged_rows):
                        last = nc.vector.tensor_copy(
                            st[:], rows[:, bass.ds(b, 1), 0:w.shape[0]].rearrange("p o d -> p (o d)"))
                    last.then_inc(staged, 1)
                    dve.wait_ge(product, b + 1)
                    nc.vector.tensor_tensor(out[:, bass.ds(b, 1), :].rearrange("p o d -> p (o d)"), ps[0:B, 0:N],
                                            bias, ALU.add).then_inc(kept, 1)

            @block.tensor
            def _(pe):
                with pe.Fori(0, NB) as b:
                    pe.wait_ge(staged, b + 1)
                    for st, pt in zip(staged_rows, ps_t):
                        last = nc.tensor.matmul(pt[0:st.shape[1], 0:B], st[:], g.ident[0:B, 0:B], start=True,
                                                stop=True)
                    last.then_inc(turned, 1)
                    pe.wait_ge(rows_t, b + 1)
                    for i, (_, w) in enumerate(terms):
                        last = nc.tensor.matmul(ps[0:B, 0:N], rowsT[i][:], w, start=(i == 0),
                                                stop=(i == len(terms) - 1))
                    last.then_inc(product, 1)

            @block.scalar
            def _(act):
                with act.Fori(0, NB) as b:
                    act.wait_ge(turned, b + 1)
                    for rt, pt in zip(rowsT, ps_t):
                        last = nc.scalar.copy(rt[:], pt[0:rt.shape[0], 0:B])
                    last.then_inc(rows_t, 1)


def store_rows(nc, name, table, rows):
    with cleared_semaphores(nc, name, "stored") as (stored,), nc.Block() as block:
        @block.sync
        def _(sp):
            sp.dma_start(table.rearrange("(b p) d -> p b d", p=B), rows).then_inc(stored, 16)
            sp.wait_ge(stored, 16)


def add_and_normalize(nc, name, c, g, x, y):
    with ExitStack() as s:
        step, var, root = s.enter_context(cleared_semaphores(nc, name, "norm_step", "var_ready", "std_ready"))
        with nc.Block() as block:
            @block.vector
            def _(dve):
                S = Steps(dve, step)
                S(nc.vector.tensor_tensor(y[:], y[:], x[:], ALU.add))
                normalize(nc, dve, S, y, g.bn, g.mv, g.std, g.rstd, x[:], var, root).then_inc(root, 1)

            @block.scalar
            def _(act):
                roots(nc, act, c, g.mv, g.std, var, root)


def any_order(nc, a, c, x, y, out):
    with ExitStack() as s:
        sb = lambda n, sh, d: s.enter_context(nc.sbuf_tensor(f"any_{n}", sh, d))
        g = Bag()
        g.src_i, g.dst_i = sb("src_i", [B, CH], I32), sb("dst_i", [B, CH], I32)
        g.src_f, g.dst_f = sb("src_f", [B, CH], F32), sb("dst_f", [B, CH], F32)
        g.w1, g.own, w = sb("w1", [B, CH], F32), sb("own", [B, CH, 3], F32), sb("w", [B, 2 * CH], F32)
        edges = sb("edges", [B, 2 * CH], I32)
        g.nodes, g.hot = sb("nodes", [B, V], F32), sb("hot", [B, V], F32)
        g.ident = c.ident
        g.bn, g.mv, g.std, g.rstd = norm_buffers(sb)
        acc = sb("acc", [B, NB, D + 3], F32)
        agg, z, z_out = sb("agg", [B, NB, H], F32), sb("z", [B, NB, H], F32), sb("z_out", [B, NB, H], F32)
        hx, hmu = sb("hx", [B, NB, D], F32), sb("hmu", [B, NB, D], F32)
        nothing = sb("nothing", [B, H], F32)
        nv = sb("nv", [B, NB], F32)
        table = nc.dram_tensor("any_table", [V, D], F32).ap()
        p_table, q_table = nc.dram_tensor("any_p", [V, H], F32).ap(), nc.dram_tensor("any_q", [V, H], F32).ap()
        n0, n1, n2, n3 = "L0_gnn_", "L1_gnn_", "L2_gnn_", "L3_gnn_"
        tables = {}
        for k, ap, sh in (("W1", a[n0 + "W1"], [D, D]), ("W2", a[n0 + "W2"], [D, D]),
                          ("eWa", a[n1 + "eW1"][0:D], [D, H]), ("eWb", a[n1 + "eW1"][D:2 * D], [D, H]),
                          ("eW2", a[n1 + "eW2"], [H, H]), ("nWa", a[n1 + "nW1"][0:D], [D, H]),
                          ("nWb", a[n1 + "nW1"][D:D + H], [H, H]), ("nW2", a[n1 + "nW2"], [H, D]),
                          ("W3T", a["W3T"], [D, D]), ("W4a", a["W4T"][0:D], [D, D]),
                          ("W4b", a["W4T"][D:2 * D], [D, D]), ("W4c", a["W4T"][2 * D:3 * D], [D, D]),
                          ("Wk", a[n3 + "W"].rearrange("k i o -> i k o"), [D, KMAX + 1, D])):
            tables[k] = (sb(k, sh, F32), ap)
        for k, ap, width in (("b1", a[n0 + "b1"], D), ("b2", a[n0 + "b2"], D), ("eb1", a[n1 + "eb1"], H),
                             ("wd", a[n1 + "eW1"][2 * D], H), ("eb2", a[n1 + "eb2"], H), ("nb1", a[n1 + "nb1"], H),
                             ("nb2", a[n1 + "nb2"], D), ("w1r", a[n2 + "W1"].rearrange("d o -> (d o)"), D),
                             ("w2r", a[n2 + "W2"].rearrange("d o -> (d o)"), D), ("bias", a[n3 + "bias"], D)):
            tables[k] = (sb(k, [B, width], F32), ap.partition_broadcast(B))
        tb = lambda k: tables[k][0]
        wide = lambda ap: ap.unsqueeze(1).broadcast_to([B, NB, ap.shape[1]])
        loaded, = s.enter_context(cleared_semaphores(nc, "any", "loaded"))
        LOADS = len(tables) + 4
        with nc.Block() as block:
            @block.sync
            def _(sp):
                sp.dma_start(edges[:], a["edges"].rearrange("(p j) -> p j", p=B)).then_inc(loaded, 16)
                sp.dma_start(w[:], a["weights"].rearrange("(p j) -> p j", p=B)).then_inc(loaded, 16)
                sp.dma_start(x[:], a["x"].rearrange("(b p) d -> p b d", p=B)).then_inc(loaded, 16)
                with nc.allow_non_contiguous_dma("one load of a column"):
                    sp.dma_start(nv[:], a["node_vec1"].rearrange("(b p) -> p b", p=B)).then_inc(loaded, 16)
                for k in tables:
                    sp.dma_start(tables[k][0][:], tables[k][1]).then_inc(loaded, 16)

            @block.gpsimd
            def _(pool):
                nc.gpsimd.iota(g.nodes[:], [[1, V]], base=0, channel_multiplier=0,
                               allow_small_or_imprecise_dtypes=True)
                nc.gpsimd.memset(nothing[:], 0.0)
                nc.gpsimd.memset(g.own[:, :, 2], 1.0)

            @block.vector
            def _(dve):
                v = nc.vector
                dve.wait_ge(loaded, 16 * LOADS)
                e2, w2 = (t[:].rearrange("p (j k) -> p j k", k=2) for t in (edges, w))
                v.tensor_copy(g.src_i[:], e2[:, :, 0])
                v.tensor_copy(g.dst_i[:], e2[:, :, 1])
                v.tensor_copy(g.src_f[:], e2[:, :, 0])
                v.tensor_copy(g.dst_f[:], e2[:, :, 1])
                v.tensor_copy(g.w1[:], w2[:, :, 0])
                v.tensor_scalar(g.own[:, :, 0], w2[:, :, 1], 0.0, None, ALU.max)
                v.tensor_scalar(g.own[:, :, 1], w2[:, :, 1], -1.0, 0.0, ALU.mult, ALU.max)
                inv = 1.0
                for k in range(1, KMAX + 1):
                    inv /= k
                    v.tensor_scalar(tb("Wk")[:, k, :], tb("Wk")[:, k, :], inv, None, ALU.mult)

        store_rows(nc, "any_x", table, x[:])
        edge_sums(nc, "any_L0a", g, table, g.src_i, g.dst_f, acc)
        node_product(nc, "any_L0h", g, [(acc, tb("W1")[:])], y, tb("b1")[:])
        with nc.Block() as block:
            @block.vector
            def _(dve):
                nc.vector.tensor_scalar(y[:], y[:], 0.0, None, ALU.max)
        store_rows(nc, "any_h", table, y[:])
        edge_sums(nc, "any_L0b", g, table, g.src_i, g.dst_f, acc)
        node_product(nc, "any_L0y", g, [(acc, tb("W2")[:])], y, tb("b2")[:])
        add_and_normalize(nc, "any_L0n", c, g, x, y)

        node_product(nc, "any_L1p", g, [(x, tb("eWa")[:])], z, nothing[:])
        store_rows(nc, "any_p", p_table, z[:])
        node_product(nc, "any_L1q", g, [(x, tb("eWb")[:])], z, nothing[:])
        store_rows(nc, "any_q", q_table, z[:])
        edge_network_sums(nc, g, p_table, q_table, tb("wd"), tb("eb1"), tb("eb2"), tb("eW2"), agg)
        node_product(nc, "any_L1z", g, [(x, tb("nWa")[:]), (agg, tb("nWb")[:])], z, tb("nb1")[:])
        with nc.Block() as block:
            @block.scalar
            def _(act):
                nc.scalar.activation(z_out[:], z[:], ACT.Silu)
        node_product(nc, "any_L1y", g, [(z_out, tb("nW2")[:])], y, tb("nb2")[:])
        add_and_normalize(nc, "any_L1n", c, g, x, y)

        he, side = z[:, :, 0:D], z[:, :, D:H]
        node_product(nc, "any_L2m", g, [(x, tb("W3T")[:])], hmu, nothing[:, 0:D])
        w2pm = sb("w2pm", [B, 2, D], F32)
        with cleared_semaphores(nc, "any_L2_step", "step") as (step,), nc.Block() as block:
            @block.vector
            def _(dve):
                S, v = Steps(dve, step), nc.vector
                S(v.tensor_scalar(hmu[:], hmu[:], 0.0, None, ALU.max))
                S(v.tensor_tensor(hx[:], nv[:].unsqueeze(2).broadcast_to([B, NB, D]), wide(tb("w1r")[:]), ALU.mult))
                S(v.tensor_scalar(w2pm[:, 0, :], tb("w2r")[:], 0.0, None, ALU.max))
                S(v.tensor_scalar(w2pm[:, 1, :], tb("w2r")[:], -1.0, 0.0, ALU.mult, ALU.max))
                S.wait()
                v.tensor_scalar(hx[:], hx[:], 0.0, None, ALU.max)
        node_product(nc, "any_L2z", g, [(hx, tb("W4a")[:]), (hmu, tb("W4c")[:])], y, nothing[:, 0:D])
        store_rows(nc, "any_z", table, y[:])
        edge_sums(nc, "any_L2s", g, table, g.dst_i, g.src_f, acc)
        with cleared_semaphores(nc, "any_he_step", "step") as (step,), nc.Block() as block:
            @block.vector
            def _(dve):
                S, v = Steps(dve, step), nc.vector
                for i, to in enumerate((he, side)):
                    S(v.tensor_tensor(to, acc[:, :, D + i:D + i + 1].broadcast_to([B, NB, D]), wide(w2pm[:, i, :]),
                                      ALU.mult))
                S.wait()
                v.tensor_tensor(he, he, side, ALU.add)
        node_product(nc, "any_L2e", g, [(z, tb("W4b")[:])], y, nothing[:, 0:D])
        some, dinv = sb("some", [B, NB], F32), sb("dinv", [B, NB], F32)
        root_deg = sb("root_deg", [B, NB], F32)
        with cleared_semaphores(nc, "any_msg", "step", "root") as (step, droot), nc.Block() as block:
            @block.vector
            def _(dve):
                S, v = Steps(dve, step), nc.vector
                deg = acc[:, :, D + 2]
                S(v.tensor_scalar(dinv[:], deg, 1.0, None, ALU.max))
                S(v.tensor_scalar(some[:], deg, 0.0, None, ALU.is_gt))
                S(v.tensor_tensor(y[:], y[:], acc[:, :, 0:D], ALU.add))
                S.wait()
                S(v.scalar_tensor_tensor(y[:], y[:], 0.0, hx[:], ALU.max, ALU.add))
                S.wait()
                S(v.tensor_tensor(y[:], y[:], hmu[:], ALU.add))
                S.wait()
                S(v.tensor_scalar(y[:], y[:], 0.0, None, ALU.max))
                dve.wait_ge(droot, 1)
                S(v.reciprocal(dinv[:], root_deg[:]))
                S.wait()
                v.tensor_tensor(dinv[:], dinv[:], some[:], ALU.mult)

            @block.scalar
            def _(act):
                act.wait_ge(step, 1)
                nc.scalar.activation(root_deg[:], dinv[:], ACT.Sqrt).then_inc(droot, 1)
        add_and_normalize(nc, "any_L2n", c, g, x, y)

        each = dinv[:].unsqueeze(2).broadcast_to([B, NB, D])
        node_product(nc, "any_L3y", g, [(x, tb("Wk")[:, KMAX, :])], y, nothing[:, 0:D])
        for k in range(KMAX - 1, -1, -1):
            with nc.Block() as block:
                @block.vector
                def _(dve):
                    nc.vector.tensor_tensor(hx[:], y[:], each, ALU.mult)
            store_rows(nc, f"any_y{k}", table, hx[:])
            edge_sums(nc, f"any_L3s{k}", g, table, g.dst_i, g.src_f, acc)
            node_product(nc, f"any_L3x{k}", g, [(x, tb("Wk")[:, k, :])], hmu, nothing[:, 0:D])
            with cleared_semaphores(nc, f"any_term{k}", "step") as (step,), nc.Block() as block:
                @block.vector
                def _(dve):
                    S, v = Steps(dve, step), nc.vector
                    S(v.tensor_tensor(hx[:], acc[:, :, 0:D], each, ALU.mult))
                    S(v.tensor_tensor(hmu[:], hmu[:], y[:], ALU.subtract))
                    S.wait()
                    v.tensor_tensor(y[:], hx[:], hmu[:], ALU.add)
        with nc.Block() as block:
            @block.vector
            def _(dve):
                nc.vector.tensor_tensor(y[:], y[:], wide(tb("bias")[:]), ALU.add)
        add_and_normalize(nc, "any_L3n", c, g, x, y)
        store_rows(nc, "any_out", out, x[:])


class Bag:
    pass


def program(nc, a, out):
    with ExitStack() as ctx:
        sb = lambda n, sh, d: ctx.enter_context(nc.sbuf_tensor(n, sh, d))
        c, t = Bag(), Bag()
        c.ones, c.ones_bf = sb("ones", [P, P], F32), sb("ones_bf", [P, P], BF16)
        c.iota1, c.iota1_bf = sb("iota1", [P, P], F32), sb("iota1_bf", [P, P], BF16)
        c.row1, c.sign = sb("row1", [P, 1], F32), sb("sign", [P, 1], F32)
        c.ident, c.ident_bf = sb("ident", [P, P], F32), sb("ident_bf", [P, P], BF16)
        c.placed_i = sb("placed_i", [1, 1], I32)
        c.eps = sb("eps", [P, 1], F32)
        t.src1 = sb("src1", [P, NT], F32)
        t.wsum = sb("wsum", [B, NB, WP], F32)
        rows_d = nc.dram_tensor("rows_d", [5 * NT * P], BF16).ap()
        m2_d = nc.dram_tensor("m2_d", [NB, B, MW], BF16).ap()
        t.xa, t.xb = sb("xa", [B, NB, D], F32), sb("xb", [B, NB, D], F32)
        with ExitStack() as right:
            t.dst1 = right.enter_context(nc.sbuf_tensor("dst1", [P, NT], F32, side="right"))
            t.wparts = right.enter_context(nc.sbuf_tensor("wparts", [P, NT, WP], BF16, side="right"))
            with nc.sbuf_tensor("slots", [P, REC, NC, NB], BF16) as slots:
                t.slots = slots
                place_edges(nc, a, c, t)
                edge_tables(nc, c, t, slots, rows_d)
            placed = nc.values_load(c.placed_i[0:1, 0:1], min_val=0, max_val=E)
            with nc.If(placed == E):
                with ExitStack() as fast:
                    t.mat = fast.enter_context(nc.sbuf_tensor("mat", [P, NB, MW], BF16))
                    with ExitStack() as early:
                        l0 = l0_inputs(nc, early, t)
                        count_matrices(nc, a, c, t, m2_d, l0)
                        right.close()
                        l1 = l1_weights(nc, early)
                        gcn_layers(nc, a, c, t, l0, l1)
                        edge_network(nc, a, c, t, rows_d, m2_d, l1)
                    message_layer(nc, a, c, t, m2_d)
                    polynomial_layer(nc, a, c, t, out)
            with nc.Else():
                any_order(nc, a, c, t.xb, t.xa, out)


_WEIGHTS = ["L0_gnn_W1", "L0_gnn_b1", "L0_gnn_W2", "L0_gnn_b2", "L1_gnn_eW1", "L1_gnn_eb1", "L1_gnn_eW2", "L1_gnn_eb2",
            "L1_gnn_nW1", "L1_gnn_nb1", "L1_gnn_nW2", "L1_gnn_nb2", "L2_gnn_W1", "L2_gnn_W2", "L3_gnn_W",
            "L3_gnn_bias"]


def kernel(**inputs):
    import concourse.bacc as _bacc
    from concourse.bass_utils import run_bass_kernel_spmd as _run

    put = {k: np.ascontiguousarray(inputs[k]) for k in ["x"] + _WEIGHTS}
    src, dst = np.asarray(inputs["src"]), np.asarray(inputs["dst"])
    put["dst"] = np.ascontiguousarray(dst)
    put["edges"] = np.stack([src, dst], -1).reshape(-1)
    put["weights"] = np.stack([np.asarray(inputs["edge_weight1"])[:, 0], np.asarray(inputs["edge_weight"])],
                              -1).reshape(-1)
    put["node_vec1"] = np.asarray(inputs["node_vec1"]).reshape(-1)
    put["xT"] = np.ascontiguousarray(np.asarray(inputs["x"]).T)
    put["W3T"] = np.ascontiguousarray(np.asarray(inputs["L2_gnn_W3"]).T)
    put["W4T"] = np.ascontiguousarray(np.asarray(inputs["L2_gnn_W4"]).T)

    nc = _bacc.Bacc("TRN2", target_bir_lowering=False, num_devices=1)
    a = {n: nc.dram_tensor(f"in_{n}", v.shape, mybir.dt.from_np(v.dtype), kind="ExternalInput").ap()
         for n, v in put.items()}
    out = nc.dram_tensor("out", [V, D], F32, kind="ExternalOutput").ap()
    program(nc, a, out)
    r = _run(nc, [{f"in_{n}": v for n, v in put.items()}], core_ids=[0])
    return r.results[0]["out"]
```

```python
import math

import numpy as np
import concourse.bass as bass
from concourse import mybir
from contextlib import ExitStack, contextmanager

F32, BF16, I32 = mybir.dt.float32, mybir.dt.bfloat16, mybir.dt.int32
ALU = mybir.AluOpType
ACT = mybir.ActivationFunctionType
X = mybir.AxisListType.X

P = 128
V, E, D, H = 3125, 53125, 64, 128
NB = 25
B = V // NB
CH = E // B
W = 18
WIN = P * W
CAP = P
NC = NB + 1
NT = NB * NC
MW = 3128
KMAX = 10
REC = 8
WP = 7
GROUPS = [list(range(g, min(g + 4, NC))) for g in range(0, NC, 4)]
EPS = 1e-5
HEAD = 15


class Steps:

    def __init__(self, eng, sem):
        self.eng, self.sem, self.base, self.n = eng, sem, 0, 0

    def __call__(self, ins):
        ins.then_inc(self.sem, 1)
        self.n += 1
        return ins

    def wait(self):
        self.eng.wait_ge(self.sem, self.base + self.n)


def in_pairs(eng, count, body, last=0):
    body(0, 0)
    pairs(eng, 1, count - last, body)
    for i in range(count - last, count):
        body(i, i % 2)


def pairs(eng, start, end, body):
    with eng.Fori(start, end, 2) as i:
        i = i.with_bounds(min_val=start, max_val=end - 2)
        body(i, 1)
        body((i + 1).with_bounds(min_val=start + 1, max_val=end - 1), 0)


def place_edges(nc, a, c, t):
    with ExitStack() as s:
        sb = lambda n, sh, d: s.enter_context(nc.sbuf_tensor(n, sh, d))
        sem = lambda n: s.enter_context(nc.semaphore(n))
        dst_i = sb("dst_i", [B, CH], I32)
        dst_f = sb("dst_f", [B, CH], F32)
        below = sb("below", [B, NB, CH], BF16)
        cnt = sb("cnt", [B, NB], F32)
        start_f = sb("start_f", [1, NB], F32)
        start_i = sb("start_i", [1, NB], I32)
        ew = sb("ew", [P, NB, W, 2], I32)
        ww = sb("ww", [P, NB, W, 2], F32)
        bcol = sb("bcol", [P, NB, W], F32)
        bsb = sb("bsb", [P, NB, W], BF16)
        keep = sb("keep", [P, NB * W], BF16)
        tri = sb("tri", [P, P], BF16)
        ps_cnt = s.enter_context(nc.psum_tensor("ps_cnt", [P, 512], F32))
        ps_cross = s.enter_context(nc.psum_tensor("ps_cross", [P, 1024], F32))
        ps_slot = [s.enter_context(nc.psum_tensor(f"ps_slot{i}", [P, 512], F32)) for i in range(2)]

        dst_in, counted, start_sum, start_ready = map(sem, ("dst_in", "counted", "start_sum", "start_ready"))
        edges_in, pool_edges_in, weights_in, consts = map(sem, ("edges_in", "pool_edges_in", "weights_in", "consts"))
        HALF = (NB + 1) // 2

        def load_windows(eng, to, pairs, lo, hi, done):
            with eng.Fori(lo, hi) as b:
                b = b.with_bounds(min_val=lo, max_val=hi - 1)
                first = eng.value_load(start_i[0:1, bass.ds(b, 1)], min_val=0, max_val=E - WIN)
                eng.dma_start(to[:, bass.ds(b, 1), :, :].rearrange("p o j k -> p (o j k)"),
                              pairs[bass.ds(first * 2, WIN * 2)].rearrange("(p j) -> p j", p=P)).then_inc(done, 16)

        with nc.Block() as block:
            @block.sync
            def _(sp):
                sp.dma_start(dst_i[:], a["dst"].rearrange("(p j) -> p j", p=B)).then_inc(dst_in, 16)
                sp.wait_ge(start_ready, 1)
                load_windows(sp, ew, a["edges"], 0, 9, edges_in)
                sp.wait_ge(edges_in, 16 * 18)

            @block.scalar
            def _(act):
                act.wait_ge(start_ready, 1)
                load_windows(act, ew, a["edges"], 9, 18, edges_in)

            @block.gpsimd
            def _(pool):
                nc.gpsimd.memset(c.ones[:], 1.0)
                nc.gpsimd.memset(c.ones_bf[:], 1.0)
                nc.gpsimd.memset(c.eps[:], EPS)
                nc.gpsimd.iota(c.sign[:], [[0, 1]], base=1 + 2 * D, channel_multiplier=-2,
                               allow_small_or_imprecise_dtypes=True)
                nc.gpsimd.iota(c.iota1[:], [[1, P]], base=1, channel_multiplier=0,
                               allow_small_or_imprecise_dtypes=True)
                nc.gpsimd.iota(c.iota1_bf[:], [[1, P]], base=1, channel_multiplier=0,
                               allow_small_or_imprecise_dtypes=True)
                nc.gpsimd.iota(c.row1[:], [[0, 1]], base=1, channel_multiplier=1,
                               allow_small_or_imprecise_dtypes=True)
                nc.gpsimd.iota(bcol[:], [[1, NB], [0, W]], base=0, channel_multiplier=0,
                               allow_small_or_imprecise_dtypes=True)
                nc.gpsimd.iota(bsb[:], [[1, NB], [0, W]], base=1, channel_multiplier=0,
                               allow_small_or_imprecise_dtypes=True)
                nc.gpsimd.memset(keep[:], 1.0).then_inc(consts, 1)
                pool.wait_ge(consts, 1)
                nc.gpsimd.memset(keep[:].rearrange("p (c j) -> p c j", j=W)[:, :, 0:1], 0.0)
                nc.gpsimd.affine_select(out=c.ident[:], in_=c.ones[:], compare_op=ALU.is_equal, fill=0.0, base=0,
                                        pattern=[[-1, P]], channel_multiplier=1)
                nc.gpsimd.affine_select(out=c.ident_bf[:], in_=c.ones_bf[:], compare_op=ALU.is_equal, fill=0.0,
                                        base=0, pattern=[[-1, P]], channel_multiplier=1)
                nc.gpsimd.affine_select(out=tri[:], in_=c.ones_bf[:], compare_op=ALU.is_gt, fill=0.0, base=0,
                                        pattern=[[1, P]], channel_multiplier=-1).then_inc(consts, 1)
                pool.wait_ge(start_ready, 1)
                load_windows(pool, ew, a["edges"], 18, NB, pool_edges_in)
                pool.wait_ge(pool_edges_in, 16 * (NB - 18))

            @block.vector
            def _(dve):
                nc.vector.memset(cnt[:, 0:1], 0.0)
                dve.wait_ge(dst_in, 16)
                nc.vector.tensor_copy(dst_f[:], dst_i[:]).then_inc(counted, 1)
                dve.wait_ge(counted, 1)
                for b in range(1, NB):
                    last = nc.vector.tensor_scalar(below[:, b, :], dst_f[:], float(B * b), 0.0, ALU.is_lt, ALU.add,
                                                   accum_out=cnt[:, b:b + 1])
                last.then_inc(counted, 1)
                dve.wait_ge(start_sum, 1)
                nc.vector.tensor_scalar(start_f[:], ps_cnt[0:1, 0:NB], float(E - WIN), None, ALU.min
                                        ).then_inc(counted, 1)
                dve.wait_ge(counted, 3)
                nc.vector.tensor_copy(start_i[:], start_f[:]).then_inc(start_ready, 1)

            @block.tensor
            def _(pe):
                pe.wait_ge(counted, 2)
                pe.wait_ge(consts, 2)
                nc.tensor.matmul(ps_cnt[0:1, 0:NB], c.ones[0:B, 0:1], cnt[:], start=True, stop=True
                                 ).then_inc(start_sum, 1)

        srcf = sb("srcf", [P, NB, W], F32)
        dstf = sb("dstf", [P, NB, W], F32)
        sblk = sb("sblk", [P, NB, W], F32)
        dblk = sb("dblk", [P, NB, W], F32)
        key = sb("key", [P, NB, W], BF16)
        diag = sb("diag", [P, NB, W], F32)
        rank = sb("rank", [P, NB, W], F32)
        slot = sb("slot", [P, NB, W], F32)
        col = sb("col", [P, NB, W], F32)
        rec = sb("rec", [P, NB, W, REC], BF16)
        cross = sb("cross", [P, NB * NB], F32)
        w_rest = [sb(f"w_rest{i}", [P, NB, W], F32) for i in range(2)]
        tmp = sb("tmp", [P, NB, W], F32)
        oh = sb("oh", [P, NB, NB, W], BF16)
        run = sb("run", [P, NB * NB, W], BF16)
        hit = [sb(f"hit{i}", [P, NB * W], F32) for i in range(2)]
        placed = sb("placed", [P, 1], F32)
        d1, ran, crossed, cross_kept, hit_ready, hit_used, cast, cut = map(sem, (
            "place_step", "ran", "crossed", "cross_kept", "hit_ready", "hit_used", "weights_cast", "weights_cut"))
        with nc.Block() as block:
            @block.vector
            def _(dve):
                D1 = Steps(dve, d1)
                D1(nc.vector.tensor_copy(srcf[:], ew[:, :, :, 0]))
                D1(nc.vector.tensor_copy(dstf[:], ew[:, :, :, 1]))
                D1.wait()
                for blk, node in ((sblk, srcf), (dblk, dstf)):
                    D1(nc.vector.tensor_scalar(blk[:], node[:], 1.0 / B, 0.5 / B - 0.5, ALU.mult, ALU.add))
                D1.wait()
                for big in (3 * 2.0 ** 22, -3 * 2.0 ** 22):
                    for blk in (sblk, dblk):
                        D1(nc.vector.tensor_scalar(blk[:], blk[:], big, None, ALU.add))
                    D1.wait()
                D1(nc.vector.tensor_tensor(tmp[:], dblk[:], bcol[:], ALU.is_equal))
                D1(nc.vector.tensor_tensor(diag[:], sblk[:], dblk[:], ALU.is_equal))
                D1(nc.vector.scalar_tensor_tensor(srcf[:], sblk[:], -float(B), srcf[:], ALU.mult, ALU.add))
                D1(nc.vector.scalar_tensor_tensor(dstf[:], dblk[:], -float(B), dstf[:], ALU.mult, ALU.add))
                D1.wait()
                D1(nc.vector.scalar_tensor_tensor(key[:], sblk[:], 1.0, tmp[:], ALU.add, ALU.mult))
                D1.wait()
                D1(nc.vector.tensor_scalar(rec[:, :, :, 0], srcf[:], 1.0, None, ALU.add))
                D1(nc.vector.tensor_scalar(rec[:, :, :, 1], dstf[:], 1.0, None, ALU.add))
                for b in range(NB):
                    D1(nc.vector.tensor_tensor(oh[:, b], key[:, b:b + 1, :].broadcast_to([P, NB, W]), bsb[:],
                                               ALU.is_equal))
                D1.wait()
                for b in range(NB):
                    last = nc.vector.tensor_tensor_scan(
                        run[:, b * NB:(b + 1) * NB, :].rearrange("p c j -> p (c j)"), keep[:],
                        oh[:, b].rearrange("p c j -> p (c j)"), 0.0, ALU.mult, ALU.add)
                last.then_inc(ran, 1)
                for b in range(NB):
                    h = hit[b % 2]
                    dve.wait_ge(hit_ready, b + 1)
                    D1(nc.vector.tensor_tensor(h[:], h[:], oh[:, b].rearrange("p c j -> p (c j)"), ALU.mult))
                    D1.wait()
                    nc.vector.reduce_sum(rank[:, b, :], h[:].rearrange("p (c j) -> p j c", j=W), X
                                         ).then_inc(hit_used, 1)
                dve.wait_ge(hit_used, NB)
                D1(nc.vector.scalar_tensor_tensor(tmp[:], rank[:], float(CAP), diag[:], ALU.is_gt, ALU.mult))
                D1(nc.vector.tensor_scalar(col[:], sblk[:], -1.0, float(NB), ALU.mult, ALU.add))
                D1.wait()
                D1(nc.vector.scalar_tensor_tensor(slot[:], tmp[:], -float(CAP), rank[:], ALU.mult, ALU.add))
                D1(nc.vector.tensor_tensor(col[:], col[:], tmp[:], ALU.mult))
                D1.wait()
                D1(nc.vector.scalar_tensor_tensor(col[:], col[:], 1.0, sblk[:], ALU.add, ALU.add))
                D1(nc.vector.tensor_scalar(tmp[:], slot[:], 1.0, None, ALU.is_ge))
                D1.wait()
                D1(nc.vector.scalar_tensor_tensor(diag[:], slot[:], float(CAP), tmp[:], ALU.is_le, ALU.mult))
                D1.wait()
                nc.vector.reduce_sum(placed[:], diag[:].rearrange("p b j -> p (b j)"), X).then_inc(ran, 1)

            @block.tensor
            def _(pe):
                pe.wait_ge(ran, 1)
                nc.tensor.matmul(ps_cross[:, 0:500], tri[:], run[:, 0:500, W - 1], start=True, stop=True)
                nc.tensor.matmul(ps_cross[:, 512:637], tri[:], run[:, 500:625, W - 1], start=True, stop=True
                                 ).then_inc(crossed, 1)
                pe.wait_ge(ran, 2)
                nc.tensor.matmul(ps_cnt[0:1, 0:1], placed[:], c.ones[:, 0:1], start=True, stop=True
                                 ).then_inc(crossed, 1)

            @block.gpsimd
            def _(pool):
                pool.wait_ge(cast, 2)
                for i in range(2):
                    nc.gpsimd.tensor_tensor(w_rest[i][:], ww[:, :, :, i], rec[:, :, :, 2 + 3 * i], ALU.subtract
                                            ).then_inc(cut, 1)
                pool.wait_ge(cast, 4)
                for i in range(2):
                    nc.gpsimd.tensor_tensor(rec[:, :, :, 4 + 3 * i], w_rest[i][:], rec[:, :, :, 3 + 3 * i],
                                            ALU.subtract)
                pool.wait_ge(cross_kept, 1)
                for b in range(NB):
                    if b >= 2:
                        pool.wait_ge(hit_used, b - 1)
                    nc.gpsimd.tensor_tensor(
                        hit[b % 2][:].rearrange("p (c j) -> p c j", j=W), run[:, b * NB:(b + 1) * NB, :],
                        cross[:, b * NB:(b + 1) * NB].unsqueeze(2).broadcast_to([P, NB, W]), ALU.add
                        ).then_inc(hit_ready, 1)

            @block.sync
            def _(sp):
                load_windows(sp, ww, a["weights"], 0, HALF, weights_in)
                sp.wait_ge(weights_in, 16 * NB)

            @block.scalar
            def _(act):
                load_windows(act, ww, a["weights"], HALF, NB, weights_in)
                act.wait_ge(weights_in, 16 * NB)
                for i in range(2):
                    nc.scalar.copy(rec[:, :, :, 2 + 3 * i], ww[:, :, :, i]).then_inc(cast, 1)
                act.wait_ge(cut, 2)
                for i in range(2):
                    nc.scalar.copy(rec[:, :, :, 3 + 3 * i], w_rest[i][:]).then_inc(cast, 1)
                act.wait_ge(crossed, 1)
                nc.scalar.copy(cross[:, 0:500], ps_cross[:, 0:500])
                nc.scalar.copy(cross[:, 500:625], ps_cross[:, 512:637]).then_inc(cross_kept, 1)
                act.wait_ge(crossed, 2)
                nc.scalar.copy(c.placed_i[:], ps_cnt[0:1, 0:1])

        HOT = W // 2
        DR = 4
        ohr = sb("ohr", [P, 2, W, P], BF16)
        away = sb("away", [P, W - HOT, P], BF16)
        ohc = sb("ohc", [P, 2, W, NC], BF16)
        rows = sb("rows", [P, 2, W, NC * REC], BF16)
        iotac = sb("iotac", [P, W, NC], F32)
        stage = sb("stage", [P, 2, W], F32)
        srec = sb("srec", [P, 2, W, REC], BF16)
        (iotac_set, stage_set, ohc_ready, dve_ready, pool_ready, away_ready, act_ready, win_used,
         slot_used) = map(sem, (
            "iotac_set", "stage_set", "ohc_ready", "dve_part_ready", "pool_part_ready", "away_ready", "act_part_ready",
            "win_used", "slot_used"))
        with nc.Block() as block:
            @block.gpsimd
            def _(pool):
                nc.gpsimd.iota(iotac[:], [[0, W], [1, NC]], base=1, channel_multiplier=0,
                               allow_small_or_imprecise_dtypes=True).then_inc(iotac_set, 1)

                def body(b, k):
                    pool.wait_ge(ohc_ready, b + 1)
                    nc.gpsimd.tensor_tensor(
                        rows[:, k].rearrange("p j (c r) -> p j c r", r=REC)[:, :, :, DR:REC],
                        ohc[:, k].unsqueeze(3).broadcast_to([P, W, NC, REC - DR]),
                        srec[:, k, :, DR:REC].unsqueeze(2).broadcast_to([P, W, NC, REC - DR]), ALU.mult
                        ).then_inc(pool_ready, 1)
                in_pairs(pool, NB, body)

            @block.vector
            def _(dve):
                dve.wait_ge(iotac_set, 1)

                def body(b, k):
                    dve.wait_ge(win_used, b + 1)
                    nc.vector.tensor_copy(stage[:, k, :], slot[:, bass.ds(b, 1), :].rearrange("p o j -> p (o j)"))
                    nc.vector.tensor_copy(srec[:, k], rec[:, bass.ds(b, 1), :, :].rearrange("p o j r -> p (o j) r")
                                          ).then_inc(stage_set, 1)
                    nc.vector.tensor_tensor(
                        ohc[:, k], col[:, bass.ds(b, 1), :].rearrange("p o j -> p j o").broadcast_to([P, W, NC]),
                        iotac[:], ALU.is_equal).then_inc(ohc_ready, 1)
                    dve.wait_ge(stage_set, b + 1)
                    nc.vector.tensor_tensor(
                        ohr[:, k, 0:HOT, :], c.iota1_bf[:].unsqueeze(1).broadcast_to([P, HOT, P]),
                        stage[:, k, 0:HOT].unsqueeze(2).broadcast_to([P, HOT, P]), ALU.is_equal)
                    dve.wait_ge(ohc_ready, b + 1)
                    nc.vector.tensor_tensor(
                        rows[:, k].rearrange("p j (c r) -> p j c r", r=REC)[:, :, :, 0:DR],
                        ohc[:, k].unsqueeze(3).broadcast_to([P, W, NC, DR]),
                        srec[:, k, :, 0:DR].unsqueeze(2).broadcast_to([P, W, NC, DR]), ALU.mult
                        ).then_inc(dve_ready, 1)
                in_pairs(dve, NB, body)

            @block.tensor
            def _(pe):
                pe.sem_inc(win_used, 2)

                def body(b, k):
                    pe.wait_ge(dve_ready, b + 1)
                    pe.wait_ge(pool_ready, b + 1)
                    pe.wait_ge(act_ready, b + 1)
                    pe.wait_ge(slot_used, b + 1)
                    for j in range(W):
                        last = nc.tensor.matmul(ps_slot[k][:, 0:NC * REC], ohr[:, k, j, :], rows[:, k, j, :],
                                                start=(j == 0), stop=(j == W - 1))
                    last.then_inc(win_used, 1)
                in_pairs(pe, NB, body)

            @block.scalar
            def _(act):
                act.sem_inc(slot_used, 2)

                def keep_slots(b, k):
                    act.wait_ge(win_used, b + 3)
                    nc.scalar.copy(t.slots[:, :, :, bass.ds(b, 1)].rearrange("p r c o -> p r (c o)"),
                                   ps_slot[k][:, 0:NC * REC].rearrange("p (c r) -> p r c", r=REC)
                                   ).then_inc(slot_used, 1)

                def body(b, k):
                    act.wait_ge(stage_set, b + 1)
                    act.wait_ge(act_ready, b)
                    for j in range(HOT, W):
                        last = nc.scalar.activation(away[:, j - HOT, :], c.iota1_bf[:], ACT.Abs,
                                                    bias=stage[:, k, j:j + 1], scale=-1.0)
                    last.then_inc(away_ready, 1)
                    act.wait_ge(away_ready, b + 1)
                    nc.scalar.activation(ohr[:, k, HOT:W, :], away[:], ACT.Relu, bias=1.0, scale=-1.0
                                         ).then_inc(act_ready, 1)
                    if not (isinstance(b, int) and b == 0):
                        keep_slots(b - 1, 1 - k)
                in_pairs(act, NB, body)
                keep_slots(NB - 1, 0)


def edge_tables(nc, c, t, slots, rows_d):
    with ExitStack() as s:
        sb = lambda n, sh, d: s.enter_context(nc.sbuf_tensor(n, sh, d))
        sem = lambda n: s.enter_context(nc.semaphore(n))
        minus = sb("minus", [P, NT], F32)
        row_sb = sb("row_sb", [B, NC, P], BF16)
        ps = [s.enter_context(nc.psum_tensor(f"ps_row{i}", [P, 8, P], BF16)) for i in range(4)]
        done, rowed, row_out, rows_out = map(sem, ("table_step", "rowed", "row_out", "rows_out"))
        wv = lambda k: t.wparts[:, :, k]
        field = [slots[:, r].rearrange("p c b -> p (c b)") for r in range(REC)]
        w = field[5:8]
        with nc.Block() as block:
            @block.vector
            def _(dve):
                v = nc.vector
                v.tensor_copy(t.src1[:], field[0])
                v.tensor_copy(t.dst1[:], field[1])
                v.tensor_scalar(minus[:], w[0], 0.0, -1.0, ALU.is_lt, ALU.mult).then_inc(done, 1)
                for r in range(3):
                    v.scalar_tensor_tensor(wv(r), w[0], 0.0, w[r], ALU.is_gt, ALU.mult)
                dve.wait_ge(done, 1)
                for r in range(3):
                    v.tensor_tensor(wv(3 + r), minus[:], w[r], ALU.mult)

            @block.gpsimd
            def _(pool):
                nc.gpsimd.memset(wv(6), 1.0)

            @block.tensor
            def _(pe):
                flat = slots[:, 0:5].rearrange("p r c b -> p (r c b)")
                for i in range(NC):
                    last = nc.tensor.transpose(ps[i // 8][0:B, i % 8, :], flat[:, i * B:(i + 1) * B], c.ident_bf[:])
                    if i % 8 == 7 or i == NC - 1:
                        last.then_inc(rowed, 1)

            @block.scalar
            def _(act):
                for g in range(4):
                    n = min(8, NC - 8 * g)
                    act.wait_ge(rowed, g + 1)
                    nc.scalar.copy(row_sb[:, 8 * g:8 * g + n, :], ps[g][0:B, 0:n, :]).then_inc(row_out, 1)

            @block.sync
            def _(sp):
                sp.wait_ge(row_out, 4)
                sp.dma_start(rows_d.rearrange("(n p r) -> p n r", p=B, r=P), row_sb[:]).then_inc(rows_out, 16)
                sp.wait_ge(rows_out, 16)


def l0_inputs(nc, ctx, t):
    sb = lambda n, sh, d: ctx.enter_context(nc.sbuf_tensor(f"L0_{n}", sh, d))
    sem = lambda n: ctx.enter_context(nc.semaphore(f"L0_{n}"))
    l = Bag()
    l.W1, l.W2, l.b1, l.b2 = sb("W1", [D, D], F32), sb("W2", [D, D], F32), sb("b1", [D, 1], F32), sb("b2", [B, D], F32)
    l.groups = [range(g, min(g + 6, NB)) for g in range(0, NB, 6)]
    xa = t.xa[0:D].rearrange("p b d -> p (b d)")
    l.xT = [xa[:, i * 6 * B:(i + 1) * 6 * B] for i in range(2)]
    l.small_in, l.x_in, l.xT_in = sem("small_in"), sem("x_in"), [sem("xT0_in"), sem("xT1_in")]
    return l


def load_xT(sp, a, l, g):
    lo, hi = l.groups[g][0] * B, (l.groups[g][-1] + 1) * B
    sp.dma_start(l.xT[g % 2][:, 0:hi - lo], a["xT"][:, lo:hi]).then_inc(l.xT_in[g % 2], 16)


def l1_weights(nc, ctx):
    sb = lambda n, sh, d: ctx.enter_context(nc.sbuf_tensor(f"L1_{n}", sh, d))
    w = Bag()
    w.eWa, w.eWb, w.eW2 = sb("eWa", [D, H], F32), sb("eWb", [D, H], F32), sb("eW2", [H, H], F32)
    w.nWa, w.nWb, w.nW2 = sb("nWa", [D, H], F32), sb("nWb", [H, H], F32), sb("nW2", [H, D], F32)
    w.eb1, w.nb1, w.nb2 = sb("eb1", [H, 1], F32), sb("nb1", [H, 1], F32), sb("nb2", [B, D], F32)
    w.wd, w.eb2 = sb("wd", [P, H], F32), sb("eb2", [P, H], F32)
    w.w_in = ctx.enter_context(nc.semaphore("L1_weights_in"))
    return w


def load_l1_weights(sp, a, w):
    n = "L1_gnn_"
    for out_, in_ in ((w.eWa[:], a[n + "eW1"][0:D]), (w.eWb[:], a[n + "eW1"][D:2 * D]), (w.eW2[:], a[n + "eW2"]),
                      (w.nWa[:], a[n + "nW1"][0:D]), (w.nWb[:], a[n + "nW1"][D:D + H]), (w.nW2[:], a[n + "nW2"]),
                      (w.eb1[:], a[n + "eb1"].rearrange("(d o) -> d o", o=1)),
                      (w.nb1[:], a[n + "nb1"].rearrange("(d o) -> d o", o=1)),
                      (w.nb2[:], a[n + "nb2"].partition_broadcast(B)),
                      (w.wd[:], a[n + "eW1"][2 * D].partition_broadcast(P)),
                      (w.eb2[:], a[n + "eb2"].partition_broadcast(P))):
        sp.dma_start(out_, in_).then_inc(w.w_in, 16)


def count_matrices(nc, a, c, t, m2_d, l0):
    with ExitStack() as s:
        sb = lambda n, sh, d: s.enter_context(nc.sbuf_tensor(n, sh, d))
        sem = lambda n: s.enter_context(nc.semaphore(n))
        pb = lambda n: s.enter_context(nc.psum_tensor(n, [P, 512], F32))
        POOL = [2, 6]
        DVE = [g for g in range(len(GROUPS)) if g not in POOL]
        dve_hot = [sb(f"onehot{i}", [P, 4, 2, P], BF16) for i in range(2)]
        pool_hot = [sb(f"pool_onehot{i}", [P, 4, 2, P], BF16) for i in range(2)]
        last_hot = [sb(f"last_onehot{i}", [P, 1, 2, P], BF16) for i in range(2)]
        hot_of = lambda k, g: (pool_hot[POOL.index(g)] if g in POOL else dve_hot[(len(DVE) * k + DVE.index(g)) % 2])
        stage = [sb(f"codes{i}", [P, NC, 2], F32) for i in range(2)]
        panel = [sb(f"panel{i}", [B, MW], BF16) for i in range(2)]
        extra = sb("w_extra", [B, NB, WP], F32)
        A2, A1, WS = ([pb(f"{n}{i}") for i in range(2)] for n in ("ps_dst", "ps_src", "ps_w"))
        NG, ND = len(GROUPS), len(DVE) + 1
        stored = [sem("panel0_stored"), sem("panel1_stored")]
        turn = sb("pool_turn", [P, len(POOL)], F32)
        padded, staged, turns, dve_ready, pool_ready, counted, moved, added, wdone = map(sem, (
            "padded", "codes_staged", "pool_turns", "dve_onehots_ready", "pool_onehots_ready", "counted",
            "blocks_moved", "extras_added", "w_summed"))

        src1 = t.src1[:].rearrange("p (c b) -> p c b", b=NB)
        dst1 = t.dst1[:].rearrange("p (c b) -> p c b", b=NB)
        wparts = t.wparts[:].rearrange("p (c b) k -> p c b k", b=NB)
        with nc.Block() as block:
            @block.gpsimd
            def _(pool):
                nc.gpsimd.memset(t.mat[0:B, :, V:MW], 0.0)
                for k in range(2):
                    nc.gpsimd.memset(panel[k][:, V:MW], 0.0)
                nc.gpsimd.memset(t.wsum[:], 0.0).then_inc(padded, 1)
                pool.sem_inc(pool_ready, 1)

                def body(b, k):
                    pool.wait_ge(staged, b + 1)
                    for j, g in enumerate(POOL):
                        if not (isinstance(b, int) and b == 0):
                            pool.wait_ge(counted, NG * (b - 1) + g + 3)
                        nc.gpsimd.tensor_tensor(turn[:, j:j + 1], c.ones[:, 0:1], c.ones[:, 0:1], ALU.add
                                                ).then_inc(turns, 1)
                        for i, cc in enumerate(t for t in GROUPS[g] if t != NC - 1):
                            for e in range(2):
                                last = nc.gpsimd.tensor_scalar(hot_of(k, g)[:, i, e, :], c.iota1_bf[:],
                                                               stage[k][:, cc, e:e + 1], None, ALU.is_equal)
                        last.then_inc(pool_ready, 1)
                in_pairs(pool, NB, body)

            @block.vector
            def _(dve):
                dve.wait_ge(padded, 1)
                dve.sem_inc(added, 1)

                def add_extras(b, k):
                    dve.wait_ge(moved, NG * b + NG)
                    v = panel[k][:, bass.ds(b * B, B)]
                    nc.vector.tensor_tensor(v, v, WS[k][0:B, 256:256 + B], ALU.add)
                    m = t.mat[0:B, bass.ds(b, 1), bass.ds(b * B, B)].rearrange("p o n -> p (o n)")
                    nc.vector.tensor_tensor(m, m, WS[k][0:B, 384:384 + B], ALU.add)
                    nc.vector.tensor_copy(extra[:, bass.ds(b, 1), :].rearrange("p o w -> p (o w)"),
                                          WS[k][0:B, NB * WP:NC * WP])
                    w = t.wsum[:].rearrange("p b w -> p (b w)")
                    nc.vector.tensor_tensor(w, w, WS[k][0:B, 0:NB * WP], ALU.add).then_inc(added, 1)

                def stage_codes(b, k):
                    if not (isinstance(b, int) and b == 0):
                        dve.wait_ge(dve_ready, ND * (b - 1))
                        dve.wait_ge(pool_ready, len(POOL) * (b - 1) + 1)
                        dve.wait_ge(turns, len(POOL) * (b - 1))
                    nc.vector.tensor_copy(stage[k][:, :, 0], src1[:, :, bass.ds(b, 1)].rearrange("p c o -> p (c o)"))
                    nc.vector.tensor_copy(stage[k][:, :, 1], dst1[:, :, bass.ds(b, 1)].rearrange("p c o -> p (c o)")
                                          ).then_inc(staged, 1)

                def one_hots(hot, k, lo, n):
                    nc.vector.tensor_tensor(
                        hot[:, 0:n], c.iota1_bf[:].unsqueeze(1).unsqueeze(1).broadcast_to([P, n, 2, P]),
                        stage[k][:, lo:lo + n, :].unsqueeze(3).broadcast_to([P, n, 2, P]), ALU.is_equal
                        ).then_inc(dve_ready, 1)

                def body(b, k):
                    for j, g in enumerate(DVE):
                        before = NG * b + DVE[j - 2] - (0 if j >= 2 else NG)
                        if not (isinstance(b, int) and b == 0 and j < 2):
                            dve.wait_ge(counted, before + 3)
                        if j == 0:
                            dve.wait_ge(staged, b + 1)
                        one_hots(hot_of(k, g), k, GROUPS[g][0], len(GROUPS[g]))
                        if j == len(DVE) - 1:
                            one_hots(last_hot[k], k, NC - 1, 1)
                        if j == 2 and not (isinstance(b, int) and b == NB - 1):
                            stage_codes(b + 1, 1 - k)
                        if g == 3 and not (isinstance(b, int) and b == 0):
                            dve.wait_ge(added, b)
                            add_extras(b - 1, 1 - k)
                stage_codes(0, 0)
                in_pairs(dve, NB, body, last=2)
                dve.wait_ge(added, NB)
                add_extras(NB - 1, 0)
                dve.wait_ge(added, NB + 1)
                nc.vector.tensor_tensor(t.wsum[:], t.wsum[:], extra[:], ALU.add).then_inc(wdone, 1)

            @block.tensor
            def _(pe):
                pe.sem_inc(counted, 2)

                def body(b, k):
                    for g, tiles in enumerate(GROUPS):
                        bank = (k * NG + g) % 2
                        if g in POOL:
                            pe.wait_ge(pool_ready, len(POOL) * b + POOL.index(g) + 2)
                        else:
                            pe.wait_ge(dve_ready, ND * b + DVE.index(g) + 1)
                        if not (isinstance(b, int) and b == 0 and g < 2):
                            pe.wait_ge(moved, NG * b + g - 1)
                        if g == 0 and not (isinstance(b, int) and b == 0):
                            pe.wait_ge(added, b)
                        for i, cc in enumerate(tiles):
                            s1, d1 = hot_of(k, g)[:, i, 0, :], hot_of(k, g)[:, i, 1, :]
                            if cc == NC - 1:
                                pe.wait_ge(dve_ready, ND * (b + 1))
                                s1, d1 = last_hot[k][:, 0, 0, :], last_hot[k][:, 0, 1, :]
                            o = slice(i * B, i * B + B)
                            to_dst, to_src = ((A2[bank][:, o], A1[bank][:, o]) if cc < NB else
                                              (WS[k][:, 256:256 + B], WS[k][:, 384:384 + B]))
                            nc.tensor.matmul(to_dst, d1, s1[:, 0:B], start=True, stop=True)
                            nc.tensor.matmul(to_src, s1, d1[:, 0:B], start=True, stop=True)
                            last = nc.tensor.matmul(
                                WS[k][:, cc * WP:(cc + 1) * WP], s1,
                                wparts[:, cc, bass.ds(b, 1), :].rearrange("p o w -> p (o w)"), start=True, stop=True)
                        last.then_inc(counted, 1)
                in_pairs(pe, NB, body)

            @block.scalar
            def _(act):
                act.wait_ge(padded, 1)

                def body(b, k):
                    for g, tiles in enumerate(GROUPS):
                        bank, n = (k * NG + g) % 2, min(len(tiles), NB - tiles[0])
                        act.wait_ge(counted, NG * b + g + 3)
                        if g == 0 and not (isinstance(b, int) and b == 0):
                            act.wait_ge(stored[k], 8 * (b - k) + 16)
                        nc.scalar.copy(panel[k][:, tiles[0] * B:(tiles[0] + n) * B], A2[bank][0:B, 0:n * B])
                        nc.scalar.copy(t.mat[0:B, tiles[0]:tiles[0] + n, bass.ds(b * B, B)],
                                       A1[bank][0:B, 0:n * B].rearrange("p (c n) -> p c n", n=B)).then_inc(moved, 1)
                in_pairs(act, NB, body)

            @block.sync
            def _(sp):
                sp.dma_start(l0.W1[:], a["L0_gnn_W1"]).then_inc(l0.small_in, 16)
                sp.dma_start(l0.W2[:], a["L0_gnn_W2"]).then_inc(l0.small_in, 16)
                sp.dma_start(l0.b1[:], a["L0_gnn_b1"].rearrange("(d o) -> d o", o=1)).then_inc(l0.small_in, 16)
                sp.dma_start(l0.b2[:], a["L0_gnn_b2"].partition_broadcast(B)).then_inc(l0.small_in, 16)
                sp.dma_start(t.xb[:], a["x"].rearrange("(b p) d -> p b d", p=B)).then_inc(l0.x_in, 16)
                for g in range(2):
                    load_xT(sp, a, l0, g)
                for k in range(2):
                    sp.sem_inc(stored[k], 16)

                def body(b, k):
                    sp.wait_ge(added, b + 2)
                    sp.dma_start(m2_d[bass.ds(b, 1)].rearrange("o p n -> p (o n)"), panel[k][:]).then_inc(stored[k], 16)
                in_pairs(sp, NB, body)
                sp.wait_ge(stored[0], 16 * ((NB + 1) // 2) + 16)
                sp.wait_ge(stored[1], 16 * (NB // 2) + 16)


def spread(pe, nc, mat, ob, parts, ps):
    for kb in range(NB):
        last = nc.tensor.matmul(ps[:, 0:3 * D], mat[0:B, kb, ob * B:ob * B + P],
                                parts[:, kb].rearrange("p r d -> p (r d)"), start=(kb == 0), stop=(kb == NB - 1))
    return last


def split(nc, S, parts, src, rest):
    S(nc.vector.tensor_copy(parts(0), src))
    S.wait()
    S(nc.vector.tensor_tensor(rest, src, parts(0), ALU.subtract))
    S.wait()
    S(nc.vector.tensor_copy(parts(1), rest))
    S.wait()
    return nc.vector.tensor_tensor(parts(2), rest, parts(1), ALU.subtract)


def halves(n):
    cuts = [NB * i // n for i in range(n + 1)]
    return [slice(lo, hi) for lo, hi in zip(cuts, cuts[1:])]


def normalize(nc, dve, S, y, stats, mv, std, rstd, out, var_ready, std_ready, counted=0, known=0, chunks=1,
              chunk_done=None):
    S.wait()
    for b in range(counted, NB):
        S(nc.vector.bn_stats(stats[:, b, :], y[:, b, :]))
    S.wait()
    for b in range(known, NB):
        last = nc.vector.bn_aggr(mv[:, b, :], stats[:, b, :])
    last.then_inc(var_ready, 1)
    dve.wait_ge(var_ready, 1)
    S(nc.vector.tensor_tensor(y[:], y[:], mv[:, :, 0:1].broadcast_to([B, NB, D]), ALU.subtract))
    dve.wait_ge(std_ready, 1)
    S(nc.vector.reciprocal(rstd[:], std[:]))
    S.wait()
    for blocks in halves(chunks):
        last = nc.vector.tensor_tensor(out[:, blocks], y[:, blocks], rstd[:, blocks].unsqueeze(2).broadcast_to(
            [B, blocks.stop - blocks.start, D]), ALU.mult)
        if chunk_done:
            last.then_inc(chunk_done, 1)
    return last


def roots(nc, act, c, mv, std, var_ready, std_ready):
    act.wait_ge(var_ready, 1)
    nc.scalar.activation(std[:], mv[:, :, 1], ACT.Sqrt, bias=c.eps[0:B, :]).then_inc(std_ready, 1)


def norm_buffers(sb):
    return (sb("bn", [B, NB, 6], F32), sb("mean_var", [B, NB, 2], F32), sb("std", [B, NB], F32),
            sb("rstd", [B, NB], F32))


def gcn_layers(nc, a, c, t, l0, l1):
    with ExitStack() as s:
        sb = lambda n, sh, d: s.enter_context(nc.sbuf_tensor(f"L0_{n}", sh, d))
        sem = lambda n: s.enter_context(nc.semaphore(f"L0_{n}"))
        pb = lambda n: s.enter_context(nc.psum_tensor(f"L0_{n}", [P, 512], F32))
        parts = [sb(f"gparts{i}", [B, NB, 3, D], BF16) for i in range(2)]
        xT, W1, W2, b1, b2, groups = l0.xT, l0.W1, l0.W2, l0.b1, l0.b2, l0.groups
        small_in, x_in, xT_in = l0.small_in, l0.x_in, l0.xT_in
        rest = sb("rest", [B, 6, D], F32)
        sumr = [sb(f"sumr{i}", [B, D], F32) for i in range(2)]
        hT = [sb(f"hT{i}", [D, B], F32) for i in range(2)]
        bn, mv, std, rstd = norm_buffers(sb)
        psA, psT, psZ = ([pb(f"{n}{i}") for i in range(2)] for n in ("psA", "psT", "psZ"))
        h_ready, parts_ready, sums, summed, turned, relued, z_ready, step, xb, y2, var, root = map(
            sem, ("h_ready", "parts_ready", "sums_ready", "sum_kept",
                  "turned", "hidden_ready", "z_ready", "gcn_step", "x_bias", "rows_done", "var_ready", "std_ready"))
        y = t.xa
        with nc.Block() as block:
            @block.sync
            def _(sp):
                for g in range(2, len(groups)):
                    sp.wait_ge(h_ready, g - 1)
                    load_xT(sp, a, l0, g)
                load_l1_weights(sp, a, l1)

            @block.tensor
            def _(pe):
                pe.wait_ge(small_in, 64)
                for g, blocks in enumerate(groups):
                    pe.wait_ge(xT_in[g % 2], 16 * (g // 2 + 1))
                    if g >= 2:
                        pe.wait_ge(parts_ready, g - 1)
                    for b in blocks:
                        last = nc.tensor.matmul(psZ[g % 2][0:B, (b % 6) * D:(b % 6 + 1) * D],
                                                xT[g % 2][:, b % 6 * B:(b % 6 + 1) * B],
                                                W1[:], start=True, stop=True)
                    last.then_inc(h_ready, 1)
                pe.wait_ge(parts_ready, len(groups))

                def turn(b):
                    pe.wait_ge(summed, b + 1)
                    if b >= 2:
                        pe.wait_ge(relued, b - 1)
                    nc.tensor.transpose(psT[b % 2][0:D, 0:B], sumr[b % 2][:], c.ident[0:B, 0:B]).then_inc(turned, 1)

                def times_w2(b):
                    pe.wait_ge(relued, b + 1)
                    if b >= 2:
                        pe.wait_ge(parts_ready, len(groups) + b - 1)
                    nc.tensor.matmul(psZ[b % 2][0:B, 0:D], hT[b % 2][:], W2[:], start=True, stop=True
                                     ).then_inc(z_ready, 1)

                for b in range(NB):
                    if b >= 2:
                        pe.wait_ge(summed, b - 1)
                    spread(pe, nc, t.mat, b, parts[0], psA[b % 2]).then_inc(sums, 1)
                    if b >= 1:
                        turn(b - 1)
                    if b >= 2:
                        times_w2(b - 2)
                turn(NB - 1)
                times_w2(NB - 2)
                times_w2(NB - 1)
                pe.wait_ge(parts_ready, len(groups) + NB)
                for b in range(NB):
                    if b >= 2:
                        pe.wait_ge(y2, b - 1)
                    spread(pe, nc, t.mat, b, parts[1], psA[b % 2]).then_inc(sums, 1)

            @block.scalar
            def _(act):
                act.wait_ge(small_in, 64)
                for b in range(NB):
                    act.wait_ge(turned, b + 1)
                    if b >= 2:
                        act.wait_ge(z_ready, b - 1)
                    nc.scalar.activation(hT[b % 2][:], psT[b % 2][0:D, 0:B], ACT.Relu, bias=b1[:]).then_inc(relued, 1)
                roots(nc, act, c, mv, std, var, root)

            @block.vector
            def _(dve):
                S = Steps(dve, step)

                def hidden_parts(b):
                    dve.wait_ge(z_ready, b + 1)
                    dve.wait_ge(parts_ready, len(groups) + b)
                    split(nc, S, lambda r: parts[1][:, b, r, :], psZ[b % 2][0:B, 0:D], rest[:, 0, :]
                          ).then_inc(parts_ready, 1)

                dve.wait_ge(small_in, 64)
                dve.wait_ge(x_in, 16)
                nc.vector.tensor_tensor(t.xb[:], t.xb[:], b2[:].unsqueeze(1).broadcast_to([B, NB, D]), ALU.add
                                        ).then_inc(xb, 1)
                for g, blocks in enumerate(groups):
                    n, b = len(blocks), blocks[0]
                    src = psZ[g % 2][0:B, 0:n * D].rearrange("p (b d) -> p b d", d=D)
                    dve.wait_ge(h_ready, g + 1)
                    if g:
                        dve.wait_ge(parts_ready, g)
                    split(nc, S, lambda r: parts[0][:, b:b + n, r, :], src, rest[:, 0:n, :]).then_inc(parts_ready, 1)
                for b in range(NB):
                    dve.wait_ge(sums, b + 1)
                    if b >= 2:
                        dve.wait_ge(turned, b - 1)
                    nc.vector.reduce_sum(sumr[b % 2][:], psA[b % 2][0:B, 0:3 * D].rearrange("p (r d) -> p d r", r=3),
                                         X).then_inc(summed, 1)
                    if b >= 2:
                        hidden_parts(b - 2)
                hidden_parts(NB - 2)
                hidden_parts(NB - 1)
                dve.wait_ge(xb, 1)
                for b in range(NB):
                    k = b % 2
                    dve.wait_ge(sums, NB + b + 1)
                    if b == 0:
                        S.wait()
                        dve.wait_ge(summed, NB)
                    else:
                        dve.wait_ge(y2, b)
                    S(nc.vector.reduce_sum(sumr[k][:], psA[k][0:B, 0:3 * D].rearrange("p (r d) -> p d r", r=3), X))
                    S.wait()
                    nc.vector.tensor_tensor(y[:, b, :], sumr[k][:], t.xb[:, b, :], ALU.add).then_inc(y2, 1)
                    if b >= 1:
                        S(nc.vector.bn_stats(bn[:, b - 1, :], y[:, b - 1, :]))
                    if b >= 2:
                        S(nc.vector.bn_aggr(mv[:, b - 2, :], bn[:, b - 2, :]))
                dve.wait_ge(y2, NB)
                normalize(nc, dve, S, y, bn, mv, std, rstd, t.xb, var, root, NB - 1, NB - 2
                          ).then_inc(xb, 1)


def edge_network(nc, a, c, t, rows_d, m2_d, w, l2):
    HOT = NC * P
    with ExitStack() as s:
        sb = lambda n, sh, d: s.enter_context(nc.sbuf_tensor(f"L1_{n}", sh, d))
        sem = lambda n: s.enter_context(nc.semaphore(f"L1_{n}"))
        pb = lambda n: s.enter_context(nc.psum_tensor(f"L1_{n}", [P, 512], F32))
        room = t.mat[:, HEAD:NB, :].rearrange("p a b -> p (a b)")
        q = room[:, 0:NB * 3 * H].rearrange("p (b r h) -> p b r h", r=3, h=H)
        o = NB * 3 * H
        x1T = room[0:D, o:o + 2 * (NB + 1) * B].bitcast(F32)
        o += 2 * (NB + 1) * B
        srow = [room[:, o + i * HOT:o + (i + 1) * HOT] for i in range(2)]
        drow = [sb(f"drow{i}", [P, HOT], BF16) for i in range(2)]
        eWa, eWb, eW2, nWa, nWb, nW2 = w.eWa, w.eWb, w.eW2, w.nWa, w.nWb, w.nW2
        eb1, nb1, nb2, wd, eb2, w_in = w.eb1, w.nb1, w.nb2, w.wd, w.eb2, w.w_in
        wd3 = sb("wd3", [P, 3, H], BF16)
        o += 2 * HOT
        rest = room[:, o:o + 8 * H].bitcast(F32)
        rest2 = room[:, o + 8 * H:o + 16 * H].bitcast(F32)
        pp = [sb(f"pp{i}", [B, 3, H], BF16) for i in range(2)]
        xs = [sb(f"xs{i}", [D, B], F32) for i in range(2)]
        codes = [sb(f"scodes{i}", [P, NC], F32) for i in range(2)]
        hot = [sb(f"hot{i}", [P, 4, B], BF16) for i in range(2)]
        e1 = [sb("e1", [H, 4 * P], F32), rest2]
        o += 16 * H
        e2 = [sb(f"e2_{i}", [P, 4 * H], F32)[:] for i in range(2)]
        e2 += [room[:, o + i * 8 * H:o + (i + 1) * 8 * H].bitcast(F32) for i in range(2)]
        o += 16 * H
        over = [room[:, o + i * 8 * H:o + (i + 1) * 8 * H].bitcast(F32) for i in range(2)]
        o += 16 * H
        last_part = [room[:, o + i * 4 * H:o + (i + 1) * 4 * H] for i in range(2)]
        high = lambda ap: ap.bitcast(BF16).rearrange("p (n two) -> p n two", two=2)[:, :, 1]
        e2_of = lambda k, g: e2[(0, 1, 2, 0, 1, 2, 0, 1, 2, 3, 0, 1, 2, 3)[k * len(GROUPS) + g]]
        aggs = [sb(f"aggs{i}", [H, B], F32) for i in range(2)]
        z1 = sb("z1", [H, B], F32)
        bn, mv, std, rstd = norm_buffers(sb)
        ps_pre, ps_z2, ps_agg = ([pb(f"{n}{i}") for i in range(2)] for n in ("ps_pre", "ps_z2", "ps_agg"))
        ps_n, ps_p = pb("ps_n"), pb("ps_p")
        turned, x1t_ready, q_ps, q_cast, q_cut, q_done, prep, wd_set, q_tail = map(sem, (
            "x1_turned", "x1T_ready", "q_ready", "q_cast", "q_cut", "q_split", "prep_step", "wd_parts", "q_tail"))
        rows_in = [sem("rows0_in"), sem("rows1_in")]
        rows = rows_d.rearrange("(f c b r) -> f c b r", f=5, c=NC, r=P)
        one = lambda ap: ap.rearrange("o n -> (o n)")

        def load_rows(sp, b, k):
            for buf, f in ((srow, 0), (drow, 1)):
                sp.dma_start(buf[k][0:B, 0:NB * P],
                             one(rows[f, bass.ds(b, 1)].rearrange("o b r -> o (b r)")).partition_broadcast(B)
                             ).then_inc(rows_in[k], 16)
                sp.dma_start(buf[k][0:B, NB * P:HOT],
                             one(rows[f, NB, bass.ds(b, 1)]).partition_broadcast(B)).then_inc(rows_in[k], 16)
            sp.dma_start(drow[k][B:P, 0:NB * P], rows[2:5, bass.ds(b, 1)].rearrange("f o b r -> f (o b r)")
                         ).then_inc(rows_in[k], 16)
            sp.dma_start(drow[k][B:P, NB * P:HOT], rows[2:5, NB, bass.ds(b, 1)].rearrange("f o r -> f (o r)")
                         ).then_inc(rows_in[k], 16)

        NG = len(GROUPS)
        tile_groups = [range(g, min(g + 4, NB)) for g in range(0, NB, 4)]
        q_part = lambda g, r: q[0:B, tile_groups[g][0]:tile_groups[g][-1] + 1, r, :]
        by_block = lambda ap, g: ap[0:B, 0:len(tile_groups[g]) * H].rearrange("p (b h) -> p b h", h=H)
        q_sum = lambda g: by_block(ps_z2[g % 2], g)
        q_rest = lambda g: by_block((rest, rest2)[g % 2], g)
        with nc.Block() as block:
            @block.sync
            def _(sp):
                load_rows(sp, 0, 0)
                load_l2_weights(sp, a, l2)
                sp.wait_ge(wd_set, 1)
                sp.dma_start(q[B:P], wd3[B:P].unsqueeze(1).broadcast_to([3, NB, 3, H])).then_inc(q_tail, 16)
                sp.wait_ge(q_tail, 16)

            @block.gpsimd
            def _(pool):
                nc.gpsimd.memset(x1T[:, NB * B:], 0.0)

            @block.tensor
            def _(pe):
                for g, blocks in enumerate(tile_groups):
                    if g >= 2:
                        pe.wait_ge(x1t_ready, g - 1)
                    for i, b in enumerate(blocks):
                        last = nc.tensor.transpose(ps_pre[g % 2][0:D, i * P:i * P + B], t.xb[:, b, :],
                                                   c.ident[0:B, 0:B])
                    last.then_inc(turned, 1)
                pe.wait_ge(w_in, 16 * 11)
                for g, blocks in enumerate(tile_groups):
                    pe.wait_ge(x1t_ready, g + 1)
                    if g >= 2:
                        pe.wait_ge(q_cut, g - 1)
                    for i, b in enumerate(blocks):
                        last = nc.tensor.matmul(ps_z2[g % 2][0:B, i * H:(i + 1) * H], x1T[:, b * B:(b + 1) * B],
                                                eWb[:], start=True, stop=True)
                    last.then_inc(q_ps, 1)

            @block.scalar
            def _(act):
                for g, blocks in enumerate(tile_groups):
                    act.wait_ge(turned, g + 1)
                    n = len(blocks)
                    nc.scalar.copy(x1T[:, 4 * g * B:(4 * g + n) * B].rearrange("p (b n) -> p b n", n=B),
                                   ps_pre[g % 2][0:D, 0:n * P].rearrange("p (b n) -> p b n", n=P)[:, :, 0:B]
                                   ).then_inc(x1t_ready, 1)
                for g in range(len(tile_groups) + 1):
                    if g < len(tile_groups):
                        act.wait_ge(q_ps, g + 1)
                        nc.scalar.copy(q_part(g, 0), q_sum(g)).then_inc(q_cast, 1)
                    if g >= 1:
                        act.wait_ge(q_cut, g)
                        nc.scalar.copy(q_part(g - 1, 1), q_rest(g - 1)).then_inc(q_cast, 1)

            @block.vector
            def _(dve):
                S = Steps(dve, prep)
                dve.wait_ge(w_in, 16 * 11)
                split(nc, S, lambda r: wd3[:, r, :], wd[:], rest[:, 0:H]).then_inc(wd_set, 1)
                dve.wait_ge(turned, len(tile_groups))
                S(nc.vector.tensor_tensor(t.xb[:], t.xb[:], nb2[:].unsqueeze(1).broadcast_to([B, NB, D]), ALU.add))
                dve.wait_ge(wd_set, 1)
                for g in range(len(tile_groups) + 1):
                    if g < len(tile_groups):
                        dve.wait_ge(q_cast, max(1, 2 * g))
                        if g >= 2:
                            dve.wait_ge(q_done, g - 1)
                        nc.vector.tensor_tensor(q_rest(g), q_sum(g), q_part(g, 0), ALU.subtract).then_inc(q_cut, 1)
                    if g >= 1:
                        dve.wait_ge(q_cast, 2 * g + 1 if g < len(tile_groups) else 2 * g)
                        nc.vector.tensor_tensor(q_part(g - 1, 2), q_rest(g - 1), q_part(g - 1, 1), ALU.subtract
                                                ).then_inc(q_done, 1)

        (panels_in, rows_hot, staged, pre_done, e1_ready, z2_done, biased, silu2_done, cut, e2_ready,
         hot_ready, seg_done, agg_ready, n1_ready, z1_ready, out_ready, out_kept, stats, xs_ready, p_ps, p_ready, var,
         root, step) = map(sem, (
             "panels_in", "rows_hot", "codes_staged", "pre_done", "e1_ready", "z2_done", "biased", "silu2_done",
             "cut", "e2_ready",
             "onehots_ready", "seg_done", "agg_ready", "n1_ready", "z1_ready", "out_ready", "out_kept", "stats_taken",
             "xs_ready", "p_product", "p_ready", "var_ready", "std_ready", "net_step"))
        first = lambda b: isinstance(b, int) and b == 0
        done = lambda b, g: NG * b + g + 1

        def before(b, k, g, lag):
            if g >= lag:
                return (b, k, g - lag),
            return () if first(b) else ((b - 1, 1 - k, NG + g - lag),)

        with nc.Block() as block:
            @block.sync
            def _(sp):
                def body(b, k):
                    if not first(b):
                        sp.wait_ge(pre_done, NG * (b - 1) + 1)
                        load_rows(sp, b, k)
                in_pairs(sp, NB, body)
                sp.wait_ge(panels_in, 16 * HEAD)

            @block.gpsimd
            def _(pool):
                def panel(i):
                    pool.wait_ge(pre_done, NG * i + 1)
                    pool.wait_ge(xs_ready, 1)
                    pool.dma_start(t.mat[0:B, bass.ds(i, 1), :].rearrange("p o n -> p (o n)"),
                                   m2_d[bass.ds(i, 1)].rearrange("o p n -> p (o n)")).then_inc(panels_in, 16)

                def cuts(b, k):
                    for g, tiles in enumerate(GROUPS):
                        bank, n = (k * NG + g) % 2, len(tiles) * H
                        pool.wait_ge(silu2_done, done(b, g))
                        if not (first(b) and g < 2):
                            pool.wait_ge(seg_done, done(b, g) - 2)
                        e = e2_of(k, g)[:, 0:n]
                        nc.gpsimd.tensor_tensor(over[bank][:, 0:n], e, high(e), ALU.subtract).then_inc(cut, 1)

                def with_panel(b, k):
                    panel(b)
                    cuts(b, k)
                with_panel(0, 0)
                pairs(pool, 1, HEAD, with_panel)
                pairs(pool, HEAD, NB, cuts)

            @block.tensor
            def _(pe):
                def product_p(b, k):
                    pe.wait_ge(xs_ready, b + 1)
                    nc.tensor.matmul(ps_p[0:B, 0:H], xs[k][:], eWa[:], start=True, stop=True).then_inc(p_ps, 1)

                def layer1(b, k, g):
                    bank, tiles = (k * NG + g) % 2, GROUPS[g]
                    lo, hi = tiles[0] * P, (tiles[-1] + 1) * P
                    if g == 0:
                        pe.wait_ge(rows_hot, b + 1)
                        pe.wait_ge(p_ready, b + 1)
                    if not (first(b) and g < 2):
                        pe.wait_ge(e1_ready, NG * b + g - 1)
                    for r in range(3):
                        nc.tensor.matmul(ps_pre[bank][:, 0:hi - lo], pp[k][:, r, :], srow[k][0:B, lo:hi],
                                         start=(r == 0), stop=False)
                    for i, cc in enumerate(tiles):
                        for r in range(3):
                            w = (q[:, cc, r, :] if cc < NB else
                                 q[:, bass.ds(b, 1), r, :].rearrange("p o h -> p (o h)"))
                            last = nc.tensor.matmul(ps_pre[bank][:, i * P:(i + 1) * P], w,
                                                    drow[k][:, cc * P:(cc + 1) * P], start=False,
                                                    stop=(r == 2 and cc == tiles[-1]))
                    last.then_inc(pre_done, 1)

                def layer2(b, k, g):
                    bank, tiles = (k * NG + g) % 2, GROUPS[g]
                    pe.wait_ge(e1_ready, NG * b + g + 1)
                    if not (first(b) and g < 2):
                        pe.wait_ge(biased, NG * b + g - 1)
                    for i, cc in enumerate(tiles):
                        last = nc.tensor.matmul(ps_z2[bank][:, i * H:(i + 1) * H], e1[bank][:, i * P:(i + 1) * P],
                                                eW2[:], start=True, stop=True)
                    last.then_inc(z2_done, 1)

                def by_src(b, k, g):
                    bank, tiles = (k * NG + g) % 2, GROUPS[g]
                    pe.wait_ge(e2_ready, NG * b + g + 1)
                    pe.wait_ge(hot_ready, NG * b + g + 2)
                    if g == 0 and not first(b):
                        pe.wait_ge(agg_ready, b)
                    for i, cc in enumerate(tiles):
                        cols = slice(i * H, (i + 1) * H)
                        for r, part in enumerate((high(e2_of(k, g)[:, cols]), high(over[bank][:, cols]),
                                                  last_part[bank][:, cols])):
                            last = nc.tensor.matmul(ps_agg[k][:, 0:B], part, hot[bank][:, i, :],
                                                    start=(cc == 0 and r == 0), stop=(cc == NC - 1 and r == 2))
                    last.then_inc(seg_done, 1)

                def node1(b, k):
                    pe.wait_ge(agg_ready, b + 2)
                    if not first(b):
                        pe.wait_ge(out_kept, b + 1)
                    nc.tensor.matmul(ps_n[:, 0:B], nWa[:], xs[k][:], start=True, stop=False)
                    nc.tensor.matmul(ps_n[:, 0:B], nWb[:], aggs[k][:], start=False, stop=True).then_inc(n1_ready, 1)

                def node2(b, k):
                    pe.wait_ge(z1_ready, b + 1)
                    nc.tensor.matmul(ps_n[0:B, 256:256 + D], z1[:], nW2[:], start=True, stop=True
                                     ).then_inc(out_ready, 1)

                def body(b, k):
                    was = None if first(b) else (b - 1, 1 - k)
                    for g in range(NG):
                        layer1(b, k, g)
                        if was and g == 4:
                            node1(*was)
                        if was and g == 5:
                            node2(*was)
                        for group in before(b, k, g, 1):
                            layer2(*group)
                        for group in before(b, k, g, 3):
                            by_src(*group)
                        if g == 4:
                            product_p(b + 1, 1 - k)
                for count in (pre_done, n1_ready, out_ready):
                    pe.sem_inc(count, 1)
                product_p(0, 0)
                in_pairs(pe, NB, body)
                z = NB - 1
                layer2(z, 0, NG - 1)
                by_src(z, 0, NG - 3)
                by_src(z, 0, NG - 2)
                by_src(z, 0, NG - 1)
                node1(z, 0)
                node2(z, 0)

            @block.scalar
            def _(act):
                def stage_x(b, k):
                    nc.scalar.copy(xs[k][:], x1T[:, bass.ds(b * B, B)]).then_inc(xs_ready, 1)

                def silu1(b, k, g):
                    bank, n = (k * NG + g) % 2, len(GROUPS[g]) * P
                    act.wait_ge(pre_done, NG * b + g + 2)
                    if not (first(b) and g < 2):
                        act.wait_ge(z2_done, NG * b + g - 1)
                    nc.scalar.activation(e1[bank][:, 0:n], ps_pre[bank][:, 0:n], ACT.Silu, bias=eb1[:]
                                         ).then_inc(e1_ready, 1)

                def silu2(b, k, g):
                    e = e2_of(k, g)[:, 0:len(GROUPS[g]) * H]
                    act.wait_ge(biased, done(b, g))
                    nc.scalar.activation(e, e, ACT.Silu).then_inc(silu2_done, 1)

                def keep_agg(b, k):
                    act.wait_ge(seg_done, NG * b + NG)
                    act.wait_ge(n1_ready, b + 1)
                    nc.scalar.copy(aggs[k][:], ps_agg[k][:, 0:B]).then_inc(agg_ready, 1)

                def node_silu(b, k):
                    act.wait_ge(n1_ready, b + 2)
                    if not first(b):
                        act.wait_ge(out_ready, b + 1)
                    nc.scalar.activation(z1[:], ps_n[:, 0:B], ACT.Silu, bias=nb1[:]).then_inc(z1_ready, 1)

                def body(b, k):
                    was = None if first(b) else (b - 1, 1 - k)
                    for g in range(NG):
                        silu1(b, k, g)
                        if was and g == 3:
                            keep_agg(*was)
                        if was and g == 4:
                            node_silu(*was)
                        if g == 4:
                            act.wait_ge(p_ps, b + 1)
                            stage_x(b + 1, 1 - k)
                        for group in before(b, k, g, 1):
                            silu2(*group)
                act.sem_inc(agg_ready, 1)
                stage_x(0, 0)
                in_pairs(act, NB, body)
                z = NB - 1
                silu2(z, 0, NG - 1)
                keep_agg(z, 0)
                node_silu(z, 0)
                roots(nc, act, c, mv, std, var, root)

            @block.vector
            def _(dve):
                S = Steps(dve, step)

                def split_p(b, k):
                    dve.wait_ge(p_ps, b + 1)
                    if not first(b):
                        dve.wait_ge(p_ready, b)
                        dve.wait_ge(pre_done, NG * (b - 1) + 1)
                    dve.wait_ge(step, 3 * b)
                    v = nc.vector
                    v.tensor_copy(pp[k][:, 0, :], ps_p[0:B, 0:H]).then_inc(step, 1)
                    dve.wait_ge(step, 3 * b + 1)
                    v.tensor_tensor(rest[0:B, 0:H], ps_p[0:B, 0:H], pp[k][:, 0, :], ALU.subtract).then_inc(step, 1)
                    dve.wait_ge(step, 3 * b + 2)
                    v.tensor_copy(pp[k][:, 1, :], rest[0:B, 0:H]).then_inc(step, 1)
                    dve.wait_ge(step, 3 * b + 3)
                    v.tensor_tensor(pp[k][:, 2, :], rest[0:B, 0:H], pp[k][:, 1, :], ALU.subtract).then_inc(p_ready, 1)

                def take_stats(b):
                    dve.wait_ge(out_kept, b + 2)
                    row = lambda x: x[:, bass.ds(b, 1), :].rearrange("p o d -> p (o d)")
                    nc.vector.bn_stats(row(bn), row(t.xa)).then_inc(stats, 1)

                def keep_out(b, k):
                    dve.wait_ge(out_ready, b + 2)
                    nc.vector.tensor_tensor(t.xa[:, bass.ds(b, 1), :].rearrange("p o d -> p (o d)"),
                                            ps_n[0:B, 256:256 + D],
                                            t.xb[:, bass.ds(b, 1), :].rearrange("p o d -> p (o d)"), ALU.add
                                            ).then_inc(out_kept, 1)

                def rows_to_hot(b, k):
                    if not first(b):
                        dve.wait_ge(hot_ready, NG * (b - 1) + 1)
                    nc.vector.tensor_copy(codes[k][:, 0:NB], t.src1[:, bass.ds(b * NB, NB)])
                    nc.vector.tensor_copy(codes[k][:, NB:NC], t.src1[:, bass.ds(b + NB * NB, 1)]).then_inc(staged, 1)
                    dve.wait_ge(rows_in[k], 48 * (b - k) + 96)
                    nc.vector.tensor_scalar(srow[k][0:B, :], srow[k][0:B, :], c.row1[0:B, :], None, ALU.is_equal)

                def dst_rows_to_hot(b, k):
                    nc.vector.tensor_scalar(drow[k][0:B, :], drow[k][0:B, :], c.row1[0:B, :], None, ALU.is_equal
                                            ).then_inc(rows_hot, 1)

                def add_bias(b, k, g):
                    bank, tiles = (k * NG + g) % 2, GROUPS[g]
                    dve.wait_ge(z2_done, NG * b + g + 1)
                    if not (first(b) and g < 3):
                        dve.wait_ge(seg_done, done(b, g) - 3)
                    grp = lambda t: t[:, 0:len(tiles) * H].rearrange("p (i h) -> p i h", h=H)
                    nc.vector.tensor_tensor(grp(e2_of(k, g)), grp(ps_z2[bank]),
                                            eb2[:].unsqueeze(1).broadcast_to([P, len(tiles), H]), ALU.add
                                            ).then_inc(biased, 1)

                def third_part(b, k, g):
                    bank, n = (k * NG + g) % 2, len(GROUPS[g]) * H
                    dve.wait_ge(cut, done(b, g))
                    if not (first(b) and g < 2):
                        dve.wait_ge(seg_done, done(b, g) - 2)
                    rest_ = over[bank][:, 0:n]
                    nc.vector.tensor_tensor(last_part[bank][:, 0:n], rest_, high(rest_), ALU.subtract
                                            ).then_inc(e2_ready, 1)

                def src_one_hots(b, k, g):
                    bank = (k * NG + g) % 2
                    if not (first(b) and g < 2):
                        dve.wait_ge(seg_done, done(b, g) - 2)
                    for i, cc in enumerate(GROUPS[g]):
                        last = nc.vector.tensor_scalar(hot[bank][:, i, :], c.iota1_bf[:, 0:B], codes[k][:, cc:cc + 1],
                                                       None, ALU.is_equal)
                    last.then_inc(hot_ready, 1)

                def body(b, k):
                    dve.wait_ge(staged, b + 1)
                    for g in range(NG):
                        if g == 5:
                            split_p(b + 1, 1 - k)
                        for group in before(b, k, g, 1):
                            add_bias(*group)
                        for group in before(b, k, g, 2):
                            third_part(*group)
                            src_one_hots(*group)
                        if g == 5 and not first(b):
                            keep_out(b - 1, 1 - k)
                        if g == 6 and not first(b):
                            take_stats(b - 1)
                        if not (isinstance(b, int) and b == NB - 1):
                            if g == 2:
                                rows_to_hot(b + 1, 1 - k)
                            if g == 3:
                                dst_rows_to_hot(b + 1, 1 - k)
                for count in (hot_ready, out_kept):
                    dve.sem_inc(count, 1)
                rows_to_hot(0, 0)
                dst_rows_to_hot(0, 0)
                split_p(0, 0)
                in_pairs(dve, NB, body, last=2)
                z = NB - 1
                add_bias(z, 0, NG - 1)
                third_part(z, 0, NG - 2)
                src_one_hots(z, 0, NG - 2)
                third_part(z, 0, NG - 1)
                src_one_hots(z, 0, NG - 1)
                keep_out(NB - 1, 0)
                dve.wait_ge(out_kept, NB + 1)
                dve.wait_ge(stats, NB - 1)
                S.n = 3 * (NB + 1)
                normalize(nc, dve, S, t.xa, bn, mv, std, rstd, t.xb, var, root, NB - 1)


def l2_weights(nc, ctx):
    sb = lambda n, sh, d: ctx.enter_context(nc.sbuf_tensor(f"L2_{n}", sh, d))
    w = Bag()
    w.W3T, w.W4a, w.W4b = (sb(n, [D, D], F32) for n in ("W3T", "W4a", "W4b"))
    w.w1c, w.w2c = sb("w1c", [D, 1], F32), sb("w2c", [D, 1], F32)
    w.mix = sb("mix", [D + 2, 2 * D], F32)
    w.w_in = ctx.enter_context(nc.semaphore("L2_weights_in"))
    return w


def load_l2_weights(sp, a, w):
    n = "L2_gnn_"
    for out_, in_ in ((w.W3T[:], a["W3T"]), (w.W4a[:], a["W4T"][0:D]), (w.W4b[:], a["W4T"][D:2 * D]),
                      (w.mix[0:D, 0:D], a["W4T"][2 * D:3 * D]), (w.w1c[:], a[n + "W1"]), (w.w2c[:], a[n + "W2"]),
                      (w.mix[D:D + 2, D:2 * D], a[n + "W1"].rearrange("d o -> (d o)").partition_broadcast(2))):
        sp.dma_start(out_, in_).then_inc(w.w_in, 16)


def message_layer(nc, a, c, t, m2_d, l2):
    with ExitStack() as s:
        sb = lambda n, sh, d: s.enter_context(nc.sbuf_tensor(f"L2_{n}", sh, d))
        sem = lambda n: s.enter_context(nc.semaphore(f"L2_{n}"))
        pb = lambda n: s.enter_context(nc.psum_tensor(f"L2_{n}", [P, 512], F32))
        parts = sb("parts", [B, NB, 3, D], BF16)
        base = sb("base", [B, NB, D], F32)
        x2T = [sb(f"x2T{i}", [D, 4 * B], F32) for i in range(2)]
        feat = sb("feat", [D + 2, V], F32)
        mix, W3T, W4a, W4b, w1c, w2c, w_in = l2.mix, l2.W3T, l2.W4a, l2.W4b, l2.w1c, l2.w2c, l2.w_in
        w1pm, w2pm, ge = sb("w1pm", [D, D + 2], F32), sb("w2pm", [D, 2, B], F32), sb("ge", [B, 2, D], F32)
        we = sb("we", [B, NB, 2], F32)
        sumr = [sb(f"sumr{i}", [B, D], F32) for i in range(2)]
        rest = sb("rest", [B, 4, D], F32)
        old = lambda lo, hi: t.src1[0:B, lo * NB:hi * NB].rearrange("p (b s) -> p b s", s=hi - lo)
        bn, mv = old(0, 6), old(6, 8)
        std, rstd = t.src1[0:B, 8 * NB:9 * NB], t.src1[0:B, 9 * NB:10 * NB]
        psT, psM, psZ = ([pb(f"{n}{i}") for i in range(2)] for n in ("psT", "psM", "psZ"))
        psG = pb("psG")
        (nv_in, tail_in, turned, x2t, hmu_ps, hmut, z_ps, parts_ready, nv_set, w_set, g_ps, g_set, sums,
         kept, var, root, step) = map(sem, (
             "nv_in", "tail_in", "x2_turned", "x2T_ready", "hmu_product", "hmuT_ready", "z_product",
             "parts_ready", "nv_set", "w_parts", "g_product", "g_set", "sums_ready", "rows_kept", "var_ready",
             "std_ready", "msg_step"))
        groups = [range(g, min(g + 4, NB)) for g in range(0, NB, 4)]
        cols = lambda g: slice(groups[g][0] * B, (groups[g][-1] + 1) * B)
        z_of = lambda g: psZ[g % 2][0:B, 0:len(groups[g]) * 2 * D].rearrange("p (b d) -> p b d", d=2 * D)
        with nc.Block() as block:
            @block.sync
            def _(sp):
                sp.dma_start(feat[D:D + 2, :], a["node_vec1"].partition_broadcast(2)).then_inc(nv_in, 16)

            @block.gpsimd
            def _(pool):
                pool.wait_ge(nv_in, 16)
                for g in range(len(groups)):
                    nv = feat[D:D + 2, cols(g)]
                    nc.gpsimd.tensor_scalar(nv, nv, c.sign[D:D + 2, :], 0.0, ALU.mult, ALU.max).then_inc(nv_set, 1)

            @block.scalar
            def _(act):
                for b in range(HEAD, NB):
                    act.dma_start(t.mat[0:B, b, :], m2_d[b]).then_inc(tail_in, 16)
                def keep_columns(g):
                    n = len(groups[g])
                    act.wait_ge(turned, g + 1)
                    if g >= 2:
                        act.wait_ge(hmu_ps, g - 1)
                    nc.scalar.copy(x2T[g % 2][:, 0:n * B].rearrange("p (b n) -> p b n", n=B),
                                   psT[g % 2][0:D, 0:n * P].rearrange("p (b n) -> p b n", n=P)[:, :, 0:B]
                                   ).then_inc(x2t, 1)
                keep_columns(0)
                for g, blocks in enumerate(groups):
                    if g + 1 < len(groups):
                        keep_columns(g + 1)
                    act.wait_ge(hmu_ps, g + 1)
                    nc.scalar.activation(feat[0:D, cols(g)], psM[g % 2][0:D, 0:len(blocks) * B], ACT.Relu
                                         ).then_inc(hmut, 1)
                roots(nc, act, c, mv, std, var, root)

            @block.tensor
            def _(pe):
                def turn(g):
                    if g >= 2:
                        pe.wait_ge(x2t, g - 1)
                    for i, b in enumerate(groups[g]):
                        last = nc.tensor.transpose(psT[g % 2][0:D, i * P:i * P + B], t.xb[:, b, :], c.ident[0:B, 0:B])
                    last.then_inc(turned, 1)
                turn(0)
                pe.wait_ge(w_in, 16 * 7)
                pe.wait_ge(w_set, 1)
                nc.tensor.matmul(psG[0:D + 2, 128:128 + D], w1pm[:], W4a[:], start=True, stop=True)
                for i in range(2):
                    last = nc.tensor.matmul(psG[0:B, i * D:(i + 1) * D], w2pm[:, i, :], W4b[:], start=True,
                                            stop=True)
                last.then_inc(g_ps, 1)

                def hidden(g):
                    n = len(groups[g])
                    pe.wait_ge(x2t, g + 1)
                    if g >= 2:
                        pe.wait_ge(hmut, g - 1)
                    nc.tensor.matmul(psM[g % 2][0:D, 0:n * B], W3T[:], x2T[g % 2][:, 0:n * B], start=True, stop=True
                                     ).then_inc(hmu_ps, 1)
                turn(1)
                hidden(0)
                pe.wait_ge(g_set, 1)
                for g, blocks in enumerate(groups):
                    k, n = g % 2, len(blocks)
                    if g + 2 < len(groups):
                        turn(g + 2)
                    if g + 1 < len(groups):
                        hidden(g + 1)
                    if g >= 2:
                        pe.wait_ge(parts_ready, g - 1)
                    pe.wait_ge(nv_set, g + 1)
                    pe.wait_ge(hmut, g + 1)
                    for i in range(n):
                        b = blocks[i]
                        last = nc.tensor.matmul(psZ[k][0:B, i * 2 * D:(i + 1) * 2 * D], feat[:, b * B:(b + 1) * B],
                                                mix[:], start=True, stop=True)
                    last.then_inc(z_ps, 1)
                pe.wait_ge(tail_in, 16 * (NB - HEAD))
                pe.wait_ge(parts_ready, len(groups))
                for b in range(NB):
                    if b >= 2:
                        pe.wait_ge(kept, b - 1)
                    spread(pe, nc, t.mat, b, parts, psT[b % 2]).then_inc(sums, 1)

            @block.vector
            def _(dve):
                S = Steps(dve, step)
                v = nc.vector
                dve.wait_ge(w_in, 16 * 7)
                S(v.memset(w1pm[:, 0:D], 0.0))
                S(v.tensor_copy(mix[0:D, D:2 * D], c.ident[0:D, 0:D]))
                S(v.tensor_scalar(w1pm[:, D:D + 1], w1c[:], 0.0, None, ALU.max))
                S(v.tensor_scalar(w1pm[:, D + 1:D + 2], w1c[:], -1.0, 0.0, ALU.mult, ALU.max))
                S(v.tensor_scalar(w2pm[:, 0, :], c.ones[0:D, 0:B], w2c[:], 0.0, ALU.mult, ALU.max))
                S(v.tensor_scalar(w2pm[:, 1, :], c.ones[0:D, 0:B], w2c[:], -1.0, ALU.mult, ALU.mult))
                S(v.tensor_scalar(mix[D:D + 2, D:2 * D], mix[D:D + 2, D:2 * D], c.sign[D:D + 2, :], 0.0, ALU.mult,
                                  ALU.max))
                S(v.reduce_sum(we[:], t.wsum[:, :, 0:6].rearrange("p b (s r) -> p b s r", r=3), X))
                S.wait()
                v.tensor_scalar(w2pm[:, 1, :], w2pm[:, 1, :], 0.0, None, ALU.max).then_inc(w_set, 1)
                dve.wait_ge(g_ps, 1)
                v.tensor_copy(ge[:].rearrange("p s d -> p (s d)"), psG[0:B, 0:2 * D])
                v.tensor_copy(mix[D:D + 2, 0:D], psG[D:D + 2, 128:128 + D]).then_inc(g_set, 1)
                for g, blocks in enumerate(groups):
                    n, b = len(blocks), blocks[0]
                    dve.wait_ge(z_ps, g + 1)
                    S(v.tensor_copy(base[:, b:b + n, :], z_of(g)[:, :, D:2 * D]))
                    if g:
                        dve.wait_ge(parts_ready, g)
                    split(nc, S, lambda r: parts[:, b:b + n, r, :], z_of(g)[:, :, 0:D], rest[:, 0:n, :]
                          ).then_inc(parts_ready, 1)
                dve.wait_ge(parts_ready, len(groups))
                for b in range(NB):
                    r = sumr[b % 2][:]
                    dve.wait_ge(sums, b + 1)
                    if b >= 1:
                        dve.wait_ge(kept, b)
                    S(v.reduce_sum(r, psT[b % 2][0:B, 0:3 * D].rearrange("p (r d) -> p d r", r=3), X))
                    S.wait()
                    for i in range(2):
                        S(v.scalar_tensor_tensor(r, ge[:, i, :], we[:, b, i:i + 1], r, ALU.mult, ALU.add))
                        S.wait()
                    S(v.scalar_tensor_tensor(r, r, 0.0, base[:, b, :], ALU.max, ALU.add))
                    S.wait()
                    v.scalar_tensor_tensor(t.xa[:, b, :], r, 0.0, t.xb[:, b, :], ALU.max, ALU.add).then_inc(kept, 1)
                    if b >= 1:
                        S(v.bn_stats(bn[:, b - 1, :], t.xa[:, b - 1, :]))
                    if b >= 2:
                        S(v.bn_aggr(mv[:, b - 2, :], bn[:, b - 2, :]))
                dve.wait_ge(kept, NB)
                normalize(nc, dve, S, t.xa, bn, mv, std, rstd, t.xb, var, root, NB - 1, NB - 2)


def polynomial_layer(nc, a, c, t, out):
    with ExitStack() as s:
        sb = lambda n, sh, d: s.enter_context(nc.sbuf_tensor(f"L3_{n}", sh, d))
        sem = lambda n: s.enter_context(nc.semaphore(f"L3_{n}"))
        pb = lambda n: s.enter_context(nc.psum_tensor(f"L3_{n}", [P, 512], F32))
        parts = [sb(f"parts{i}", [B, NB, 3, D], BF16) for i in range(2)]
        x3T = sb("x3T", [D, V], F32)
        Wk, bias, w_in = sb("Wk", [D, KMAX + 1, D], F32), sb("bias", [B, D], F32), sem("weights_in")
        wk = [sb(f"wk{i}", [D, D], F32) for i in range(2)]
        some, root_deg, dinv = sb("some", [B, NB], F32), sb("root_deg", [B, NB], F32), sb("dinv", [B, NB], F32)
        safe = sb("safe", [B, NB], F32)
        sumr, diff, rest = ([sb(f"{n}{i}", [B, D], F32) for i in range(2)] for n in ("sumr", "diff", "rest"))
        old = lambda lo, hi: t.src1[0:B, lo * NB:hi * NB].rearrange("p (b s) -> p b s", s=hi - lo)
        bn, mv = old(0, 6), old(6, 8)
        std, rstd = t.src1[0:B, 8 * NB:9 * NB], t.src1[0:B, 9 * NB:10 * NB]
        scaled = t.src1[0:B, 10 * NB:10 * NB + 4 * D].rearrange("p (b d) -> p b d", d=D)
        psT, psA, psY = ([pb(f"{n}{i}") for i in range(2)] for n in ("psT", "psA", "psY"))
        (turned, x3t, wk_set, wk_staged, deg_set, droot, y_ps, parts_ready, sums, bank_free, var, root, step, written,
         stored) = map(sem, (
             "x3_turned", "x3T_ready", "Wk_scaled", "wk_staged", "deg_set", "deg_root", "y_product", "parts_ready",
             "sums_ready", "bank_read", "var_ready", "std_ready", "poly_step", "out_written", "out_stored"))
        groups = [range(g, min(g + 4, NB)) for g in range(0, NB, 4)]
        y = t.xa
        PER = 6
        with nc.Block() as block:
            @block.sync
            def _(sp):
                sp.dma_start(Wk[:], a["L3_gnn_W"].rearrange("k i o -> i k o")).then_inc(w_in, 16)
                sp.dma_start(bias[:], a["L3_gnn_bias"].partition_broadcast(B)).then_inc(w_in, 16)
                rows = out.rearrange("(b p) d -> p b d", p=B)
                for i, blocks in enumerate(halves(2)):
                    sp.wait_ge(written, i + 1)
                    sp.dma_start(rows[:, blocks], t.xb[:, blocks]).then_inc(stored, 16)
                sp.wait_ge(stored, 32)

            @block.scalar
            def _(act):
                scale_weights = lambda k: nc.scalar.mul(Wk[:, k, :], Wk[:, k, :], 1.0 / math.factorial(k))
                act.wait_ge(deg_set, 1)
                nc.scalar.activation(root_deg[:], safe[:], ACT.Sqrt).then_inc(droot, 1)
                for g, blocks in enumerate(groups):
                    n = len(blocks)
                    if g == 2:
                        act.wait_ge(w_in, 32)
                        scale_weights(KMAX).then_inc(wk_set, 1)
                    act.wait_ge(turned, g + 1)
                    nc.scalar.copy(x3T[:, 4 * g * B:(4 * g + n) * B].rearrange("p (b n) -> p b n", n=B),
                                   psT[g % 2][0:D, 0:n * P].rearrange("p (b n) -> p b n", n=P)[:, :, 0:B]
                                   ).then_inc(x3t, 1)
                for k in range(1, KMAX):
                    last = scale_weights(k)
                last.then_inc(wk_set, 1)

                def stage(it, k):
                    act.wait_ge(sums, NB * it + 1)
                    nc.scalar.copy(wk[k][:], Wk[:, bass.ds(KMAX - 1 - it, 1), :].rearrange("p o d -> p (o d)")
                                   ).then_inc(wk_staged, 1)

                act.wait_ge(wk_set, 2)
                with act.Fori(0, KMAX, 2) as it:
                    it = it.with_bounds(min_val=0, max_val=KMAX - 2)
                    stage(it, 0)
                    stage((it + 1).with_bounds(min_val=1, max_val=KMAX - 1), 1)
                roots(nc, act, c, mv, std, var, root)

            @block.tensor
            def _(pe):
                def turn(g):
                    if g >= 2:
                        pe.wait_ge(x3t, g - 1)
                    for i, b in enumerate(groups[g]):
                        last = nc.tensor.transpose(psT[g % 2][0:D, i * P:i * P + B], t.xb[:, b, :], c.ident[0:B, 0:B])
                    last.then_inc(turned, 1)
                turn(0)
                turn(1)
                pe.wait_ge(wk_set, 1)
                for g, blocks in enumerate(groups):
                    if g + 2 < len(groups):
                        turn(g + 2)
                    pe.wait_ge(x3t, g + 1)
                    if g >= 2:
                        pe.wait_ge(parts_ready, 4 * (g - 1))
                    for i, b in enumerate(blocks):
                        last = nc.tensor.matmul(psY[g % 2][0:B, i * D:(i + 1) * D], x3T[:, b * B:(b + 1) * B],
                                                Wk[:, KMAX, :], start=True, stop=True)
                    last.then_inc(y_ps, 1)

                pe.sem_inc(sums, 1)

                def term(it, src):
                    for b in range(NB):
                        ps = psA[(NB * src + b) % 2]
                        pe.wait_ge(bank_free, NB * it + b + 1)
                        if b == 0:
                            pe.wait_ge(wk_staged, it + 1)
                        nc.tensor.matmul(ps[0:B, 256:256 + D], x3T[:, b * B:(b + 1) * B], wk[src][:], start=True,
                                         stop=True)
                        for kb in range(NB):
                            if b == 0:
                                pe.wait_ge(parts_ready, NB * it + kb + 1)
                            last = nc.tensor.matmul(ps[:, 0:3 * D], t.mat[0:B, kb, b * B:b * B + P],
                                                    parts[src][:, kb].rearrange("p r d -> p (r d)"),
                                                    start=(kb == 0), stop=(kb == NB - 1))
                        last.then_inc(sums, 1)

                with pe.Fori(0, KMAX, 2) as it:
                    it = it.with_bounds(min_val=0, max_val=KMAX - 2)
                    term(it, 0)
                    term((it + 1).with_bounds(min_val=1, max_val=KMAX - 1), 1)

            @block.vector
            def _(dve):
                S = Steps(dve, step)
                v = nc.vector
                dve.sem_inc(bank_free, 2)
                deg = t.wsum[:, :, WP - 1]
                S(v.tensor_scalar(some[:], deg, 0.0, None, ALU.is_gt))
                v.tensor_scalar(safe[:], deg, 1.0, None, ALU.max).then_inc(deg_set, 1)
                dve.wait_ge(droot, 1)
                S(v.reciprocal(dinv[:], root_deg[:]))
                S.wait()
                S(v.tensor_tensor(dinv[:], dinv[:], some[:], ALU.mult))
                S.wait()
                for g, blocks in enumerate(groups):
                    n, b = len(blocks), blocks[0]
                    dve.wait_ge(y_ps, g + 1)
                    if g:
                        dve.wait_ge(parts_ready, 4 * g)
                    y_in = psY[g % 2][0:B, 0:n * D].rearrange("p (b d) -> p b d", d=D)
                    S(v.tensor_tensor(scaled[:, 0:n, :], y_in, dinv[:, b:b + n].unsqueeze(2).broadcast_to([B, n, D]),
                                      ALU.mult))
                    S(v.tensor_copy(y[:, b:b + n, :], y_in))
                    S.wait()
                    split(nc, S, lambda r: parts[0][:, b:b + n, r, :], scaled[:, 0:n, :], scaled[:, 0:n, :]
                          ).then_inc(parts_ready, n)
                dve.wait_ge(w_in, 32)
                dve.wait_ge(turned, len(groups))
                S(v.tensor_tensor(t.xb[:], t.xb[:], bias[:].unsqueeze(1).broadcast_to([B, NB, D]), ALU.add))
                start = S.n

                def term(it, src):
                    S.base, S.n = start + NB * PER * it, 0
                    for b in range(NB):
                        k = b % 2
                        ps, r, d, e = psA[(NB * src + b) % 2], sumr[k][:], diff[k][:], rest[k][:]
                        p = lambda i: parts[1 - src][:, b, i, :]
                        dve.wait_ge(sums, NB * it + b + 2)
                        dve.wait_ge(parts_ready, NB * it + NB + b)
                        S(v.reduce_sum(r, ps[0:B, 0:3 * D].rearrange("p (r d) -> p d r", r=3), X))
                        v.tensor_tensor(d, ps[0:B, 256:256 + D], y[:, b, :], ALU.subtract).then_inc(bank_free, 1)
                        dve.wait_ge(bank_free, NB * it + b + 3)
                        S(v.scalar_tensor_tensor(y[:, b, :], r, dinv[:, b:b + 1], d, ALU.mult, ALU.add))
                        S.wait()
                        S(v.tensor_scalar(p(0), y[:, b, :], dinv[:, b:b + 1], None, ALU.mult))
                        S(v.tensor_scalar(r, y[:, b, :], dinv[:, b:b + 1], None, ALU.mult))
                        S.wait()
                        S(v.tensor_tensor(e, r, p(0), ALU.subtract))
                        S.wait()
                        S(v.tensor_copy(p(1), e))
                        S.wait()
                        v.tensor_tensor(p(2), e, p(1), ALU.subtract).then_inc(parts_ready, 1)
                    assert S.n == NB * PER

                with dve.Fori(0, KMAX, 2) as it:
                    it = it.with_bounds(min_val=0, max_val=KMAX - 2)
                    term(it, 0)
                    term((it + 1).with_bounds(min_val=1, max_val=KMAX - 1), 1)
                S.base, S.n = start + NB * PER * KMAX, 0
                dve.wait_ge(parts_ready, NB * (KMAX + 1))
                S(v.tensor_tensor(y[:], y[:], t.xb[:], ALU.add))
                normalize(nc, dve, S, y, bn, mv, std, rstd, t.xb, var, root, chunks=2, chunk_done=written)


@contextmanager
def cleared_semaphores(nc, prefix, *names):
    sems = [nc.alloc_semaphore(name=f"{prefix}_{n}") for n in names]
    yield sems
    nc.clear_and_free_semaphores(sems)
    nc.all_engine_barrier()


def edge_sums(nc, name, g, table, pick, node, acc):
    C = D + 3
    with ExitStack() as s:
        sb = lambda n, sh, d: s.enter_context(nc.sbuf_tensor(f"{name}_{n}", sh, d))
        pick_i, node_f, rows = sb("pick_i", [B, 1], I32), sb("node_f", [B, 1], F32), sb("rows", [B, C], F32)
        ps = s.enter_context(nc.psum_tensor(f"{name}_ps", [P, 4, 512], F32))
        turn = sb("turn", [B, 1], F32)
        cleared, staged, turns, gathered, hot_ready, product, added = s.enter_context(cleared_semaphores(
            nc, name, "cleared", "staged", "turns", "gathered", "onehot_ready", "product", "added"))
        banks = [range(lo, min(lo + 7, NB)) for lo in range(0, NB, 7)]
        with nc.Block() as block:
            @block.vector
            def _(dve):
                nc.vector.memset(acc[:], 0.0).then_inc(cleared, 1)
                dve.wait_ge(cleared, 1)
                for count in (added, turns):
                    dve.sem_inc(count, 1)
                with dve.Fori(0, CH) as it:
                    dve.wait_ge(added, it + 1)
                    dve.wait_ge(turns, it + 1)
                    nc.vector.tensor_copy(pick_i[:], pick[:, bass.ds(it, 1)])
                    nc.vector.tensor_copy(node_f[:], node[:, bass.ds(it, 1)])
                    nc.vector.tensor_copy(rows[:, D:C], g.own[:, bass.ds(it, 1), :].rearrange("p o k -> p (o k)")
                                          ).then_inc(staged, 1)
                    dve.wait_ge(staged, it + 1)
                    nc.vector.tensor_scalar(g.hot[:], g.nodes[:], node_f[:], None, ALU.is_equal
                                            ).then_inc(hot_ready, 1)
                    dve.wait_ge(product, it + 1)
                    for k, blocks in enumerate(banks):
                        n, v = len(blocks), acc[:, blocks[0]:blocks[-1] + 1, :]
                        last = nc.vector.tensor_tensor(
                            v, v, ps[0:B, k, 0:n * C].rearrange("p (b c) -> p b c", c=C), ALU.add)
                    last.then_inc(added, 1)

            @block.gpsimd
            def _(pool):
                with pool.Fori(0, CH) as it:
                    pool.wait_ge(staged, it + 1)
                    nc.gpsimd.tensor_tensor(turn[:], g.ident[0:B, 0:1], g.ident[0:B, 0:1], ALU.add
                                            ).then_inc(turns, 1)
                    nc.gpsimd.indirect_dma_start(
                        out=rows[:, 0:D], out_offset=None, in_=table,
                        in_offset=bass.IndirectOffsetOnAxis(ap=pick_i[:, 0:1], axis=0)).then_inc(gathered, 16)

            @block.tensor
            def _(pe):
                with pe.Fori(0, CH) as it:
                    pe.wait_ge(gathered, 16 * it + 16)
                    pe.wait_ge(hot_ready, it + 1)
                    for k, blocks in enumerate(banks):
                        for i, b in enumerate(blocks):
                            last = nc.tensor.matmul(ps[0:B, k, i * C:(i + 1) * C], g.hot[:, b * B:(b + 1) * B],
                                                    rows[:], start=True, stop=True)
                    last.then_inc(product, 1)


def edge_network_sums(nc, g, p_table, q_table, wd, eb1, eb2, eW2, acc):
    with ExitStack() as s:
        sb = lambda n, sh, d: s.enter_context(nc.sbuf_tensor(f"EN_{n}", sh, d))
        src_i, dst_i = sb("src_i", [B, 1], I32), sb("dst_i", [B, 1], I32)
        src_f, w1 = sb("src_f", [B, 1], F32), sb("w1", [B, 1], F32)
        pre, q, h1, h1T, z2, h2 = (sb("pre", [B, H], F32), sb("q", [B, H], F32), sb("h1", [B, H], F32),
                                   sb("h1T", [H, B], F32), sb("z2", [B, H], F32), sb("h2", [B, H], F32))
        ps = s.enter_context(nc.psum_tensor("EN_ps", [P, 4, 512], F32))
        ps_t = s.enter_context(nc.psum_tensor("EN_ps_t", [P, 512], F32))
        ps_z = s.enter_context(nc.psum_tensor("EN_ps_z", [P, 512], F32))
        turn = sb("turn", [B, 1], F32)
        (cleared, staged, turns, gathered, summed, h1_ready, turned, h1t_ready, z_ps, z2_ready, h2_ready, hot_ready,
         product, added) = s.enter_context(cleared_semaphores(
             nc, "EN", "cleared", "staged", "turns", "gathered", "summed", "h1_ready", "h1_turned", "h1T_ready",
             "z_product", "z2_ready", "h2_ready", "onehot_ready", "product", "added"))
        banks = [range(lo, min(lo + 8, NB)) for lo in range(0, NB, 8)]
        with nc.Block() as block:
            @block.vector
            def _(dve):
                nc.vector.memset(acc[:], 0.0).then_inc(cleared, 1)
                dve.wait_ge(cleared, 1)
                for count in (added, turns):
                    dve.sem_inc(count, 1)
                with dve.Fori(0, CH) as it:
                    dve.wait_ge(added, 2 * it + 1)
                    dve.wait_ge(turns, it + 1)
                    nc.vector.tensor_copy(src_i[:], g.src_i[:, bass.ds(it, 1)])
                    nc.vector.tensor_copy(dst_i[:], g.dst_i[:, bass.ds(it, 1)])
                    nc.vector.tensor_copy(src_f[:], g.src_f[:, bass.ds(it, 1)])
                    nc.vector.tensor_copy(w1[:], g.w1[:, bass.ds(it, 1)]).then_inc(staged, 1)
                    dve.wait_ge(staged, it + 1)
                    nc.vector.tensor_scalar(g.hot[:], g.nodes[:], src_f[:], None, ALU.is_equal).then_inc(hot_ready, 1)
                    dve.wait_ge(gathered, 32 * it + 32)
                    nc.vector.tensor_tensor(pre[:], pre[:], q[:], ALU.add).then_inc(summed, 1)
                    dve.wait_ge(summed, 3 * it + 1)
                    nc.vector.scalar_tensor_tensor(pre[:], wd[:], w1[:], pre[:], ALU.mult, ALU.add
                                                   ).then_inc(summed, 1)
                    dve.wait_ge(summed, 3 * it + 2)
                    nc.vector.tensor_tensor(pre[:], pre[:], eb1[:], ALU.add).then_inc(summed, 1)
                    dve.wait_ge(z_ps, it + 1)
                    nc.vector.tensor_tensor(z2[:], ps_z[0:B, 0:H], eb2[:], ALU.add).then_inc(z2_ready, 1)
                    for half in range(2):
                        dve.wait_ge(product, 2 * it + half + 1)
                        for k, blocks in enumerate(banks):
                            n, v = len(blocks), acc[:, blocks[0]:blocks[-1] + 1, half * D:(half + 1) * D]
                            last = nc.vector.tensor_tensor(
                                v, v, ps[0:B, k, 0:n * D].rearrange("p (b c) -> p b c", c=D), ALU.add)
                        last.then_inc(added, 1)

            @block.gpsimd
            def _(pool):
                with pool.Fori(0, CH) as it:
                    pool.wait_ge(staged, it + 1)
                    nc.gpsimd.tensor_tensor(turn[:], g.ident[0:B, 0:1], g.ident[0:B, 0:1], ALU.add
                                            ).then_inc(turns, 1)
                    nc.gpsimd.indirect_dma_start(
                        out=pre[:], out_offset=None, in_=p_table,
                        in_offset=bass.IndirectOffsetOnAxis(ap=src_i[:, 0:1], axis=0)).then_inc(gathered, 16)
                    nc.gpsimd.indirect_dma_start(
                        out=q[:], out_offset=None, in_=q_table,
                        in_offset=bass.IndirectOffsetOnAxis(ap=dst_i[:, 0:1], axis=0)).then_inc(gathered, 16)

            @block.scalar
            def _(act):
                with act.Fori(0, CH) as it:
                    act.wait_ge(summed, 3 * it + 3)
                    nc.scalar.activation(h1[:], pre[:], ACT.Silu).then_inc(h1_ready, 1)
                    act.wait_ge(turned, it + 1)
                    nc.scalar.copy(h1T[:], ps_t[:, 0:B]).then_inc(h1t_ready, 1)
                    act.wait_ge(z2_ready, it + 1)
                    nc.scalar.activation(h2[:], z2[:], ACT.Silu).then_inc(h2_ready, 1)

            @block.tensor
            def _(pe):
                with pe.Fori(0, CH) as it:
                    pe.wait_ge(h1_ready, it + 1)
                    nc.tensor.transpose(ps_t[:, 0:B], h1[:], g.ident[0:B, 0:B]).then_inc(turned, 1)
                    pe.wait_ge(h1t_ready, it + 1)
                    nc.tensor.matmul(ps_z[0:B, 0:H], h1T[:], eW2[:], start=True, stop=True).then_inc(z_ps, 1)
                    pe.wait_ge(h2_ready, it + 1)
                    pe.wait_ge(hot_ready, it + 1)
                    for half in range(2):
                        if half:
                            pe.wait_ge(added, 2 * it + 2)
                        for k, blocks in enumerate(banks):
                            for i, b in enumerate(blocks):
                                last = nc.tensor.matmul(ps[0:B, k, i * D:(i + 1) * D], g.hot[:, b * B:(b + 1) * B],
                                                        h2[:, half * D:(half + 1) * D], start=True, stop=True)
                        last.then_inc(product, 1)


def node_product(nc, name, g, terms, out, bias):
    with ExitStack() as s:
        N = out.shape[2]
        staged_rows = [s.enter_context(nc.sbuf_tensor(f"{name}_rows{i}", [B, w.shape[0]], F32))
                       for i, (_, w) in enumerate(terms)]
        rowsT = [s.enter_context(nc.sbuf_tensor(f"{name}_rowsT{i}", [w.shape[0], B], F32))
                 for i, (_, w) in enumerate(terms)]
        ps_t = [s.enter_context(nc.psum_tensor(f"{name}_ps_t{i}", [P, 512], F32)) for i in range(len(terms))]
        ps = s.enter_context(nc.psum_tensor(f"{name}_ps", [P, 512], F32))
        staged, turned, rows_t, product, kept = s.enter_context(cleared_semaphores(
            nc, name, "staged", "turned", "rowsT_ready", "product", "kept"))
        with nc.Block() as block:
            @block.vector
            def _(dve):
                dve.sem_inc(kept, 1)
                with dve.Fori(0, NB) as b:
                    dve.wait_ge(kept, b + 1)
                    for (rows, w), st in zip(terms, staged_rows):
                        last = nc.vector.tensor_copy(
                            st[:], rows[:, bass.ds(b, 1), 0:w.shape[0]].rearrange("p o d -> p (o d)"))
                    last.then_inc(staged, 1)
                    dve.wait_ge(product, b + 1)
                    nc.vector.tensor_tensor(out[:, bass.ds(b, 1), :].rearrange("p o d -> p (o d)"), ps[0:B, 0:N],
                                            bias, ALU.add).then_inc(kept, 1)

            @block.tensor
            def _(pe):
                with pe.Fori(0, NB) as b:
                    pe.wait_ge(staged, b + 1)
                    for st, pt in zip(staged_rows, ps_t):
                        last = nc.tensor.matmul(pt[0:st.shape[1], 0:B], st[:], g.ident[0:B, 0:B], start=True,
                                                stop=True)
                    last.then_inc(turned, 1)
                    pe.wait_ge(rows_t, b + 1)
                    for i, (_, w) in enumerate(terms):
                        last = nc.tensor.matmul(ps[0:B, 0:N], rowsT[i][:], w, start=(i == 0),
                                                stop=(i == len(terms) - 1))
                    last.then_inc(product, 1)

            @block.scalar
            def _(act):
                with act.Fori(0, NB) as b:
                    act.wait_ge(turned, b + 1)
                    for rt, pt in zip(rowsT, ps_t):
                        last = nc.scalar.copy(rt[:], pt[0:rt.shape[0], 0:B])
                    last.then_inc(rows_t, 1)


def store_rows(nc, name, table, rows):
    with cleared_semaphores(nc, name, "stored") as (stored,), nc.Block() as block:
        @block.sync
        def _(sp):
            sp.dma_start(table.rearrange("(b p) d -> p b d", p=B), rows).then_inc(stored, 16)
            sp.wait_ge(stored, 16)


def add_and_normalize(nc, name, c, g, x, y):
    with ExitStack() as s:
        step, var, root = s.enter_context(cleared_semaphores(nc, name, "norm_step", "var_ready", "std_ready"))
        with nc.Block() as block:
            @block.vector
            def _(dve):
                S = Steps(dve, step)
                S(nc.vector.tensor_tensor(y[:], y[:], x[:], ALU.add))
                normalize(nc, dve, S, y, g.bn, g.mv, g.std, g.rstd, x, var, root).then_inc(root, 1)

            @block.scalar
            def _(act):
                roots(nc, act, c, g.mv, g.std, var, root)


def any_order(nc, a, c, x, y, out):
    with ExitStack() as s:
        sb = lambda n, sh, d: s.enter_context(nc.sbuf_tensor(f"any_{n}", sh, d))
        g = Bag()
        g.src_i, g.dst_i = sb("src_i", [B, CH], I32), sb("dst_i", [B, CH], I32)
        g.src_f, g.dst_f = sb("src_f", [B, CH], F32), sb("dst_f", [B, CH], F32)
        g.w1, g.own, w = sb("w1", [B, CH], F32), sb("own", [B, CH, 3], F32), sb("w", [B, 2 * CH], F32)
        edges = sb("edges", [B, 2 * CH], I32)
        g.nodes, g.hot = sb("nodes", [B, V], F32), sb("hot", [B, V], F32)
        g.ident = c.ident
        g.bn, g.mv, g.std, g.rstd = norm_buffers(sb)
        acc = sb("acc", [B, NB, D + 3], F32)
        agg, z, z_out = sb("agg", [B, NB, H], F32), sb("z", [B, NB, H], F32), sb("z_out", [B, NB, H], F32)
        hx, hmu = sb("hx", [B, NB, D], F32), sb("hmu", [B, NB, D], F32)
        nothing = sb("nothing", [B, H], F32)
        nv = sb("nv", [B, NB], F32)
        table = nc.dram_tensor("any_table", [V, D], F32).ap()
        p_table, q_table = nc.dram_tensor("any_p", [V, H], F32).ap(), nc.dram_tensor("any_q", [V, H], F32).ap()
        n0, n1, n2, n3 = "L0_gnn_", "L1_gnn_", "L2_gnn_", "L3_gnn_"
        tables = {}
        for k, ap, sh in (("W1", a[n0 + "W1"], [D, D]), ("W2", a[n0 + "W2"], [D, D]),
                          ("eWa", a[n1 + "eW1"][0:D], [D, H]), ("eWb", a[n1 + "eW1"][D:2 * D], [D, H]),
                          ("eW2", a[n1 + "eW2"], [H, H]), ("nWa", a[n1 + "nW1"][0:D], [D, H]),
                          ("nWb", a[n1 + "nW1"][D:D + H], [H, H]), ("nW2", a[n1 + "nW2"], [H, D]),
                          ("W3T", a["W3T"], [D, D]), ("W4a", a["W4T"][0:D], [D, D]),
                          ("W4b", a["W4T"][D:2 * D], [D, D]), ("W4c", a["W4T"][2 * D:3 * D], [D, D]),
                          ("Wk", a[n3 + "W"].rearrange("k i o -> i k o"), [D, KMAX + 1, D])):
            tables[k] = (sb(k, sh, F32), ap)
        for k, ap, width in (("b1", a[n0 + "b1"], D), ("b2", a[n0 + "b2"], D), ("eb1", a[n1 + "eb1"], H),
                             ("wd", a[n1 + "eW1"][2 * D], H), ("eb2", a[n1 + "eb2"], H), ("nb1", a[n1 + "nb1"], H),
                             ("nb2", a[n1 + "nb2"], D), ("w1r", a[n2 + "W1"].rearrange("d o -> (d o)"), D),
                             ("w2r", a[n2 + "W2"].rearrange("d o -> (d o)"), D), ("bias", a[n3 + "bias"], D)):
            tables[k] = (sb(k, [B, width], F32), ap.partition_broadcast(B))
        tb = lambda k: tables[k][0]
        wide = lambda ap: ap.unsqueeze(1).broadcast_to([B, NB, ap.shape[1]])
        loaded, = s.enter_context(cleared_semaphores(nc, "any", "loaded"))
        LOADS = len(tables) + 4
        with nc.Block() as block:
            @block.sync
            def _(sp):
                sp.dma_start(edges[:], a["edges"].rearrange("(p j) -> p j", p=B)).then_inc(loaded, 16)
                sp.dma_start(w[:], a["weights"].rearrange("(p j) -> p j", p=B)).then_inc(loaded, 16)
                sp.dma_start(x[:], a["x"].rearrange("(b p) d -> p b d", p=B)).then_inc(loaded, 16)
                with nc.allow_non_contiguous_dma("one load of a column"):
                    sp.dma_start(nv[:], a["node_vec1"].rearrange("(b p) -> p b", p=B)).then_inc(loaded, 16)
                for k in tables:
                    sp.dma_start(tables[k][0][:], tables[k][1]).then_inc(loaded, 16)

            @block.gpsimd
            def _(pool):
                nc.gpsimd.iota(g.nodes[:], [[1, V]], base=0, channel_multiplier=0,
                               allow_small_or_imprecise_dtypes=True)
                nc.gpsimd.memset(nothing[:], 0.0)
                nc.gpsimd.memset(g.own[:, :, 2], 1.0)

            @block.vector
            def _(dve):
                v = nc.vector
                dve.wait_ge(loaded, 16 * LOADS)
                e2, w2 = (t[:].rearrange("p (j k) -> p j k", k=2) for t in (edges, w))
                v.tensor_copy(g.src_i[:], e2[:, :, 0])
                v.tensor_copy(g.dst_i[:], e2[:, :, 1])
                v.tensor_copy(g.src_f[:], e2[:, :, 0])
                v.tensor_copy(g.dst_f[:], e2[:, :, 1])
                v.tensor_copy(g.w1[:], w2[:, :, 0])
                v.tensor_scalar(g.own[:, :, 0], w2[:, :, 1], 0.0, None, ALU.max)
                v.tensor_scalar(g.own[:, :, 1], w2[:, :, 1], -1.0, 0.0, ALU.mult, ALU.max)
                inv = 1.0
                for k in range(1, KMAX + 1):
                    inv /= k
                    v.tensor_scalar(tb("Wk")[:, k, :], tb("Wk")[:, k, :], inv, None, ALU.mult)

        store_rows(nc, "any_x", table, x[:])
        edge_sums(nc, "any_L0a", g, table, g.src_i, g.dst_f, acc)
        node_product(nc, "any_L0h", g, [(acc, tb("W1")[:])], y, tb("b1")[:])
        with nc.Block() as block:
            @block.vector
            def _(dve):
                nc.vector.tensor_scalar(y[:], y[:], 0.0, None, ALU.max)
        store_rows(nc, "any_h", table, y[:])
        edge_sums(nc, "any_L0b", g, table, g.src_i, g.dst_f, acc)
        node_product(nc, "any_L0y", g, [(acc, tb("W2")[:])], y, tb("b2")[:])
        add_and_normalize(nc, "any_L0n", c, g, x, y)

        node_product(nc, "any_L1p", g, [(x, tb("eWa")[:])], z, nothing[:])
        store_rows(nc, "any_p", p_table, z[:])
        node_product(nc, "any_L1q", g, [(x, tb("eWb")[:])], z, nothing[:])
        store_rows(nc, "any_q", q_table, z[:])
        edge_network_sums(nc, g, p_table, q_table, tb("wd"), tb("eb1"), tb("eb2"), tb("eW2"), agg)
        node_product(nc, "any_L1z", g, [(x, tb("nWa")[:]), (agg, tb("nWb")[:])], z, tb("nb1")[:])
        with nc.Block() as block:
            @block.scalar
            def _(act):
                nc.scalar.activation(z_out[:], z[:], ACT.Silu)
        node_product(nc, "any_L1y", g, [(z_out, tb("nW2")[:])], y, tb("nb2")[:])
        add_and_normalize(nc, "any_L1n", c, g, x, y)

        he, side = z[:, :, 0:D], z[:, :, D:H]
        node_product(nc, "any_L2m", g, [(x, tb("W3T")[:])], hmu, nothing[:, 0:D])
        w2pm = sb("w2pm", [B, 2, D], F32)
        with cleared_semaphores(nc, "any_L2_step", "step") as (step,), nc.Block() as block:
            @block.vector
            def _(dve):
                S, v = Steps(dve, step), nc.vector
                S(v.tensor_scalar(hmu[:], hmu[:], 0.0, None, ALU.max))
                S(v.tensor_tensor(hx[:], nv[:].unsqueeze(2).broadcast_to([B, NB, D]), wide(tb("w1r")[:]), ALU.mult))
                S(v.tensor_scalar(w2pm[:, 0, :], tb("w2r")[:], 0.0, None, ALU.max))
                S(v.tensor_scalar(w2pm[:, 1, :], tb("w2r")[:], -1.0, 0.0, ALU.mult, ALU.max))
                S.wait()
                v.tensor_scalar(hx[:], hx[:], 0.0, None, ALU.max)
        node_product(nc, "any_L2z", g, [(hx, tb("W4a")[:]), (hmu, tb("W4c")[:])], y, nothing[:, 0:D])
        store_rows(nc, "any_z", table, y[:])
        edge_sums(nc, "any_L2s", g, table, g.dst_i, g.src_f, acc)
        with cleared_semaphores(nc, "any_he_step", "step") as (step,), nc.Block() as block:
            @block.vector
            def _(dve):
                S, v = Steps(dve, step), nc.vector
                for i, to in enumerate((he, side)):
                    S(v.tensor_tensor(to, acc[:, :, D + i:D + i + 1].broadcast_to([B, NB, D]), wide(w2pm[:, i, :]),
                                      ALU.mult))
                S.wait()
                v.tensor_tensor(he, he, side, ALU.add)
        node_product(nc, "any_L2e", g, [(z, tb("W4b")[:])], y, nothing[:, 0:D])
        some, dinv = sb("some", [B, NB], F32), sb("dinv", [B, NB], F32)
        root_deg = sb("root_deg", [B, NB], F32)
        with cleared_semaphores(nc, "any_msg", "step", "root") as (step, droot), nc.Block() as block:
            @block.vector
            def _(dve):
                S, v = Steps(dve, step), nc.vector
                deg = acc[:, :, D + 2]
                S(v.tensor_scalar(dinv[:], deg, 1.0, None, ALU.max))
                S(v.tensor_scalar(some[:], deg, 0.0, None, ALU.is_gt))
                S(v.tensor_tensor(y[:], y[:], acc[:, :, 0:D], ALU.add))
                S.wait()
                S(v.scalar_tensor_tensor(y[:], y[:], 0.0, hx[:], ALU.max, ALU.add))
                S.wait()
                S(v.tensor_tensor(y[:], y[:], hmu[:], ALU.add))
                S.wait()
                S(v.tensor_scalar(y[:], y[:], 0.0, None, ALU.max))
                dve.wait_ge(droot, 1)
                S(v.reciprocal(dinv[:], root_deg[:]))
                S.wait()
                v.tensor_tensor(dinv[:], dinv[:], some[:], ALU.mult)

            @block.scalar
            def _(act):
                act.wait_ge(step, 1)
                nc.scalar.activation(root_deg[:], dinv[:], ACT.Sqrt).then_inc(droot, 1)
        add_and_normalize(nc, "any_L2n", c, g, x, y)

        each = dinv[:].unsqueeze(2).broadcast_to([B, NB, D])
        node_product(nc, "any_L3y", g, [(x, tb("Wk")[:, KMAX, :])], y, nothing[:, 0:D])
        for k in range(KMAX - 1, -1, -1):
            with nc.Block() as block:
                @block.vector
                def _(dve):
                    nc.vector.tensor_tensor(hx[:], y[:], each, ALU.mult)
            store_rows(nc, f"any_y{k}", table, hx[:])
            edge_sums(nc, f"any_L3s{k}", g, table, g.dst_i, g.src_f, acc)
            node_product(nc, f"any_L3x{k}", g, [(x, tb("Wk")[:, k, :])], hmu, nothing[:, 0:D])
            with cleared_semaphores(nc, f"any_term{k}", "step") as (step,), nc.Block() as block:
                @block.vector
                def _(dve):
                    S, v = Steps(dve, step), nc.vector
                    S(v.tensor_tensor(hx[:], acc[:, :, 0:D], each, ALU.mult))
                    S(v.tensor_tensor(hmu[:], hmu[:], y[:], ALU.subtract))
                    S.wait()
                    v.tensor_tensor(y[:], hx[:], hmu[:], ALU.add)
        with nc.Block() as block:
            @block.vector
            def _(dve):
                nc.vector.tensor_tensor(y[:], y[:], wide(tb("bias")[:]), ALU.add)
        add_and_normalize(nc, "any_L3n", c, g, x, y)
        store_rows(nc, "any_out", out, x[:])


class Bag:
    pass


def program(nc, a, out):
    with ExitStack() as ctx:
        sb = lambda n, sh, d: ctx.enter_context(nc.sbuf_tensor(n, sh, d))
        c, t = Bag(), Bag()
        c.ones, c.ones_bf = sb("ones", [P, P], F32), sb("ones_bf", [P, P], BF16)
        c.iota1, c.iota1_bf = sb("iota1", [P, P], F32), sb("iota1_bf", [P, P], BF16)
        c.row1, c.sign = sb("row1", [P, 1], F32), sb("sign", [P, 1], F32)
        c.ident, c.ident_bf = sb("ident", [P, P], F32), sb("ident_bf", [P, P], BF16)
        c.placed_i = sb("placed_i", [1, 1], I32)
        c.eps = sb("eps", [P, 1], F32)
        t.src1 = sb("src1", [P, NT], F32)
        t.wsum = sb("wsum", [B, NB, WP], F32)
        rows_d = nc.dram_tensor("rows_d", [5 * NT * P], BF16).ap()
        m2_d = nc.dram_tensor("m2_d", [NB, B, MW], BF16).ap()
        t.xa, t.xb = sb("xa", [B, NB, D], F32), sb("xb", [B, NB, D], F32)
        with ExitStack() as right:
            t.dst1 = right.enter_context(nc.sbuf_tensor("dst1", [P, NT], F32, side="right"))
            t.wparts = right.enter_context(nc.sbuf_tensor("wparts", [P, NT, WP], BF16, side="right"))
            with nc.sbuf_tensor("slots", [P, REC, NC, NB], BF16) as slots:
                t.slots = slots
                place_edges(nc, a, c, t)
                edge_tables(nc, c, t, slots, rows_d)
            placed = nc.values_load(c.placed_i[0:1, 0:1], min_val=0, max_val=E)
            with nc.If(placed == E):
                with ExitStack() as fast:
                    t.mat = fast.enter_context(nc.sbuf_tensor("mat", [P, NB, MW], BF16))
                    with ExitStack() as early2:
                        l2 = l2_weights(nc, early2)
                        with ExitStack() as early:
                            l0 = l0_inputs(nc, early, t)
                            count_matrices(nc, a, c, t, m2_d, l0)
                            right.close()
                            l1 = l1_weights(nc, early)
                            gcn_layers(nc, a, c, t, l0, l1)
                            edge_network(nc, a, c, t, rows_d, m2_d, l1, l2)
                        message_layer(nc, a, c, t, m2_d, l2)
                    polynomial_layer(nc, a, c, t, out)
            with nc.Else():
                any_order(nc, a, c, t.xb, t.xa, out)


_WEIGHTS = ["L0_gnn_W1", "L0_gnn_b1", "L0_gnn_W2", "L0_gnn_b2", "L1_gnn_eW1", "L1_gnn_eb1", "L1_gnn_eW2", "L1_gnn_eb2",
            "L1_gnn_nW1", "L1_gnn_nb1", "L1_gnn_nW2", "L1_gnn_nb2", "L2_gnn_W1", "L2_gnn_W2", "L3_gnn_W",
            "L3_gnn_bias"]


def kernel(**inputs):
    import concourse.bacc as _bacc
    from concourse.bass_utils import run_bass_kernel_spmd as _run

    put = {k: np.ascontiguousarray(inputs[k]) for k in ["x"] + _WEIGHTS}
    src, dst = np.asarray(inputs["src"]), np.asarray(inputs["dst"])
    put["dst"] = np.ascontiguousarray(dst)
    put["edges"] = np.stack([src, dst], -1).reshape(-1)
    put["weights"] = np.stack([np.asarray(inputs["edge_weight1"])[:, 0], np.asarray(inputs["edge_weight"])],
                              -1).reshape(-1)
    put["node_vec1"] = np.asarray(inputs["node_vec1"]).reshape(-1)
    put["xT"] = np.ascontiguousarray(np.asarray(inputs["x"]).T)
    put["W3T"] = np.ascontiguousarray(np.asarray(inputs["L2_gnn_W3"]).T)
    put["W4T"] = np.ascontiguousarray(np.asarray(inputs["L2_gnn_W4"]).T)

    nc = _bacc.Bacc("TRN2", target_bir_lowering=False, num_devices=1)
    a = {n: nc.dram_tensor(f"in_{n}", v.shape, mybir.dt.from_np(v.dtype), kind="ExternalInput").ap()
         for n, v in put.items()}
    out = nc.dram_tensor("out", [V, D], F32, kind="ExternalOutput").ap()
    program(nc, a, out)
    r = _run(nc, [{f"in_{n}": v for n, v in put.items()}], core_ids=[0])
    return r.results[0]["out"]
```
